# Optimizing a Trainium2 kernel written in Bass

```python
import numpy as np
import jax
import jax.numpy as jnp

def _softmax(x, axis=-1):
    return jax.nn.softmax(x, axis=axis)

def _gelu(x):
    return jax.nn.gelu(x, approximate=True)

def _silu(x):
    return jax.nn.silu(x)

def _sigmoid(x):
    return jax.nn.sigmoid(x)

def _layernorm(x, axis=-1, eps=1e-05):
    m = jnp.mean(x, axis=axis, keepdims=True)
    v = jnp.var(x, axis=axis, keepdims=True)
    return (x - m) / jnp.sqrt(v + eps)

def _scatter_add(tgt, idx, src, axis=0):
    return tgt.at[idx].add(src)

def _segment_sum(src, seg, n):
    return jax.ops.segment_sum(src, seg, n)
kernel_name = 'mk_gnn_resnorm_d2_gnn_r32_d3fb3a'

def setup_inputs(seed: int=0):
    np.random.seed(seed)
    _w = jnp.asarray

    def _rec_inputs():
        import jax
        import jax.numpy as jnp
        _gk = jax.random.key(seed)
        x = -0.0003713 + 1 * jax.random.normal(jax.random.fold_in(_gk, 1), (3125, 128), jnp.float32)
        _s = jax.random.randint(jax.random.fold_in(_gk, 2), (50000,), 0, 3125, jnp.int32)
        _d = jax.random.randint(jax.random.fold_in(_gk, 3), (50000,), 0, 3125, jnp.int32)
        _loop = jnp.arange(3125, dtype=jnp.int32)
        src = jnp.concatenate([_s, _d, _loop])
        dst = jnp.concatenate([_d, _s, _loop])
        _o = jnp.argsort(dst, stable=True)
        src = src[_o]
        dst = dst[_o]
        edge_attr_64 = 0.000155561 + 1.00019 * jax.random.normal(jax.random.fold_in(_gk, 12), (103125, 64), jnp.float32)
        edge_weight = jax.random.uniform(jax.random.fold_in(_gk, 14), (103125,), jnp.float32, 0.0, 1)
        return (x, src, dst, edge_attr_64, edge_weight)
    x, src, dst, edge_attr_64, edge_weight = _rec_inputs()

    def _L0_gnn_setup():
        import jax, jax.numpy as jnp
        import numpy as np
        N_NODES = 3125
        D = 128
        N_EDGES = 50000
        NUM_LAYERS = 3
        key = jax.random.key(seed)
        k1, k2, k3, k4 = jax.random.split(key, 4)
        ebds = jax.random.normal(k1, (N_NODES, D), dtype=jnp.float32)
        edge_val = jax.random.uniform(k2, (N_EDGES,), dtype=jnp.float32)
        edge_row = jax.random.randint(k3, (N_EDGES,), 0, N_NODES, dtype=jnp.int32)
        edge_col = jax.random.randint(k4, (N_EDGES,), 0, N_NODES, dtype=jnp.int32)
        return {'ebds': ebds, 'edge_val': edge_val, 'edge_row': edge_row, 'edge_col': edge_col, 'num_layers': NUM_LAYERS}
    _L0_gnn_all = _L0_gnn_setup()
    _L0_gnn_in = {k: v for k, v in _L0_gnn_all.items() if k in ()}
    del _L0_gnn_all

    def _L1_gnn_setup():
        import jax, jax.numpy as jnp
        import numpy as np
        N_NODES, N_EDGES = (50000, 18750)
        NODE_DIM, EDGE_DIM = (128, 64)
        H, HD = (4, 32)
        key = jax.random.key(seed)
        k = jax.random.split(key, 6)
        node_features = jax.random.normal(k[0], (N_NODES, NODE_DIM), jnp.float32)
        edge_indices = jax.random.randint(k[1], (2, N_EDGES), 0, N_NODES, jnp.int32)
        edge_features = jax.random.normal(k[2], (N_EDGES, EDGE_DIM), jnp.float32)
        W_node = jax.random.normal(k[3], (H * HD, NODE_DIM), jnp.float32) / np.sqrt(NODE_DIM).astype(np.float32)
        W_edge = jax.random.normal(k[4], (H * HD, EDGE_DIM), jnp.float32) / np.sqrt(EDGE_DIM).astype(np.float32)
        a = jax.random.normal(k[5], (H, 3 * HD), jnp.float32)
        return {'node_features': node_features, 'edge_indices': edge_indices, 'edge_features': edge_features, 'W_node': W_node, 'W_edge': W_edge, 'a': a}
    _L1_gnn_all = _L1_gnn_setup()
    _L1_gnn_in = {k: v for k, v in _L1_gnn_all.items() if k in ('W_node', 'W_edge', 'a')}
    del _L1_gnn_all
    return {'x': x, 'src': src, 'dst': dst, 'edge_attr_64': edge_attr_64, 'edge_weight': edge_weight, 'L1_gnn_W_node': _L1_gnn_in['W_node'], 'L1_gnn_W_edge': _L1_gnn_in['W_edge'], 'L1_gnn_a': _L1_gnn_in['a']}

def reference(x, src, dst, edge_attr_64, edge_weight, L1_gnn_W_node, L1_gnn_W_edge, L1_gnn_a):
    import jax
    import jax.numpy as jnp

    def _L0_gnn_ref(ebds, edge_val, edge_row, edge_col, num_layers):
        import jax, jax.numpy as jnp
        import numpy as np
        N_NODES = 3125
        D = 128
        N_EDGES = 50000
        NUM_LAYERS = 3
        'LightGCN forward: repeated SpMM with running layer-sum.\n\n            adj is COO: out[r] += val[e] * x[c] for each edge e=(r,c).\n            Equivalent to torch.spmm(adj, x) applied num_layers times,\n            summing all layer outputs (including layer 0 input).\n            '
        n = ebds.shape[0]

        def spmm(x):
            msgs = edge_val[:, None] * x[edge_col]
            return jax.ops.segment_sum(msgs, edge_row, num_segments=n)
        acc = ebds
        cur = ebds
        for _ in range(num_layers):
            cur = spmm(cur)
            acc = acc + cur
        return acc

    def _L1_gnn_ref(node_features, edge_indices, edge_features, W_node, W_edge, a):
        import jax, jax.numpy as jnp
        import numpy as np
        N_NODES, N_EDGES = (50000, 18750)
        NODE_DIM, EDGE_DIM = (128, 64)
        H, HD = (4, 32)
        num_nodes = node_features.shape[0]
        num_edges = edge_indices.shape[1]
        h = (node_features @ W_node.T).reshape(num_nodes, H, HD)
        e = (edge_features @ W_edge.T).reshape(num_edges, H, HD)
        src, tgt = (edge_indices[0], edge_indices[1])
        h_src = h[src]
        h_tgt = h[tgt]
        att_in = jnp.concatenate([h_src, h_tgt, e], axis=-1)
        att = jnp.sum(att_in * a, axis=-1)
        att = jnp.where(att > 0, att, 0.2 * att)
        m = jnp.maximum(jax.ops.segment_max(att, tgt, num_segments=num_nodes), 0.0)
        ex = jnp.exp(att - m[tgt])
        ones = jnp.ones((num_edges,), node_features.dtype)
        deg = jax.ops.segment_sum(ones, tgt, num_segments=num_nodes)
        denom = jax.ops.segment_sum(ex, tgt, num_segments=num_nodes) + (num_edges - deg)[:, None] * jnp.exp(-m)
        w = ex / denom[tgt]
        h_prime = jax.ops.segment_sum(w[:, :, None] * h_src, tgt, num_segments=num_nodes)
        return h_prime.reshape(num_nodes, H * HD)
    edge_index = jnp.stack([src, dst])
    x = _layernorm(x + _L0_gnn_ref(x, edge_weight, src, dst, 3), axis=-1)
    x = _layernorm(x + _L1_gnn_ref(x, edge_index, edge_attr_64, L1_gnn_W_node, L1_gnn_W_edge, L1_gnn_a), axis=-1)
    return x

_drawn_inputs = setup_inputs


def setup_inputs(seed=0):
    import zlib

    import numpy as np

    out = dict(_drawn_inputs(seed))
    spreads = {}
    factors = {}
    for name, (base, spread) in spreads.items():
        noise = np.random.default_rng([zlib.crc32(name.encode()), seed]).standard_normal(out[name].shape)
        drawn = base * np.exp(spread * noise) if base else spread * noise
        out[name] = jnp.asarray(drawn.astype(out[name].dtype))
    for name, factor in factors.items():
        out[name] = (out[name] * factor).astype(out[name].dtype)
    return out
```

```python
from contextlib import ExitStack

import numpy as np

import concourse.bass as bass
from concourse import mybir

F32, BF16, I32 = mybir.dt.float32, mybir.dt.bfloat16, mybir.dt.int32
ALU, ACT = mybir.AluOpType, mybir.ActivationFunctionType
AX = mybir.AxisListType

P = 128
N, D, E, DE = 3125, 128, 103125, 64
H, HD = 4, 32
NB = -(-N // P)
NL = N - (NB - 1) * P
NP = NB * P
NT = -(-E // P)
EL = E - (NT - 1) * P
TR = 7
RW = TR * P
RF, RL = divmod(E, RW)
RR = RF + 1
TP = RR * TR
BT = 2 * NB + 1
BTP = BT + 1
HT = BTP // 2
SLOTS = P * NB * BT
REC = 8
SG = 62
SH = SG // 2
NG = NT // SG
assert NG * SG == NT and RR <= P and BT == 51 and HT == 26
LAYERS = 3
GW = D + 2 * H
TBL = NP + 2 * P
EPS = 1e-5
MW = D + H + 1
BANK = 512
BPB = BANK // P
RING = 5
assert NB % RING == 0


def banks_of(n):
    return [list(range(s, min(s + BPB, n))) for s in range(0, n, BPB)]


def build(nc, x, src, dst, edge_attr, edge_weight, w_node, w_edge, att, out):
    ctx = ExitStack()
    slots = nc.dram_tensor("slots", (SLOTS + P, REC), F32, kind="Internal").ap()
    g_x = [nc.dram_tensor(f"g_x{l}", (TBL, D), F32, kind="Internal").ap() for l in range(LAYERS + 1)]
    g_h = nc.dram_tensor("g_h", (TBL, GW), F32, kind="Internal").ap()
    g_max = nc.dram_tensor("g_max", (TBL, H), F32, kind="Internal").ap()
    g_sum = nc.dram_tensor("g_sum", (TBL, MW), F32, kind="Internal").ap()
    adj = nc.dram_tensor("adj", (NB, P, NP), F32, kind="Internal").ap()

    with ctx:
        def sb(name, shape, dt, c=ctx):
            return c.enter_context(nc.sbuf_tensor(name, shape, dt))

        def sem(name):
            return ctx.enter_context(nc.semaphore(name))

        ident = sb("ident", [P, P], F32)
        identb = sb("identb", [P, P], BF16)
        ones = sb("ones", [P, P], F32)
        zerob = sb("zerob", [P, BANK], BF16)
        iota_nt = sb("iota_nt", [P, P, BTP], BF16)
        iota_n = sb("iota_n", [P, P], F32)
        cur = sb("cur", [P, NB, D], F32)
        acc = sb("acc", [P, NB, D], F32)
        acat = sb("acat", [P, 3, H], F32)
        wn = sb("wn", [P, D], F32)
        we2 = sb("we2", [P, 2, DE], F32)
        wext = sb("wext", [P, D + 2 * H], F32)
        wedge = sb("wedge", [P, 2 * H], F32)
        st = sb("st", [P, 4, NB], F32)
        upto = sb("upto", [P, NB], F32)
        need_f = sb("need_f", [P, NB], F32)
        need = sb("need", [P, NB], I32)
        bad = sb("bad", [P, 4], F32)
        flag = sb("flag", [P, 1], I32)

        early = ExitStack()
        xs = sb("xs", [P, NB, D], F32, early)
        rec = sb("rec", [P, TP, REC], F32, early)
        slot_i = sb("slot_i", [P, TP], I32, early)
        st_rec = sb("st_rec", [P, 2, SH, REC], F32, early)
        st_slot = sb("st_slot", [P, 2, SH], I32, early)

        with ExitStack() as c:
            src_i, dst_i, w_r = sb("src_i", [P, RW], I32, c), sb("dst_i", [P, RW], I32, c), sb("w_r", [P, RW], F32, c)
            ti = sb("ti", [P, 2, RW], I32, c)
            srcb, dstb = sb("srcb", [P, RW], F32, c), sb("dstb", [P, RW], F32, c)
            src1, dst1 = sb("src1", [P, RW], F32, c), sb("dst1", [P, RW], F32, c)
            same = sb("same", [P, RW], F32, c)
            tmp = sb("tmp", [P, 4, RW], F32, c)
            rank = sb("rank", [P, RW], F32, c)
            lasts = sb("lasts", [P, NB], F32, c)
            base = sb("base", [P, NB], F32, c)
            ahead = sb("ahead", [P, P], F32, c)
            diag = sb("diag", [P, P], F32, c)
            upper = sb("upper", [P, P], F32, c)
            trash = sb("trash", [P, 2], F32, c)
            fix = sb("fix", [P, 2], F32, c)
            zrec = sb("zrec", [P, BT * REC], F32, c)
            ea = sb("ea", [P, 2, SH, 2, DE], F32, c)
            eaT = sb("eaT", [P, 2, BANK], F32, c)
        with ExitStack() as c:
            r3 = sb("r3", [P, 2, HT, REC], F32, c)
            oh_d, oh_s = sb("oh_d", [P, 2, P, HT], BF16, c), sb("oh_s", [P, 2, P, HT], BF16, c)
            oh_w = sb("oh_w", [P, 2, 3, P, HT], BF16, c)
            loc = sb("loc", [P, 2, 2, HT], BF16, c)
            wsp = sb("wsp", [P, 2, 3, HT], BF16, c)
            wres = sb("wres", [P, 2, 2, HT], F32, c)
            arow = sb("arow", [P, NP], F32, c)
        with ExitStack() as c:
            ablk = sb("ablk", [P, RING, NP], F32, c)
            stage = sb("stage", [P, RING, D], F32, c)
            curT = sb("curT", [P, NP], F32, c)
        early.close()
        with ExitStack() as c:
            hsp = sb("hsp", [P, NB, 3, D + 2 * H], BF16, c)
            r6 = sb("r6", [P, BTP, REC], F32, c)
            loc6 = sb("loc6", [P, 2, BTP], BF16, c)
            s6, d16 = sb("s6", [P, P, BTP], BF16, c), sb("d16", [P, P, BTP], BF16, c)
            d6 = sb("d6", [P, 2, BTP, P], F32, c)
            dT, sT = sb("dT", [P, BTP, P], BF16, c), sb("sT", [P, 2, BTP, P], BF16, c)
            dlr = sb("dlr", [P, BTP, H], F32, c)
            sc = sb("sc", [P, BTP, H], F32, c)
            sc2 = sb("sc2", [P, BTP, H], F32, c)
            dlT = sb("dlT", [P, 2, P], F32, c)
            keep = sb("keep", [P, 2, P], F32, c)
            endz = sb("endz", [P, 2, P], F32, c)
            run = sb("run", [P, 2, P], F32, c)
            zs = sb("zs", [P, 3, BTP, H], F32, c)
            zsp = sb("zsp", [P, 3, BTP, H], BF16, c)
            mm = sb("mm", [P, 3, H], F32, c)
            msp = sb("msp", [P, 3, H], BF16, c)
            emn = sb("emn", [P, 2, H], F32, c)
            den = sb("den", [P, 4, H], F32, c)
            num = sb("num", [P, MW], F32, c)
            me = sb("me", [P, BTP, H], F32, c)
            ex = sb("ex", [P, 2, BTP, H], F32, c)
            msg = sb("msg", [P, 2, BPB, MW], F32, c)
        with ExitStack() as c:
            sb("any_skip", [P, 2 * NP + NP + 2 * NP + RING * D + NP + NP + 2048], F32, c)
            g_src, g_dst = sb("g_src", [P, NT], I32, c), sb("g_dst", [P, NT], I32, c)
            g_att = sb("g_att", [P, NT, H], F32, c)
            g_ki, g_so = sb("g_ki", [P, 2], I32, c), sb("g_so", [P, 1], I32, c)
            g_key = sb("g_key", [P, 4], F32, c)
            g_trash, g_zero = sb("g_trash", [P, 1], F32, c), sb("g_zero", [P, GW], F32, c)
            g_low, g_same = sb("g_low", [P, P], F32, c), sb("g_same", [P, P], F32, c)
            g_diag = sb("g_diag", [P, H, P], F32, c)
            g_tmp = sb("g_tmp", [P, H, P], F32, c)
            g_a, g_b = sb("g_a", [P, GW], F32, c), sb("g_b", [P, GW], F32, c)
            g_old, g_msg, g_new = sb("g_old", [P, GW], F32, c), sb("g_msg", [P, GW], F32, c), sb("g_new", [P, GW], F32, c)
            g_s = sb("g_s", [P, 4, H], F32, c)
            g_m, g_e = sb("g_m", [P, NB, H], F32, c), sb("g_e", [P, NB, H], F32, c)
        g_num = ablk[:, 0:2, :].rearrange("p r n -> p (r n)")[:, 0:NB * MW].rearrange("p (b n) -> p b n", b=NB)
        hx = ablk[:, 0:2, :].rearrange("p r n -> p (r n)")[:, 0:NB * (D + 2 * H)].rearrange("p (b n) -> p b n", b=NB)

        bank = [ctx.enter_context(nc.psum_tensor(f"bank{i}", [P, BANK], F32)) for i in range(8)]

        names = """consts clears ld_idx ld_w ld_x zeroed ea0 ea1 first_ready base_ready ahead_bc
            ahead_ready base_ps wt_ps wt_sb eaT_ps eaT_sb se_ps se_free rec_se place_ready place_ps place_sb
            place_free rec_ready staged armed half0 half1 landed need_ready block_in upto_sb upto_ps edge_done
            r3a r3b r3_free0 r3_free1 oh_ready oh_used0 row_ps row_free row_sb diag_ps row_add adj_out
            a0 a1 a2 a3 a4 a_used0 a_used1 a_used2 a_used3 a_used4 stage_sb stage_free lay_ps lay_sb lay_T cur_sb
            x1_ready x1T_ps x1T_sb h_ps h_sb h_split
            r6_in r6_free d6_ready s6_ready d16_ready tr_ps tr_sb at_ps at_sb atT_ps z_sb zT_ps zs_sb v_ps m_sb emn_sb mg_ps arg_sb ex_sb
            flag_ready bad_sb bad_ps key_bc2 g_init g_ld g_zeroed g_x0 g_keys g_bc g_in g_armed g_msgs g_arg g_ex g_tot g_news g_out
            g_done g_back g_backed g_hx g_hr g_fin g_emn
            hg_ps msg_sb msg_used num_free y_sb outs rs_var rs_std""".split()
        s = {n: sem(n) for n in names}

        e_rows = lambda t: t[0:RF * RW].rearrange("(r w) -> r w", w=RW)
        e_rest = lambda t: t[RF * RW:E].rearrange("(r w) -> r w", r=1)

        ANY_LAYERS = [("spmm", g_x[l], g_x[l + 1], 2) for l in range(LAYERS)]
        ANY_ATT = [("max", g_h, g_max, 3), ("sum", g_h, g_sum, 3)]
        passes = ANY_LAYERS + ANY_ATT

        def any_counts(k):
            return k * NT, sum(16 * NT * passes[i][3] for i in range(k))

        block = ctx.enter_context(nc.Block())

        @block.sync
        def _(sp):
            sp.wait_ge(s["clears"], 4)
            for a, t in ((src_i, src), (dst_i, dst)):
                sp.dma_start(a[0:RF, :], e_rows(t)).then_inc(s["ld_idx"], 16)
                sp.dma_start(a[RF:RF + 1, 0:RL], e_rest(t)).then_inc(s["ld_idx"], 16)
            for h in range(H):
                sp.dma_start(acat[h * HD:(h + 1) * HD, :, h], att[h, :].rearrange("(k d) -> d k", k=3),
                             allow_slow_non_contiguous=True).then_inc(s["ld_w"], 16)
            sp.dma_start(wn[:, :], w_node).then_inc(s["ld_w"], 16)
            for k in range(2):
                sp.dma_start(we2[:, k, :], w_edge).then_inc(s["ld_w"], 16)

            def load_attr(g, buf, tiles=SH, last=0):
                view = edge_attr[bass.ds(g * (SG * P), SG * P), :] if not last else None
                if view is not None:
                    view = view.rearrange("(k u p) d -> k p u d", k=2, p=P)
                    for k in range(2):
                        sp.dma_start(ea[:, buf, :, k, :], view[k]).then_inc(s[f"ea{buf}"], 16)
                else:
                    e0 = g * SG * P
                    sp.dma_start(ea[:, buf, :, 0, :], edge_attr[e0:e0 + SH * P, :].rearrange("(u p) d -> p u d", p=P))\
                        .then_inc(s[f"ea{buf}"], 16)
                    e0 += SH * P
                    sp.dma_start(ea[:, buf, 0:SH - 1, 1, :],
                                 edge_attr[e0:e0 + (SH - 1) * P, :].rearrange("(u p) d -> p u d", p=P))\
                        .then_inc(s[f"ea{buf}"], 16)
                    e0 += (SH - 1) * P
                    sp.dma_start(ea[0:EL, buf, SH - 1, 1, :], edge_attr[e0:E, :]).then_inc(s[f"ea{buf}"], 16)

            load_attr(0, 0)
            load_attr(1, 1)
            sp.wait_ge(s["consts"], 9)
            sp.dma_start(w_r[0:RF, :], e_rows(edge_weight)).then_inc(s["ld_x"], 16)
            sp.dma_start(w_r[RF:RF + 1, 0:RL], e_rest(edge_weight)).then_inc(s["ld_x"], 16)
            sp.dma_start(xs[:, 0:NB - 1, :], x[0:(NB - 1) * P, :].rearrange("(b p) d -> p b d", p=P))\
                .then_inc(s["ld_x"], 16)
            sp.dma_start(xs[0:NL, NB - 1, :], x[(NB - 1) * P:N, :]).then_inc(s["ld_x"], 16)
            sp.dma_start(slots[0:SLOTS, :].rearrange("(p j t) f -> p j (t f)", p=P, j=NB),
                         zrec[:, :].rearrange("p (o n) -> p o n", o=1).broadcast_to([P, NB, BT * REC]))\
                .then_inc(s["zeroed"], 16)
            sp.dma_start(slots[SLOTS:SLOTS + P, :], zrec[:, 0:REC]).then_inc(s["zeroed"], 16)
            with sp.Fori(1, NG // 2) as g2:
                for buf in range(2):
                    sp.wait_ge(s["eaT_ps"], (g2 * 2 + (buf - 1)) * -(-SH // BPB))
                    load_attr(g2 * 2 + buf, buf)
            sp.wait_ge(s["eaT_ps"], (NG - 2) * -(-SH // BPB))
            load_attr(NG - 1, 0, last=1)

            all_slots = slots[0:SLOTS, :].rearrange("(p t) f -> p (t f)", p=P)

            def fast_layers():
                sp.wait_ge(s["need_ready"], 1)
                sp.wait_ge(s["edge_done"], 2)
                with sp.Fori(0, NB) as j:
                    sp.wait_ge(s["landed"], sp.value_load(need[0:1, bass.ds(j, 1)], min_val=1, max_val=2 * NG))
                    sp.sem_inc(s["block_in"], 1)
                    for c in range(2):
                        sp.wait_ge(s[f"r3_free{c}"], j + 1)
                        n = HT if c == 0 else HT - 1
                        sp.dma_start(r3[:, c, 0:n, :].rearrange("p t f -> p (t f)"),
                                     all_slots[:, bass.ds(j * (BT * REC) + c * HT * REC, n * REC)])\
                            .then_inc(s["r3a" if c == 0 else "r3b"], 16)
                sp.wait_ge(s["adj_out"], 16 * NB)
                with sp.Fori(0, LAYERS * NB // RING) as r:
                    for u in range(RING):
                        sp.wait_ge(s[f"a_used{u}"], r + 1)
                        sp.dma_start(ablk[:, u, :], adj[bass.ds((r % (NB // RING)) * RING + u, 1), :, :]
                                     .rearrange("o p n -> (o p) n")).then_inc(s[f"a{u}"], 16)

            def any_layers():
                sp.wait_ge(s["g_init"], 5)
                for a, t in ((g_src, src), (g_dst, dst)):
                    sp.dma_start(a[:, 0:NT - 1], t[0:(NT - 1) * P].rearrange("(t p) -> p t", p=P),
                                 allow_slow_non_contiguous=True).then_inc(s["g_ld"], 16)
                    sp.dma_start(a[0:EL, NT - 1:NT], t[(NT - 1) * P:E].rearrange("(p o) -> p o", o=1))\
                        .then_inc(s["g_ld"], 16)
                for t in g_x + [g_h, g_max, g_sum]:
                    w = t.shape[1]
                    sp.dma_start(t.rearrange("(p r) w -> p r w", p=P), g_zero[:, 0:w].rearrange("p (o w) -> p o w", o=1)
                                 .broadcast_to([P, TBL // P, w])).then_inc(s["g_zeroed"], 16)
                sp.wait_ge(s["g_zeroed"], 16 * (LAYERS + 4))
                sp.wait_ge(s["ld_x"], 64)
                sp.dma_start(g_x[0][0:NP, :].rearrange("(b p) d -> p b d", p=P), xs[:, :, :]).then_inc(s["g_x0"], 16)
                sp.wait_ge(s["g_done"], LAYERS * NT + 1)
                for l in range(LAYERS):
                    sp.dma_start(ablk[:, l, :].rearrange("p (b d) -> p b d", b=NB),
                                 g_x[l + 1][0:NP, :].rearrange("(b p) d -> p b d", p=P)).then_inc(s["g_back"], 16)

            def any_attention():
                sp.wait_ge(s["g_hx"], 1)
                sp.dma_start(g_h[0:NP, :].rearrange("(b p) d -> p b d", p=P), hx).then_inc(s["g_hr"], 16)
                sp.wait_ge(s["g_done"], len(passes) * NT + 1)
                sp.wait_ge(s["g_hr"], 16)
                sp.dma_start(g_num, g_sum[0:NP, :].rearrange("(b p) d -> p b d", p=P)).then_inc(s["g_fin"], 16)
                sp.dma_start(g_m[:, :, :], g_max[0:NP, :].rearrange("(b p) d -> p b d", p=P)).then_inc(s["g_fin"], 16)

            def fast_attention():
                sp.wait_ge(s["h_split"], 1)

                def load_r6(j, n):
                    sp.wait_ge(s["r6_free"], n + 1)
                    sp.dma_start(r6[:, 0:BT, :].rearrange("p t f -> p (t f)"),
                                 all_slots[:, bass.ds(j * (BT * REC), BT * REC)]).then_inc(s["r6_in"], 16)

                with sp.Fori(0, NB) as j:
                    load_r6(j, j)
                load_r6(NB - 1, NB)

            sp.wait_ge(s["flag_ready"], 1)
            plain = sp.value_load(flag[0:1, 0:1], min_val=0, max_val=1)
            with sp.If(plain):
                fast_layers()
            with sp.Else():
                any_layers()
            with sp.If(plain):
                fast_attention()
            with sp.Else():
                any_attention()
            sp.wait_ge(s["y_sb"], 1)
            sp.dma_start(out[0:(NB - 1) * P, :].rearrange("(b p) d -> p b d", p=P), cur[:, 0:NB - 1, :])\
                .then_inc(s["outs"], 16)
            sp.dma_start(out[(NB - 1) * P:N, :], cur[0:NL, NB - 1, :]).then_inc(s["outs"], 16)
            sp.wait_ge(s["outs"], 32)

        @block.gpsimd
        def _(pool):
            pool.memset(src_i[:, :], -1).then_inc(s["clears"], 1)
            pool.memset(dst_i[:, :], NP - 1).then_inc(s["clears"], 1)
            pool.memset(acat[:, :, :], 0.0).then_inc(s["clears"], 1)
            pool.memset(zrec[:, :], 0.0).then_inc(s["clears"], 1)
            c = s["consts"]
            pool.memset(w_r[:, :], 0.0).then_inc(c, 1)
            pool.memset(ident[:, :], 0.0).then_inc(c, 1)
            pool.memset(identb[:, :], 0.0).then_inc(c, 1)
            pool.memset(ones[:, :], 1.0).then_inc(c, 1)
            pool.memset(upper[:, :], 1.0).then_inc(c, 1)
            pool.memset(xs[:, NB - 1, :], 0.0).then_inc(c, 1)
            pool.memset(trash[:, 1:2], 1.0).then_inc(c, 1)
            pool.memset(zerob[:, :], 0.0).then_inc(c, 1)
            pool.memset(rec[:, :, 3:4], 0.0).then_inc(c, 1)
            pool.wait_ge(c, 9)
            pool.affine_select(out=ident[:, :], in_=ident[:, :], compare_op=ALU.not_equal, fill=1.0, base=0,
                               pattern=[[-1, P]], channel_multiplier=1).then_inc(c, 1)
            pool.affine_select(out=identb[:, :], in_=identb[:, :], compare_op=ALU.not_equal, fill=1.0, base=0,
                               pattern=[[-1, P]], channel_multiplier=1).then_inc(c, 1)
            pool.affine_select(out=upper[:, :], in_=upper[:, :], compare_op=ALU.is_ge, fill=0.0, base=-1,
                               pattern=[[1, P]], channel_multiplier=-1).then_inc(c, 1)
            pool.affine_select(out=trash[:, 1:2], in_=trash[:, 1:2], compare_op=ALU.is_ge, fill=0.0, base=EL - 1,
                               pattern=[[0, 1]], channel_multiplier=-1).then_inc(c, 1)
            pool.iota(trash[:, 0:1], pattern=[[0, 1]], base=SLOTS, channel_multiplier=1,
                      allow_small_or_imprecise_dtypes=True).then_inc(c, 1)
            pool.iota(iota_n[:, :], pattern=[[1, P]], base=1, channel_multiplier=0,
                      allow_small_or_imprecise_dtypes=True).then_inc(c, 1)
            pool.iota(iota_nt[:, :, :], pattern=[[1, P], [0, BTP]], base=1, channel_multiplier=0,
                      allow_small_or_imprecise_dtypes=True).then_inc(c, 1)

            pool.wait_ge(s["zeroed"], 32)
            pool.wait_ge(s["rec_ready"], 1)

            def scatter(g, k):
                pool.tensor_copy(st_rec[:, k, :, :], rec[:, bass.ds(g * SG + k * SH, SH), :]).then_inc(s["staged"], 1)
                pool.tensor_copy(st_slot[:, k, :], slot_i[:, bass.ds(g * SG + k * SH, SH)]).then_inc(s["staged"], 1)
                pool.wait_ge(s["staged"], g * 4 + (2 * k + 2))
                pool.sem_inc(s["armed"], 1)
                for u in range(SH):
                    pool.indirect_dma_start(
                        out=slots, out_offset=bass.IndirectOffsetOnAxis(ap=st_slot[:, k, u:u + 1], axis=0),
                        in_=st_rec[:, k, u, :], in_offset=None).then_inc(s[f"half{k}"], 16)

            def fast_scatter():
                pool.wait_ge(s["rec_se"], 2)
                for k in range(2):
                    scatter(0, k)
                with pool.Fori(1, NG) as g:
                    pool.wait_ge(s["rec_se"], g + 2)
                    for k in range(2):
                        pool.wait_ge(s[f"half{k}"], g * (16 * SH))
                        pool.sem_inc(s["landed"], 1)
                        scatter(g, k)
                for k in range(2):
                    pool.wait_ge(s[f"half{k}"], NG * 16 * SH)
                    pool.sem_inc(s["landed"], 1)

            def any_tiles(k):
                kind, table, result, gathers = passes[k]
                n0, in0 = any_counts(k)
                with pool.Fori(0, NT) as t:
                    pool.wait_ge(s["g_keys"], t + (n0 + 1))
                    pool.sem_inc(s["g_armed"], 1)

                    def gather(rows, t_, col, w):
                        pool.indirect_dma_start(out=rows[:, 0:w], out_offset=None, in_=t_,
                                                in_offset=bass.IndirectOffsetOnAxis(ap=g_ki[:, col:col + 1], axis=0))\
                            .then_inc(s["g_in"], 16)
                    gather(g_a, table, 0, table.shape[1])
                    if kind == "max":
                        gather(g_b, g_h, 1, GW)
                    elif kind == "sum":
                        gather(g_b, g_max, 1, H)
                    gather(g_old, result, 1, result.shape[1])
                    pool.wait_ge(s["g_news"], t + (n0 + 1))
                    pool.sem_inc(s["g_armed"], 1)
                    pool.indirect_dma_start(out=result, out_offset=bass.IndirectOffsetOnAxis(ap=g_so[:, 0:1], axis=0),
                                            in_=g_new[:, 0:result.shape[1]], in_offset=None).then_inc(s["g_out"], 16)
                    pool.wait_ge(s["g_out"], t * 16 + (n0 + 1) * 16)
                    pool.sem_inc(s["g_done"], 1)

            def any_layers():
                pool.memset(g_src[:, :], NP).then_inc(s["g_init"], 1)
                pool.memset(g_dst[:, :], NP).then_inc(s["g_init"], 1)
                pool.memset(g_zero[:, :], 0.0).then_inc(s["g_init"], 1)
                pool.memset(g_low[:, :], 1.0).then_inc(s["g_init"], 1)
                pool.iota(g_trash[:, :], pattern=[[0, 1]], base=NP + P, channel_multiplier=1,
                          allow_small_or_imprecise_dtypes=True).then_inc(s["g_init"], 1)
                pool.wait_ge(s["g_init"], 5)
                pool.affine_select(out=g_low[:, :], in_=g_low[:, :], compare_op=ALU.is_ge, fill=0.0, base=-1,
                                   pattern=[[-1, P]], channel_multiplier=1).then_inc(s["g_init"], 1)
                pool.sem_inc(s["g_done"], 1)
                pool.wait_ge(s["g_x0"], 16)
                for k in range(LAYERS):
                    any_tiles(k)

            def any_attention():
                pool.wait_ge(s["g_hr"], 16)
                for k in range(LAYERS, len(passes)):
                    any_tiles(k)

            pool.wait_ge(s["flag_ready"], 1)
            plain = pool.value_load(flag[0:1, 0:1], min_val=0, max_val=1)
            with pool.If(plain):
                fast_scatter()
            with pool.Else():
                any_layers()
            with pool.If(plain):
                pool.sem_inc(s["block_in"], 1)
            with pool.Else():
                any_attention()

        @block.tensor
        def _(pe):
            for u in range(RING):
                pe.sem_inc(s[f"a_used{u}"], 1)
            pe.wait_ge(s["consts"], 16)
            pe.wait_ge(s["ld_w"], 16 * (H + 3))
            pe.transpose(bank[0][:, 0:D], wn[:, :], ident[:, :])
            pe.matmul(bank[1][:, 0:2 * H], wn[:, :], acat[:, 0:2, :].rearrange("p k h -> p (k h)"),
                      start=True, stop=True)
            pe.matmul(bank[2][:, 0:H], we2[:, :, :].rearrange("p k d -> p (k d)"), acat[:, 2, :],
                      start=True, stop=True).then_inc(s["wt_ps"], 1)
            pe.wait_ge(s["first_ready"], 1)
            pe.matmul(bank[3][:, 0:P], ones[:, :], diag[:, :], start=True, stop=True).then_inc(s["ahead_bc"], 1)
            pe.wait_ge(s["ahead_ready"], 1)
            pe.matmul(bank[4][:, 0:NB], ahead[:, :], lasts[:, :], start=True, stop=True).then_inc(s["base_ps"], 1)

            pe.wait_ge(s["wt_sb"], 1)
            chunks = [list(range(u, min(u + BPB, SH))) for u in range(0, SH, BPB)]
            NC = len(chunks)

            def group(g, buf, load_count):
                pe.wait_ge(s[f"ea{buf}"], load_count)
                for ci in range(NC + 1):
                    if ci < NC:
                        r = ci % 2
                        if ci:
                            pe.wait_ge(s["eaT_sb"], g * NC + (ci - 1))
                        for k, u in enumerate(chunks[ci]):
                            m = pe.transpose(bank[5 + r][:, k * P:(k + 1) * P],
                                             ea[:, buf, u, :, :].rearrange("p k d -> p (k d)"), ident[:, :])
                        m.then_inc(s["eaT_ps"], 1)
                    if ci >= 1:
                        if ci == 1:
                            pe.wait_ge(s["rec_se"], g + 1)
                        pe.wait_ge(s["eaT_sb"], g * NC + ci)
                        for k, u in enumerate(chunks[ci - 1]):
                            m = pe.matmul(bank[7][:, u * 2 * H:(u + 1) * 2 * H],
                                          eaT[:, (ci - 1) % 2, k * P:(k + 1) * P], wedge[:, :], start=True, stop=True)
                m.then_inc(s["se_ps"], 1)

            for buf in range(2):
                group(buf, buf, 32)

            pe.wait_ge(s["bad_sb"], 1)
            pe.matmul(bank[3][:, 0:P], ones[:, :], diag[:, :], start=True, stop=True).then_inc(s["key_bc2"], 1)
            pe.wait_ge(s["bad_sb"], 2)
            pe.matmul(bank[4][:, 0:1], ones[:, :], bad[:, 3:4], start=True, stop=True).then_inc(s["bad_ps"], 1)
            pe.wait_ge(s["place_ready"], 1)
            for n in range(4 * TR):
                f, b = n // TR, n % TR
                if n >= 2:
                    pe.wait_ge(s["place_sb"], n - 1)
                a = (rank, w_r, src1, dst1)[f]
                pe.transpose(bank[n % 2][:, 0:P], a[:, b * P:(b + 1) * P], ident[:, :]).then_inc(s["place_ps"], 1)
            pe.wait_ge(s["upto_sb"], 1)
            pe.matmul(bank[2][:, 0:NB], ones[:, :], upto[:, :], start=True, stop=True).then_inc(s["upto_ps"], 1)
            with pe.Fori(1, NG // 2) as g2:
                for buf in range(2):
                    group(g2 * 2 + buf, buf, (g2 + 1) * 32)
            group(NG - 1, 0, NG // 2 * 32 + 48)

            def fast_layers():
                groups = banks_of(NB)
                pe.wait_ge(s["rec_se"], NG + 1)
                with pe.Fori(0, NB) as j:
                    for i in range(NB):
                        if i % BPB == 0:
                            pe.wait_ge(s["row_free"], j * len(groups) + (i // BPB + 1))
                        n = 0
                        for t in (2 * i, 2 * i + 1):
                            c, u = divmod(t, HT)
                            if u == 0:
                                pe.wait_ge(s["oh_ready"], j * 2 + (c + 1))
                            for k in range(3):
                                m = pe.matmul(bank[i // BPB][:, i % BPB * P:(i % BPB + 1) * P], oh_d[:, c, :, u],
                                              oh_w[:, c, k, :, u], start=(n == 0), stop=(n == 5))
                                n += 1
                        if i == groups[i // BPB][-1]:
                            m.then_inc(s["row_ps"], 1)
                        elif 2 * i + 1 == HT - 1:
                            m.then_inc(s["oh_used0"], 1)
                    pe.wait_ge(s["row_add"], j + 1)
                    for k in range(3):
                        m = pe.matmul(bank[7][:, 0:P], oh_d[:, 1, :, BT - 1 - HT], oh_w[:, 1, k, :, BT - 1 - HT],
                                      start=(k == 0), stop=(k == 2))
                    m.then_inc(s["diag_ps"], 1)

                with pe.Fori(0, LAYERS) as l:
                    pe.wait_ge(s["row_sb"], NB * len(groups))
                    pe.wait_ge(s["cur_sb"], l * len(groups) + 1)
                    for g, bs in enumerate(groups):
                        pe.matmul(bank[g][:, 0:len(bs) * P], zerob[:, 0:P], zerob[:, 0:len(bs) * P], start=True, stop=False)
                    with pe.Fori(0, NB // RING) as r:
                        for u in range(RING):
                            pe.wait_ge(s[f"a{u}"], (l * (NB // RING) + r + 1) * 16)
                            pe.wait_ge(s["stage_sb"], l * NB + r * RING + (u + 1))
                            for g, bs in enumerate(groups):
                                w = len(bs) * P
                                m = pe.matmul(bank[g][:, 0:w], stage[:, u, :], ablk[:, u, g * BANK:g * BANK + w],
                                              start=False, stop=False)
                            m.then_inc(s[f"a_used{u}"], 1)
                    for g, bs in enumerate(groups):
                        m = pe.matmul(bank[g][:, 0:len(bs) * P], zerob[:, 0:P], zerob[:, 0:len(bs) * P], start=False, stop=True)
                        m.then_inc(s["lay_ps"], 1)
                    for g, bs in enumerate(groups):
                        pe.wait_ge(s["lay_sb"], l * len(groups) + (g + 1))
                        for k, b in enumerate(bs):
                            m = pe.transpose(bank[g][:, k * P:(k + 1) * P], curT[:, b * P:(b + 1) * P], ident[:, :])
                        m.then_inc(s["lay_T"], 1)

            def any_tiles(k):
                kind = passes[k][0]
                w = {"spmm": D, "max": H * P, "sum": MW}[kind]
                n0 = any_counts(k)[0]
                with pe.Fori(0, NT) as t:
                    pe.wait_ge(s["g_keys"], t + (n0 + 1))
                    pe.matmul(bank[0][:, 0:P], ones[:, :], g_diag[:, 0, :], start=True, stop=True).then_inc(s["g_bc"], 1)
                    pe.wait_ge(s["g_msgs"], t + (n0 + 1))
                    if kind == "max":
                        m = pe.matmul(bank[1][:, :], ones[:, :], g_diag[:, :, :].rearrange("p h n -> p (h n)"), start=True, stop=True)
                    else:
                        m = pe.matmul(bank[1][:, 0:w], g_same[:, :], g_msg[:, 0:w], start=True, stop=True)
                    m.then_inc(s["g_tot"], 1)

            def any_layers():
                for k in range(LAYERS):
                    any_tiles(k)

            def any_attention():
                for k in range(LAYERS, len(passes)):
                    any_tiles(k)

            pe.wait_ge(s["flag_ready"], 1)
            plain = pe.value_load(flag[0:1, 0:1], min_val=0, max_val=1)
            with pe.If(plain):
                fast_layers()
            with pe.Else():
                any_layers()
            groups = banks_of(NB)
            pe.wait_ge(s["x1_ready"], 1)
            for g, bs in enumerate(groups):
                for k, b in enumerate(bs):
                    m = pe.transpose(bank[g][:, k * P:(k + 1) * P], cur[:, b, :], ident[:, :])
                m.then_inc(s["x1T_ps"], 1)
            W = D + 2 * H
            for b in range(NB):
                g, k = divmod(b, 3)
                if k == 0:
                    pe.wait_ge(s["x1T_sb"], len(groups))
                    if g >= 8:
                        pe.wait_ge(s["h_sb"], g - 7)
                m = pe.matmul(bank[g % 8][:, k * W:(k + 1) * W], curT[:, b * P:(b + 1) * P], wext[:, :],
                              start=True, stop=True)
                if k == 2 or b == NB - 1:
                    m.then_inc(s["h_ps"], 1)
            pe.wait_ge(s["h_split"], 1)

            NQ = BTP // BPB

            def block_rows(j):
                return hsp[:, bass.ds(j, 1), :, :].rearrange("p o k n -> p (o k) n")

            def src_rows(t, j):
                return hsp[:, t // 2, :, :] if t < BT - 1 else block_rows(j)

            def turn(j, par, lo, hi):
                for q in range(lo, hi):
                    if q == 0:
                        pe.wait_ge(s["s6_ready"], j + 1)
                        pe.wait_ge(s["d16_ready"], j + 1)
                    if q >= 2:
                        pe.wait_ge(s["tr_sb"], j * (2 * NQ) + 2 * (q - 1))
                    for k, rows in enumerate((d16, s6)):
                        for v in range(BPB):
                            m = pe.transpose(bank[q % 2][:, k * BANK // 2:(k + 1) * BANK // 2].bitcast(BF16)[:, v * P:(v + 1) * P],
                                             rows[:, :, BPB * q + v], identb[:, :])
                    m.then_inc(s["tr_ps"], 1)

            def gather_h(j, par, q):
                if q >= 2:
                    pe.wait_ge(s["msg_sb"], j * NQ + (q - 1))
                for v in range(BPB):
                    t = BPB * q + v
                    if t < BT:
                        for k in range(3):
                            m = pe.matmul(bank[3 + q % 2][:, v * P:(v + 1) * P], sT[:, par, t, :], src_rows(t, j)[:, k, 0:D],
                                          start=(k == 0), stop=(k == 2))
                m.then_inc(s["hg_ps"], 1)

            def sum_dst(j, par, q):
                if q == 0:
                    pe.wait_ge(s["num_free"], j + 1)
                    pe.wait_ge(s["d6_ready"], j + 1)
                pe.wait_ge(s["msg_sb"], j * NQ + (q + 1))
                for v in range(BPB):
                    t = BPB * q + v
                    if t < BT:
                        m = pe.matmul(bank[2][:, 0:MW], d6[:, par, t, :], msg[:, q % 2, v, :],
                                      start=(t == 0), stop=(t == BT - 1))
                m.then_inc(s["msg_used"], 1)

            def step(j, par, sums=True):
                def sums_of(lo, hi):
                    for q in range(lo, hi):
                        if sums:
                            if q < NQ:
                                gather_h(j - 1, 1 - par, q)
                            if q >= 1:
                                sum_dst(j - 1, 1 - par, q - 1)
                for part in range(6):
                    turn(j, par, 2 * part, 2 * part + 2 if part < 5 else NQ)
                    sums_of(part, part + 1)
                for t in range(BT):
                    if t % BPB == 0:
                        pe.wait_ge(s["tr_sb"], j * (2 * NQ) + (2 * (t // BPB) + 2))
                    o = bank[5 + t // 40][:, t % 40 * 3 * H:(t % 40 + 1) * 3 * H]
                    pe.matmul(o, sT[:, par, t, :], src_rows(t, j)[:, :, D:D + H], start=True, stop=False)
                    m = pe.matmul(o, dT[:, t, :], block_rows(j)[:, :, D + H:D + 2 * H], start=False, stop=True)
                m.then_inc(s["at_ps"], 1)
                sums_of(6, 7)
                pe.wait_ge(s["at_sb"], j + 1)
                for k in range(2):
                    for n, a in enumerate((sc, dlr)):
                        m = pe.transpose(bank[7][0:HT * H, (2 * n + k) * P:(2 * n + k + 1) * P],
                                         a[:, k * HT:(k + 1) * HT, :].rearrange("p t h -> p (t h)"), ident[:, :])
                m.then_inc(s["atT_ps"], 1)
                sums_of(7, 9)
                pe.wait_ge(s["z_sb"], j + 1)
                for k in range(2):
                    m = pe.transpose(bank[7][:, k * HT * H:(k + 1) * HT * H], run[0:HT * H, k, :], ident[0:HT * H, 0:HT * H])
                m.then_inc(s["zT_ps"], 1)
                sums_of(9, 10)
                pe.wait_ge(s["zs_sb"], j + 1)
                for t in range(BT):
                    m = pe.matmul(bank[5 + t // 40][:, t % 40 * 3 * H:(t % 40 + 1) * 3 * H], d16[:, :, t],
                                  zsp[:, :, t, :], start=True, stop=True)
                m.then_inc(s["v_ps"], 1)
                sums_of(10, 12)
                pe.wait_ge(s["m_sb"], j + 1)
                for t in range(BT):
                    m = pe.matmul(bank[6 + t // 40][:, t % 40 * 3 * H:(t % 40 + 1) * 3 * H], dT[:, t, :],
                                  msp[:, :, :].rearrange("p k h -> p (k h)"), start=True, stop=True)
                m.then_inc(s["mg_ps"], 1)
                sums_of(12, NQ + 1)

            def fast_attention():
                step(0, 0, sums=False)
                with pe.Fori(0, (NB - 1) // 2) as i:
                    step(i * 2 + 1, 1)
                    step(i * 2 + 2, 0)
                for q in range(NQ + 1):
                    if q < NQ:
                        gather_h(NB - 1, 0, q)
                    if q >= 1:
                        sum_dst(NB - 1, 0, q - 1)

            with pe.If(plain):
                fast_attention()
            with pe.Else():
                any_attention()

        @block.scalar
        def _(act):
            act.sem_inc(s["rec_se"], 1)
            act.sem_inc(s["row_free"], len(banks_of(NB)))
            act.wait_ge(s["wt_ps"], 1)
            act.copy(wext[:, 0:D], bank[0][:, 0:D])
            act.copy(wext[:, D:D + 2 * H], bank[1][:, 0:2 * H])
            act.mul(wedge[:, :], ones[:, 0:2 * H], 0.0)
            act.drain()
            act.copy(wedge[0:DE, 0:H], bank[2][0:DE, 0:H])
            act.copy(wedge[DE:2 * DE, H:2 * H], bank[2][DE:2 * DE, 0:H])
            act.drain()
            act.nop().then_inc(s["wt_sb"], 1)
            NC = -(-SH // BPB)

            def group(g):
                for ci in range(NC):
                    act.wait_ge(s["eaT_ps"], g * NC + (ci + 1))
                    w = (min(SH, BPB * (ci + 1)) - BPB * ci) * P
                    act.copy(eaT[:, ci % 2, 0:w], bank[5 + ci % 2][:, 0:w]).then_inc(s["eaT_sb"], 1)
                act.wait_ge(s["se_ps"], g + 1)
                act.copy(rec[:, bass.ds(g * SG, SG), H:2 * H].rearrange("p (k u) f -> p u k f", k=2),
                         bank[7][:, 0:SH * 2 * H].rearrange("p (u k f) -> p u k f", k=2, f=H)).then_inc(s["rec_se"], 1)

            with act.Fori(0, NG // 2) as g2:
                for b in range(2):
                    group(g2 * 2 + b)
            group(NG - 1)
            act.nop().then_inc(s["edge_done"], 1)

            def fast_layers():
                groups = banks_of(NB)
                with act.Fori(0, NB) as j:
                    for g, bs in enumerate(groups):
                        act.wait_ge(s["row_ps"], j * len(groups) + (g + 1))
                        act.copy(arow[:, g * BANK:g * BANK + len(bs) * P], bank[g][:, 0:len(bs) * P])
                        act.drain()
                        act.nop().then_inc(s["row_free"], 1)
                        act.nop().then_inc(s["row_sb"], 1)
                    act.wait_ge(s["row_add"], j + 2)
                    act.dma_start(adj[bass.ds(j, 1), :, :].rearrange("o p n -> (o p) n"), arow[:, :])\
                        .then_inc(s["adj_out"], 16)
                    act.wait_ge(s["adj_out"], j * 16 + 16)

                with act.Fori(0, LAYERS) as l:
                    act.wait_ge(s["cur_sb"], l * len(groups) + 1)
                    with act.Fori(0, NB // RING) as r:
                        for u in range(RING):
                            act.wait_ge(s[f"a_used{u}"], l * (NB // RING) + r + 1)
                            act.copy(stage[:, u, :], cur[:, bass.ds(r * RING + u, 1), :].rearrange("p o n -> p (o n)"))\
                                .then_inc(s["stage_sb"], 1)
                    for g, bs in enumerate(groups):
                        act.wait_ge(s["lay_ps"], l * len(groups) + (g + 1))
                        act.copy(curT[:, g * BANK:g * BANK + len(bs) * P], bank[g][:, 0:len(bs) * P]).then_inc(s["lay_sb"], 1)

            def any_attention():
                with act.Fori(0, NT) as t:
                    act.wait_ge(s["g_arg"], t + 1)
                    act.activation(g_s[:, 2, :], g_s[:, 1, :], ACT.Exp).then_inc(s["g_ex"], 1)
                act.wait_ge(s["g_fin"], 32)
                act.activation(g_e[:, :, :], g_m[:, :, :], ACT.Exp, scale=-1.0).then_inc(s["g_emn"], 1)

            act.wait_ge(s["flag_ready"], 1)
            plain = act.value_load(flag[0:1, 0:1], min_val=0, max_val=1)
            with act.If(plain):
                fast_layers()
            groups = banks_of(NB)
            act.wait_ge(s["rs_var"], 1)
            act.activation(st[:, 2, :], st[:, 1, :], ACT.Sqrt).then_inc(s["rs_std"], 1)
            for g, bs in enumerate(groups):
                act.wait_ge(s["x1T_ps"], g + 1)
                act.copy(curT[:, g * BANK:g * BANK + len(bs) * P], bank[g][:, 0:len(bs) * P]).then_inc(s["x1T_sb"], 1)
            W = D + 2 * H
            for g in range(-(-NB // 3)):
                n = min(NB, 3 * g + 3) - 3 * g
                act.wait_ge(s["h_ps"], g + 1)
                act.copy(hx[:, 3 * g:3 * g + n, :].rearrange("p b n -> p (b n)"), bank[g % 8][:, 0:n * W]).then_inc(s["h_sb"], 1)
            act.wait_ge(s["h_split"], 1)

            NQ = BTP // BPB

            def step(j, par):
                for q in range(NQ):
                    act.wait_ge(s["tr_ps"], j * NQ + (q + 1))
                    for k, rows in enumerate((dT[:, BPB * q:BPB * (q + 1), :], sT[:, par, BPB * q:BPB * (q + 1), :])):
                        act.copy(rows.rearrange("p t n -> p (t n)"),
                                 bank[q % 2][:, k * BANK // 2:(k + 1) * BANK // 2].bitcast(BF16)).then_inc(s["tr_sb"], 1)
                act.copy(d6[:, par, :, :], d16[:, :, :].rearrange("p n t -> p t n")).then_inc(s["d6_ready"], 1)
                act.wait_ge(s["m_sb"], j + 1)
                act.activation(emn[:, par, :], mm[:, 0, :], ACT.Exp, scale=-1.0).then_inc(s["emn_sb"], 1)
                act.wait_ge(s["arg_sb"], j + 1)
                act.activation(ex[:, par, 0:BT, 0:H], me[:, 0:BT, :], ACT.Exp).then_inc(s["ex_sb"], 1)

            def fast_attention():
                step(0, 0)
                with act.Fori(0, (NB - 1) // 2) as i:
                    step(i * 2 + 1, 1)
                    step(i * 2 + 2, 0)

            with act.If(plain):
                fast_attention()
            with act.Else():
                any_attention()
            act.wait_ge(s["rs_var"], 2)
            act.activation(st[:, 2, :], st[:, 1, :], ACT.Sqrt).then_inc(s["rs_std"], 1)

        @block.vector
        def _(dve):
            def norm(dest, a, part):
                mean, var, std = st[:, 0, :], st[:, 1, :], st[:, 2, :]
                wide = lambda v: v.rearrange("p (b o) -> p b o", o=1).broadcast_to([P, NB, D])
                dve.tensor_reduce(mean, a, AX.X, ALU.add)
                dve.drain()
                dve.tensor_scalar(mean, mean, 1.0 / D, None, ALU.mult)
                dve.drain()
                dve.tensor_tensor(a, a, wide(mean), ALU.subtract)
                dve.drain()
                dve.tensor_tensor(dest, a, a, ALU.mult)
                dve.drain()
                dve.tensor_reduce(var, dest, AX.X, ALU.add)
                dve.drain()
                dve.tensor_scalar(var, var, 1.0 / D, EPS, ALU.mult, ALU.add)
                dve.drain()
                dve.nop().then_inc(s["rs_var"], 1)
                dve.wait_ge(s["rs_std"], part)
                dve.reciprocal(st[:, 3, :], std)
                dve.drain()
                dve.tensor_tensor(dest, a, wide(st[:, 3, :]), ALU.mult)
                dve.drain()

            for n in ("r3_free0", "r3_free1", "r6_free", "row_add", "num_free"):
                dve.sem_inc(s[n], 1)
            dve.wait_ge(s["ld_idx"], 64)
            dve.wait_ge(s["consts"], 16)
            dve.tensor_single_scalar(ti[:, 0, :], dst_i[:, :], 7, op=ALU.arith_shift_right)
            dve.tensor_single_scalar(ti[:, 1, :], src_i[:, :], 7, op=ALU.arith_shift_right)
            dve.drain()
            dve.tensor_copy(dstb[:, :], ti[:, 0, :])
            dve.tensor_copy(srcb[:, :], ti[:, 1, :])
            dve.drain()
            dve.tensor_scalar(diag[:, :], ident[:, :], dstb[:, 0:1], None, ALU.mult)
            dve.drain()
            dve.nop().then_inc(s["first_ready"], 1)
            dve.tensor_single_scalar(ti[:, 0, :], dst_i[:, :], P - 1, op=ALU.bitwise_and)
            dve.tensor_single_scalar(ti[:, 1, :], src_i[:, :], P - 1, op=ALU.bitwise_and)
            dve.tensor_tensor(same[:, 1:RW], dstb[:, 1:RW], dstb[:, 0:RW - 1], ALU.is_equal)
            dve.memset(same[:, 0:1], 1.0)
            dve.tensor_scalar(tmp[:, 0, :], srcb[:, :], 1.0, None, ALU.add)
            dve.drain()
            dve.scalar_tensor_tensor(out=tmp[:, 1, :], in0=dstb[:, :], scalar=dstb[:, RW - 1:RW], in1=tmp[:, 0, :],
                                     op0=ALU.is_equal, op1=ALU.mult)
            dve.tensor_scalar(dst1[:, :], ti[:, 0, :], 1.0, None, ALU.add)
            dve.tensor_scalar(src1[:, :], ti[:, 1, :], 1.0, None, ALU.add)
            dve.drain()
            for i in range(NB):
                dve.tensor_scalar(tmp[:, 2 + i % 2, :], tmp[:, 1, :], float(i + 1), 0.0, ALU.is_equal, ALU.add,
                                  accum_out=lasts[:, i:i + 1])
                dve.drain()
            dve.wait_ge(s["ahead_bc"], 1)
            dve.scalar_tensor_tensor(out=ahead[:, :], in0=bank[3][:, 0:P], scalar=dstb[:, RW - 1:RW], in1=upper[:, :],
                                     op0=ALU.is_equal, op1=ALU.mult)
            dve.drain()
            dve.nop().then_inc(s["ahead_ready"], 1)
            dve.wait_ge(s["base_ps"], 1)
            dve.tensor_copy(base[:, :], bank[4][:, 0:NB])
            dve.memset(rank[:, :], -1.0)
            dve.drain()
            for i in range(NB):
                dve.tensor_scalar(tmp[:, 0, :], srcb[:, :], float(i), None, ALU.is_equal)
                dve.drain()
                dve.tensor_tensor_scan(tmp[:, 1, :], same[:, :], tmp[:, 0, :], base[:, i:i + 1], ALU.mult, ALU.add)
                dve.drain()
                dve.tensor_tensor(tmp[:, 2, :], tmp[:, 0, :], tmp[:, 1, :], ALU.mult)
                dve.drain()
                dve.tensor_tensor(rank[:, :], rank[:, :], tmp[:, 2, :], ALU.add)
                dve.drain()
            dve.scalar_tensor_tensor(out=tmp[:, 3, :], in0=dstb[:, :], scalar=float(P), in1=dst1[:, :], op0=ALU.mult, op1=ALU.add)
            dve.drain()
            dve.tensor_scalar(diag[:, :], ident[:, :], tmp[:, 3, 0:1], None, ALU.mult)
            dve.tensor_tensor(tmp[:, 2, 1:RW], tmp[:, 3, 1:RW], tmp[:, 3, 0:RW - 1], ALU.is_lt)
            dve.drain()
            dve.sem_inc(s["bad_sb"], 1)
            dve.tensor_reduce(bad[:, 0:1], tmp[:, 2, 1:RW], AX.X, ALU.max)
            dve.wait_ge(s["key_bc2"], 1)
            dve.scalar_tensor_tensor(out=ahead[:, :], in0=bank[3][:, 0:P], scalar=tmp[:, 3, RW - 1:RW], in1=upper[:, :],
                                     op0=ALU.is_lt, op1=ALU.mult)
            dve.drain()
            dve.tensor_reduce(bad[:, 1:2], ahead[:, :], AX.X, ALU.max)
            dve.drain()
            dve.tensor_copy(ti[:, 0, :], rank[:, :])
            dve.drain()
            dve.tensor_single_scalar(ti[:, 1, :], ti[:, 0, :], 7, op=ALU.arith_shift_right)
            dve.drain()
            dve.tensor_single_scalar(ti[:, 0, :], ti[:, 0, :], P - 1, op=ALU.bitwise_and)
            dve.tensor_copy(tmp[:, 0, :], ti[:, 1, :])
            dve.drain()
            dve.tensor_copy(rank[:, :], ti[:, 0, :])
            dve.scalar_tensor_tensor(out=tmp[:, 1, :], in0=srcb[:, :], scalar=2.0, in1=tmp[:, 0, :],
                                     op0=ALU.mult, op1=ALU.add)
            dve.drain()
            dve.tensor_tensor(tmp[:, 2, :], dstb[:, :], srcb[:, :], ALU.is_equal)
            dve.drain()
            dve.tensor_tensor(tmp[:, 3, :], tmp[:, 0, :], tmp[:, 2, :], ALU.subtract)
            dve.drain()
            dve.tensor_reduce(bad[:, 2:3], tmp[:, 3, :], AX.X, ALU.max)
            dve.drain()
            dve.tensor_scalar(bad[:, 2:3], bad[:, 2:3], 2.0, None, ALU.is_ge)
            dve.drain()
            dve.tensor_reduce(bad[:, 3:4], bad[:, 0:3], AX.X, ALU.add)
            dve.drain()
            dve.sem_inc(s["bad_sb"], 1)
            dve.tensor_scalar(tmp[:, 2, :], tmp[:, 1, :], -1.0, float(BT - 1), ALU.mult, ALU.add)
            dve.tensor_scalar(tmp[:, 3, :], tmp[:, 0, :], 2.0, None, ALU.is_equal)
            dve.drain()
            dve.tensor_tensor(tmp[:, 2, :], tmp[:, 2, :], tmp[:, 3, :], ALU.mult)
            dve.scalar_tensor_tensor(out=tmp[:, 1, :], in0=dstb[:, :], scalar=float(BT), in1=tmp[:, 1, :],
                                     op0=ALU.mult, op1=ALU.add)
            dve.drain()
            dve.tensor_tensor(tmp[:, 1, :], tmp[:, 1, :], tmp[:, 2, :], ALU.add)
            dve.drain()
            dve.scalar_tensor_tensor(out=rank[:, :], in0=rank[:, :], scalar=float(NB * BT), in1=tmp[:, 1, :],
                                     op0=ALU.mult, op1=ALU.add)
            dve.wait_ge(s["ld_x"], 64)
            dve.drain()
            dve.nop().then_inc(s["place_ready"], 1)
            dve.wait_ge(s["bad_ps"], 1)
            dve.tensor_scalar(flag[:, :], bank[4][:, 0:1], 0.0, None, ALU.is_equal)
            dve.drain()
            dve.sem_inc(s["flag_ready"], 1)
            for n in range(4 * TR):
                f, b = n // TR, n % TR
                o = (slot_i[:, :] if f == 0 else rec[:, :, f - 1]).rearrange("q (r b) -> q r b", b=TR)[:, :, b]
                dve.wait_ge(s["place_ps"], n + 1)
                dve.tensor_copy(o, bank[n % 2][:, 0:RR]).then_inc(s["place_sb"], 1)
            dve.drain()
            dve.tensor_copy(fix[:, 0:1], slot_i[:, NT - 1:NT])
            dve.drain()
            dve.tensor_tensor(fix[:, 1:2], fix[:, 0:1], trash[:, 0:1], ALU.subtract)
            dve.drain()
            dve.tensor_tensor(fix[:, 0:1], fix[:, 1:2], trash[:, 1:2], ALU.mult)
            dve.drain()
            dve.tensor_tensor(slot_i[:, NT - 1:NT], fix[:, 0:1], trash[:, 0:1], ALU.add)
            dve.drain()
            dve.nop().then_inc(s["rec_ready"], 1)
            for i in range(NB):
                dve.tensor_scalar(tmp[:, i % 2, :], dstb[:, :], float(i), 0.0, ALU.is_le, ALU.add,
                                  accum_out=upto[:, i:i + 1])
                dve.drain()
            dve.nop().then_inc(s["upto_sb"], 1)
            dve.wait_ge(s["upto_ps"], 1)
            dve.tensor_scalar(need_f[:, :], bank[2][:, 0:NB], 1.0 / (SH * P), 1.0, ALU.mult, ALU.add)
            dve.drain()
            dve.tensor_scalar(need[:, :], need_f[:, :], float(2 * NG), None, ALU.min)
            dve.drain()
            dve.nop().then_inc(s["need_ready"], 1)
            dve.nop().then_inc(s["edge_done"], 1)

            def fast_layers():
                dve.wait_ge(s["edge_done"], 2)
                dve.memset(r3[:, 1, HT - 1:HT, :], 0.0)
                iota_h = iota_nt[:, :, 0:HT]
                tall = lambda a: a.rearrange("p (o t) -> p o t", o=1).broadcast_to([P, P, HT])
                def one_hots(j, c):
                    dve.wait_ge(s["r3a" if c == 0 else "r3b"], j * 16 + 16)
                    r = r3[:, c, :, :]
                    dve.tensor_copy(loc[:, c, 0, :], r[:, :, 1])
                    dve.tensor_copy(loc[:, c, 1, :], r[:, :, 2])
                    dve.tensor_copy(wsp[:, c, 0, :], r[:, :, 0])
                    dve.drain()
                    dve.tensor_tensor(wres[:, c, 0, :], r[:, :, 0], wsp[:, c, 0, :], ALU.subtract)
                    dve.drain()
                    dve.nop().then_inc(s[f"r3_free{c}"], 1)
                    dve.tensor_copy(wsp[:, c, 1, :], wres[:, c, 0, :])
                    dve.drain()
                    dve.tensor_tensor(wres[:, c, 1, :], wres[:, c, 0, :], wsp[:, c, 1, :], ALU.subtract)
                    dve.drain()
                    dve.tensor_copy(wsp[:, c, 2, :], wres[:, c, 1, :])
                    dve.wait_ge(s["oh_used0" if c == 0 else "diag_ps"], j)
                    dve.tensor_tensor(oh_s[:, c, :, :], iota_h, tall(loc[:, c, 0, :]), ALU.is_equal)
                    dve.tensor_tensor(oh_d[:, c, :, :], iota_h, tall(loc[:, c, 1, :]), ALU.is_equal)
                    dve.drain()
                    for k in range(3):
                        dve.tensor_tensor(oh_w[:, c, k, :, :], oh_s[:, c, :, :], tall(wsp[:, c, k, :]), ALU.mult)
                    dve.drain()
                    dve.nop().then_inc(s["oh_ready"], 1)

                def add_diagonal(j):
                    dve.wait_ge(s["row_sb"], (j + 1) * len(banks_of(NB)))
                    dve.wait_ge(s["diag_ps"], j + 1)
                    a = arow[:, bass.ds(j * P, P)]
                    dve.tensor_tensor(a, a, bank[7][:, 0:P], ALU.add)
                    dve.drain()
                    dve.nop().then_inc(s["row_add"], 1)

                one_hots(0, 0)
                one_hots(0, 1)
                with dve.Fori(1, NB) as j:
                    one_hots(j, 0)
                    add_diagonal(j - 1)
                    one_hots(j, 1)
                add_diagonal(NB - 1)

                groups = banks_of(NB)
                NGR = len(groups)
                dve.tensor_copy(cur[:, :, :], xs[:, :, :])
                dve.tensor_scalar(acc[:, :, :], xs[:, :, :], 2.0, None, ALU.mult)
                dve.drain()
                dve.nop().then_inc(s["cur_sb"], 1)
                for l in range(LAYERS):
                    for g, bs in enumerate(groups):
                        n = len(bs)
                        dve.wait_ge(s["lay_T"], l * NGR + (g + 1))
                        dve.tensor_copy(cur[:, bs[0]:bs[0] + n, :].rearrange("p b n -> p (b n)"), bank[g][:, 0:n * P])
                        dve.tensor_tensor(acc[:, bs[0]:bs[0] + n, :].rearrange("p b n -> p (b n)"),
                                          acc[:, bs[0]:bs[0] + n, :].rearrange("p b n -> p (b n)"), bank[g][:, 0:n * P], ALU.add)
                        dve.drain()
                        dve.nop().then_inc(s["cur_sb"], 1)

            def any_tiles(k):
                kind = passes[k][0]
                n0, in0 = any_counts(k)
                gathers = passes[k][3]
                ia, ib = (g_dst, g_src) if kind == "spmm" else (g_src, g_dst)
                key, lead, shift, place = (g_key[:, c:c + 1] for c in range(4))
                with dve.Fori(0, NT) as t:
                    dve.wait_ge(s["g_done"], t + (n0 + 1))
                    dve.tensor_copy(g_ki[:, 0:1], ia[:, bass.ds(t, 1)])
                    dve.tensor_copy(g_ki[:, 1:2], ib[:, bass.ds(t, 1)])
                    dve.tensor_copy(key, ib[:, bass.ds(t, 1)])
                    dve.drain()
                    dve.tensor_scalar(g_diag[:, 0, :], ident[:, :], key, None, ALU.mult)
                    dve.drain()
                    dve.sem_inc(s["g_keys"], 1)
                    dve.wait_ge(s["g_bc"], t + (n0 + 1))
                    dve.tensor_scalar(g_same[:, :], bank[0][:, 0:P], key, None, ALU.is_equal)
                    dve.drain()
                    dve.tensor_tensor(g_tmp[:, 0, :], g_same[:, :], g_low[:, :], ALU.mult)
                    dve.tensor_tensor(shift, key, g_trash[:, :], ALU.subtract)
                    dve.drain()
                    dve.tensor_reduce(place, g_tmp[:, 0, :], AX.X, ALU.max)
                    dve.drain()
                    dve.tensor_scalar(lead, place, 0.0, None, ALU.is_equal)
                    dve.drain()
                    dve.tensor_tensor(place, lead, shift, ALU.mult)
                    dve.drain()
                    dve.tensor_tensor(g_so[:, :], place, g_trash[:, :], ALU.add)
                    dve.wait_ge(s["g_in"], t * (16 * gathers) + (in0 + 16 * gathers))
                    if kind == "spmm":
                        dve.tensor_scalar(g_msg[:, 0:D], g_a[:, 0:D], rec[:, bass.ds(t, 1), 0], None, ALU.mult)
                    elif kind == "max":
                        row = g_att[:, bass.ds(t, 1), :].rearrange("p o h -> p (o h)")
                        dve.tensor_tensor(g_s[:, 0, :], g_a[:, D:D + H], g_b[:, D + H:D + 2 * H], ALU.add)
                        dve.drain()
                        dve.tensor_tensor(g_s[:, 1, :], g_s[:, 0, :], row, ALU.add)
                        dve.drain()
                        dve.scalar_tensor_tensor(out=g_s[:, 2, :], in0=g_s[:, 1, :], scalar=0.2, in1=g_s[:, 1, :],
                                                 op0=ALU.mult, op1=ALU.max)
                        dve.drain()
                        dve.tensor_copy(row, g_s[:, 2, :])
                        for h in range(H):
                            dve.tensor_scalar(g_diag[:, h, :], ident[:, :], g_s[:, 2, h:h + 1], None, ALU.mult)
                    else:
                        dve.tensor_tensor(g_s[:, 1, :], g_att[:, bass.ds(t, 1), :].rearrange("p o h -> p (o h)"),
                                          g_b[:, 0:H], ALU.subtract)
                        dve.drain()
                        dve.sem_inc(s["g_arg"], 1)
                        dve.wait_ge(s["g_ex"], t + 1)
                        dve.tensor_tensor(g_msg[:, 0:D].rearrange("p (h d) -> p h d", h=H),
                                          g_a[:, 0:D].rearrange("p (h d) -> p h d", h=H),
                                          g_s[:, 2, :].rearrange("p (h o) -> p h o", o=1).broadcast_to([P, H, HD]), ALU.mult)
                        dve.tensor_copy(g_msg[:, D:D + H], g_s[:, 2, :])
                        dve.memset(g_msg[:, D + H:MW], 1.0)
                    dve.drain()
                    dve.sem_inc(s["g_msgs"], 1)
                    dve.wait_ge(s["g_tot"], t + (n0 + 1))
                    if kind == "max":
                        dve.tensor_tensor(g_tmp[:, :, :], bank[1][:, :].rearrange("p (h n) -> p h n", h=H),
                                          g_same[:, :].rearrange("p (o n) -> p o n", o=1).broadcast_to([P, H, P]), ALU.mult)
                        dve.drain()
                        dve.tensor_reduce(g_s[:, 3, :], g_tmp[:, :, :], AX.X, ALU.max)
                        dve.drain()
                        dve.tensor_tensor(g_new[:, 0:H], g_s[:, 3, :], g_old[:, 0:H], ALU.max)
                    else:
                        w = D if kind == "spmm" else MW
                        dve.tensor_tensor(g_new[:, 0:w], bank[1][:, 0:w], g_old[:, 0:w], ALU.add)
                    dve.drain()
                    dve.sem_inc(s["g_news"], 1)

            def any_layers():
                dve.wait_ge(s["g_init"], 6)
                dve.wait_ge(s["g_ld"], 64)
                dve.wait_ge(s["rec_se"], NG + 1)
                dve.tensor_copy(g_att[:, :, :], rec[:, 0:NT, H:2 * H])
                dve.tensor_scalar(acc[:, :, :], xs[:, :, :], 2.0, None, ALU.mult)
                dve.drain()
                for k in range(LAYERS):
                    any_tiles(k)
                dve.wait_ge(s["g_back"], 16 * LAYERS)
                for l in range(LAYERS):
                    dve.tensor_tensor(acc[:, :, :], acc[:, :, :], ablk[:, l, :].rearrange("p (b d) -> p b d", b=NB), ALU.add)
                    dve.drain()

            def any_attention():
                dve.tensor_tensor(hx, hsp[:, :, 0, :], hsp[:, :, 1, :], ALU.add)
                dve.drain()
                dve.tensor_tensor(hx, hx, hsp[:, :, 2, :], ALU.add)
                dve.drain()
                dve.sem_inc(s["g_hx"], 1)
                for k in range(LAYERS, len(passes)):
                    any_tiles(k)
                dve.wait_ge(s["g_fin"], 32)
                dve.wait_ge(s["g_emn"], 1)
                dve.tensor_scalar(g_m[:, :, :], g_num[:, :, D + H:MW].broadcast_to([P, NB, H]), -1.0, float(E), ALU.mult, ALU.add)
                dve.drain()
                dve.tensor_tensor(g_m[:, :, :], g_m[:, :, :], g_e[:, :, :], ALU.mult)
                dve.drain()
                dve.tensor_tensor(g_m[:, :, :], g_m[:, :, :], g_num[:, :, D:D + H], ALU.add)
                dve.drain()
                dve.reciprocal(g_e[:, :, :], g_m[:, :, :])
                dve.drain()
                for h in range(H):
                    dve.tensor_tensor(acc[:, :, h * HD:(h + 1) * HD], g_num[:, :, h * HD:(h + 1) * HD],
                                      g_e[:, :, h:h + 1].broadcast_to([P, NB, HD]), ALU.mult)
                dve.drain()

            dve.wait_ge(s["flag_ready"], 1)
            plain = dve.value_load(flag[0:1, 0:1], min_val=0, max_val=1)
            with dve.If(plain):
                fast_layers()
            with dve.Else():
                any_layers()
            groups = banks_of(NB)
            norm(cur[:, :, :], acc[:, :, :], 1)
            dve.nop().then_inc(s["x1_ready"], 1)
            dve.wait_ge(s["h_sb"], -(-NB // 3))
            for k in range(3):
                dve.tensor_copy(hsp[:, :, k, :], hx[:, :, :])
                dve.drain()
                if k < 2:
                    dve.tensor_tensor(hx[:, :, :], hx[:, :, :], hsp[:, :, k, :], ALU.subtract)
                    dve.drain()
            dve.nop().then_inc(s["h_split"], 1)

            NQ = BTP // BPB
            RH = HT * H

            def take_records(j):
                dve.wait_ge(s["r6_in"], j * 16 + 16)
                dve.tensor_copy(loc6[:, 0, :], r6[:, :, 1])
                dve.tensor_copy(loc6[:, 1, :], r6[:, :, 2])
                dve.tensor_copy(dlr[:, :, :], r6[:, :, 2:3].broadcast_to([P, BTP, H]))
                dve.drain()

            def one_hot(rows, local, ready):
                dve.tensor_tensor(rows[:, :, :], iota_nt[:, :, :],
                                  local.rearrange("p (o t) -> p o t", o=1).broadcast_to([P, P, BTP]), ALU.is_equal)\
                    .then_inc(s[ready], 1)

            def messages(j, par, lo, hi):
                for q in range(lo, hi):
                    n = min(BT, BPB * (q + 1)) - BPB * q
                    if q == 0:
                        dve.wait_ge(s["ex_sb"], j + 1)
                    dve.wait_ge(s["hg_ps"], j * NQ + (q + 1))
                    if q >= 2:
                        dve.wait_ge(s["msg_used"], j * NQ + (q - 1))
                    dve.tensor_copy(msg[:, q % 2, 0:n, D:D + H], ex[:, par, BPB * q:BPB * q + n, :])
                    dve.tensor_tensor(
                        msg[:, q % 2, 0:n, 0:D].rearrange("p t (h d) -> p t h d", h=H),
                        bank[3 + q % 2][:, 0:n * P].rearrange("p (t h d) -> p t h d", h=H, d=HD),
                        ex[:, par, BPB * q:BPB * q + n, 0:H].rearrange("p t (h o) -> p t h o", o=1).broadcast_to([P, n, H, HD]),
                        ALU.mult)
                    dve.drain()
                    dve.sem_inc(s["msg_sb"], 1)

            def finish(j, par):
                dve.wait_ge(s["msg_used"], (j + 1) * NQ)
                dve.tensor_copy(num[:, :], bank[2][:, 0:MW])
                dve.drain()
                dve.sem_inc(s["num_free"], 1)
                dve.wait_ge(s["emn_sb"], j + 1)
                dve.tensor_scalar(den[:, 0, :], num[:, D + H:D + H + 1].broadcast_to([P, H]), -1.0, float(E), ALU.mult, ALU.add)
                dve.drain()
                dve.tensor_tensor(den[:, 1, :], den[:, 0, :], emn[:, par, :], ALU.mult)
                dve.drain()
                dve.tensor_tensor(den[:, 2, :], den[:, 1, :], num[:, D:D + H], ALU.add)
                dve.drain()
                dve.reciprocal(den[:, 3, :], den[:, 2, :])
                dve.drain()
                dve.tensor_tensor(acc[:, bass.ds(j, 1), :].rearrange("p o (h d) -> p (o h) d", h=H),
                                  num[:, 0:D].rearrange("p (h d) -> p h d", h=H),
                                  den[:, 3, :].rearrange("p (h o) -> p h o", o=1).broadcast_to([P, H, HD]), ALU.mult)
                dve.drain()

            def sum_parts(b):
                for lo, hi, k in ((0, 40, b), (40, BT, b + 1)):
                    dve.tensor_reduce(sc2[:, lo:hi, :], bank[k][:, 0:(hi - lo) * 3 * H]
                                      .rearrange("p (t k h) -> p t h k", k=3, h=H), AX.X, ALU.add)
                dve.drain()

            def step(j, par, sums=True):
                def msgs(lo, hi):
                    if sums:
                        messages(j - 1, 1 - par, lo, hi)

                msgs(0, 6)
                dve.wait_ge(s["at_ps"], j + 1)
                sum_parts(5)
                dve.tensor_tensor(sc2[:, 0:BT, :], sc2[:, 0:BT, :], r6[:, 0:BT, H:2 * H], ALU.add)
                dve.drain()
                dve.sem_inc(s["r6_free"], 1)
                dve.scalar_tensor_tensor(out=sc[:, 0:BT, :], in0=sc2[:, 0:BT, :], scalar=0.2, in1=sc2[:, 0:BT, :],
                                         op0=ALU.mult, op1=ALU.max)
                dve.drain()
                dve.sem_inc(s["at_sb"], 1)
                msgs(6, 7)
                dve.wait_ge(s["atT_ps"], j + 1)
                dve.tensor_copy(dlT[0:RH, :, :].rearrange("p k n -> p (k n)"), bank[7][0:RH, 2 * P:4 * P])
                dve.drain()
                dve.tensor_tensor(keep[0:RH, :, 1:P], dlT[0:RH, :, 1:P], dlT[0:RH, :, 0:P - 1], ALU.is_equal)
                dve.tensor_tensor(endz[0:RH, :, 0:P - 1], dlT[0:RH, :, 1:P], dlT[0:RH, :, 0:P - 1], ALU.not_equal)
                dve.drain()
                dve.tensor_tensor_scan(run[0:RH, :, :].rearrange("p k n -> p (k n)"),
                                       keep[0:RH, :, :].rearrange("p k n -> p (k n)"), bank[7][0:RH, 0:2 * P],
                                       0.0, ALU.mult, ALU.max)
                dve.drain()
                dve.tensor_tensor(run[0:RH, :, :], run[0:RH, :, :], endz[0:RH, :, :], ALU.mult)
                dve.drain()
                dve.sem_inc(s["z_sb"], 1)
                take_records(j + 1)
                msgs(7, 9)
                dve.wait_ge(s["zT_ps"], j + 1)
                dve.tensor_copy(zs[:, 0, :, :].rearrange("p t h -> p (t h)"), bank[7][:, 0:BTP * H])
                dve.drain()
                for k in range(3):
                    dve.tensor_copy(zsp[:, k, :, :], zs[:, k, :, :])
                    dve.drain()
                    if k < 2:
                        dve.tensor_tensor(zs[:, k + 1, :, :], zs[:, k, :, :], zsp[:, k, :, :], ALU.subtract)
                        dve.drain()
                dve.sem_inc(s["zs_sb"], 1)
                one_hot(s6, loc6[:, 0, :], "s6_ready")
                msgs(9, 10)
                dve.wait_ge(s["v_ps"], j + 1)
                sum_parts(5)
                dve.tensor_reduce(mm[:, 0, :], sc2[:, 0:BT, :].rearrange("p t h -> p h t"), AX.X, ALU.max)
                dve.drain()
                dve.tensor_copy(msp[:, 0, :], mm[:, 0, :])
                dve.drain()
                dve.tensor_tensor(mm[:, 1, :], mm[:, 0, :], msp[:, 0, :], ALU.subtract)
                dve.drain()
                dve.tensor_copy(msp[:, 1, :], mm[:, 1, :])
                dve.drain()
                dve.tensor_tensor(mm[:, 2, :], mm[:, 1, :], msp[:, 1, :], ALU.subtract)
                dve.drain()
                dve.tensor_copy(msp[:, 2, :], mm[:, 2, :])
                dve.drain()
                dve.sem_inc(s["m_sb"], 1)
                msgs(10, 12)
                dve.wait_ge(s["d6_ready"], j + 1)
                one_hot(d16, loc6[:, 1, :], "d16_ready")
                dve.wait_ge(s["mg_ps"], j + 1)
                sum_parts(6)
                dve.tensor_tensor(me[:, 0:BT, :], sc[:, 0:BT, :], sc2[:, 0:BT, :], ALU.subtract)
                dve.drain()
                dve.sem_inc(s["arg_sb"], 1)
                msgs(12, NQ)
                if sums:
                    finish(j - 1, 1 - par)

            def fast_attention():
                dve.memset(r6[:, BT:BTP, :], 0.0)
                dve.memset(sc[:, BT:BTP, :], 0.0)
                dve.memset(keep[:, :, 0:1], 0.0)
                dve.memset(endz[:, :, P - 1:P], 1.0)
                dve.memset(msg[:, :, :, D + H:MW], 1.0)
                dve.drain()
                take_records(0)
                one_hot(s6, loc6[:, 0, :], "s6_ready")
                one_hot(d16, loc6[:, 1, :], "d16_ready")
                step(0, 0, sums=False)
                with dve.Fori(0, (NB - 1) // 2) as i:
                    step(i * 2 + 1, 1)
                    step(i * 2 + 2, 0)
                messages(NB - 1, 0, 0, NQ)
                finish(NB - 1, 0)

            with dve.If(plain):
                fast_attention()
            with dve.Else():
                any_attention()
            dve.tensor_tensor(acc[:, :, :], acc[:, :, :], cur[:, :, :], ALU.add)
            dve.drain()
            norm(cur[:, :, :], acc[:, :, :], 2)
            dve.nop().then_inc(s["y_sb"], 1)


INPUTS = ["x", "src", "dst", "edge_attr_64", "edge_weight", "L1_gnn_W_node", "L1_gnn_W_edge", "L1_gnn_a"]


def kernel(**inputs):
    import concourse.bacc as bacc
    from concourse.bass_utils import run_bass_kernel_spmd as run

    nc = bacc.Bacc("TRN2", target_bir_lowering=False, num_devices=1)
    arrays, args = {}, []
    for name in INPUTS:
        a = np.ascontiguousarray(inputs[name])
        arrays[f"in_{name}"] = a
        args.append(nc.dram_tensor(f"in_{name}", a.shape, mybir.dt.from_np(a.dtype), kind="ExternalInput").ap())
    out = nc.dram_tensor("out", (N, D), F32, kind="ExternalOutput").ap()
    build(nc, *args, out)
    r = run(nc, [arrays], core_ids=[0])
    return r.results[0]["out"]
```

```python
from contextlib import ExitStack

import numpy as np

import concourse.bass as bass
from concourse import mybir

F32, BF16, I32 = mybir.dt.float32, mybir.dt.bfloat16, mybir.dt.int32
ALU, ACT = mybir.AluOpType, mybir.ActivationFunctionType
AX = mybir.AxisListType

P = 128
N, D, E, DE = 3125, 128, 103125, 64
H, HD = 4, 32
NB = -(-N // P)
NL = N - (NB - 1) * P
NP = NB * P
NT = -(-E // P)
EL = E - (NT - 1) * P
TR = 7
RW = TR * P
RF, RL = divmod(E, RW)
RR = RF + 1
TP = RR * TR
BT = 2 * NB + 1
BTP = BT + 1
HT = BTP // 2
SLOTS = P * NB * BT
REC = 8
SG = 62
SH = SG // 2
NG = NT // SG
assert NG * SG == NT and RR <= P and BT == 51 and HT == 26
LAYERS = 3
GW = D + 2 * H
TBL = NP + 2 * P
EPS = 1e-5
MW = D + H + 1
BANK = 512
BPB = BANK // P
RING = 5
NQ = BTP // BPB
TI = -(-HT // BPB)
RB = 3
HR, MR = 3, 4
assert NB % RING == 0 and NB % 6 == 1


def banks_of(n):
    return [list(range(s, min(s + BPB, n))) for s in range(0, n, BPB)]


def before(n, ring):
    if n >= ring:
        return NQ + n - ring + 1
    return max(m for m in range(NQ) if m % ring == n) + 1


def build(nc, x, src, dst, edge_attr, edge_weight, w_node, w_edge, att, out):
    ctx = ExitStack()
    slots = nc.dram_tensor("slots", (SLOTS + P, REC), F32, kind="Internal").ap()
    g_x = [nc.dram_tensor(f"g_x{l}", (TBL, D), F32, kind="Internal").ap() for l in range(LAYERS + 1)]
    g_h = nc.dram_tensor("g_h", (TBL, GW), F32, kind="Internal").ap()
    g_max = nc.dram_tensor("g_max", (TBL, H), F32, kind="Internal").ap()
    g_sum = nc.dram_tensor("g_sum", (TBL, MW), F32, kind="Internal").ap()
    turned = nc.dram_tensor("turned", (NB, P, BTP, 2, P), BF16, kind="Internal").ap()
    adj = nc.dram_tensor("adj", (NB, P, NP), F32, kind="Internal").ap()

    with ctx:
        def sb(name, shape, dt, c=ctx):
            return c.enter_context(nc.sbuf_tensor(name, shape, dt))

        def sem(name):
            return ctx.enter_context(nc.semaphore(name))

        ident = sb("ident", [P, P], F32)
        identb = sb("identb", [P, P], BF16)
        ones = sb("ones", [P, P], F32)
        zerob = sb("zerob", [P, BANK], BF16)
        iota_nt = sb("iota_nt", [P, P, BTP], BF16)
        iota_n = sb("iota_n", [P, P], F32)
        cur = sb("cur", [P, NB, D], F32)
        acc = sb("acc", [P, NB, D], F32)
        acat = sb("acat", [P, 3, H], F32)
        wn = sb("wn", [P, D], F32)
        we2 = sb("we2", [P, 2, DE], F32)
        wext = sb("wext", [P, D + 2 * H], F32)
        wedge = sb("wedge", [P, 2 * H], F32)
        st = sb("st", [P, 4, NB], F32)
        upto = sb("upto", [P, NB], F32)
        need_f = sb("need_f", [P, NB], F32)
        need = sb("need", [P, NB], I32)
        bad = sb("bad", [P, 4], F32)
        flag = sb("flag", [P, 1], I32)

        early = ExitStack()
        xs = sb("xs", [P, NB, D], F32, early)
        rec = sb("rec", [P, TP, REC], F32, early)
        slot_i = sb("slot_i", [P, TP], I32, early)
        st_rec = sb("st_rec", [P, 2, SH, REC], F32, early)
        st_slot = sb("st_slot", [P, 2, SH], I32, early)

        with ExitStack() as c:
            src_i, dst_i, w_r = sb("src_i", [P, RW], I32, c), sb("dst_i", [P, RW], I32, c), sb("w_r", [P, RW], F32, c)
            ti = sb("ti", [P, 2, RW], I32, c)
            srcb, dstb = sb("srcb", [P, RW], F32, c), sb("dstb", [P, RW], F32, c)
            src1, dst1 = sb("src1", [P, RW], F32, c), sb("dst1", [P, RW], F32, c)
            same = sb("same", [P, RW], F32, c)
            tmp = sb("tmp", [P, 4, RW], F32, c)
            rank = sb("rank", [P, RW], F32, c)
            lasts = sb("lasts", [P, NB], F32, c)
            base = sb("base", [P, NB], F32, c)
            ahead = sb("ahead", [P, P], F32, c)
            diag = sb("diag", [P, P], F32, c)
            upper = sb("upper", [P, P], F32, c)
            trash = sb("trash", [P, 2], F32, c)
            fix = sb("fix", [P, 2], F32, c)
            zrec = sb("zrec", [P, BT * REC], F32, c)
            ea = sb("ea", [P, 2, SH, 2, DE], F32, c)
            eaT = sb("eaT", [P, 2, BANK], F32, c)
        with ExitStack() as c:
            r3 = sb("r3", [P, 2, HT, REC], F32, c)
            oh_d, oh_s = sb("oh_d", [P, 2, P, HT], BF16, c), sb("oh_s", [P, 2, P, HT], BF16, c)
            oh_w = sb("oh_w", [P, 2, 3, P, HT], BF16, c)
            loc = sb("loc", [P, 2, 2, HT], BF16, c)
            wsp = sb("wsp", [P, 2, 3, HT], BF16, c)
            wres = sb("wres", [P, 2, 2, HT], F32, c)
            arow0 = sb("arow0", [P, NP], F32, c)
            xst = sb("xst", [P, 2, D], F32, c)
            tb = sb("tb", [P, 2, HT, 2, P], BF16, c)
        with ExitStack() as c:
            ablk = sb("ablk", [P, RING, NP], F32, c)
            stage = sb("stage", [P, RING, D], F32, c)
            curT = sb("curT", [P, NP], F32, c)
        early.close()
        with ExitStack() as c:
            hsp = sb("hsp", [P, NB, 3, D + 2 * H], BF16, c)
            r6 = sb("r6", [P, 3, BTP, REC], F32, c)
            loc6 = sb("loc6", [P, 3, BTP], BF16, c)
            d16 = sb("d16", [P, 2, P, BTP], BF16, c)
            d6 = sb("d6", [P, MR, BPB, P], F32, c)
            rT = sb("rT", [P, 3, BTP, 2, P], BF16, c)
            dlr = sb("dlr", [P, BTP, H], F32, c)
            sc = sb("sc", [P, BTP, H], F32, c)
            sc2 = sb("sc2", [P, BTP, H], F32, c)
            dlT = sb("dlT", [P, 2, P], F32, c)
            keep = sb("keep", [P, 2, P], F32, c)
            endz = sb("endz", [P, 2, P], F32, c)
            run = sb("run", [P, 2, P], F32, c)
            zs = sb("zs", [P, 3, BTP, H], F32, c)
            zsp = sb("zsp", [P, 3, BTP, H], BF16, c)
            mm = sb("mm", [P, 3, H], F32, c)
            msp = sb("msp", [P, 3, H], BF16, c)
            emn = sb("emn", [P, NB, H], F32, c)
            dens = sb("dens", [P, NB, H + 1], F32, c)
            den = sb("den", [P, 2, NB, H], F32, c)
            me = sb("me", [P, BTP, H], F32, c)
            ex = sb("ex", [P, 3, BTP, H], F32, c)
            msg = sb("msg", [P, MR, BPB, MW], F32, c)
        with ExitStack() as c:
            sb("any_skip", [P, NB * D + TP * (REC + 1) + 2 * SH * (REC + 1) + RING * (NP + D) + NP], F32, c)
            g_src, g_dst = sb("g_src", [P, NT], I32, c), sb("g_dst", [P, NT], I32, c)
            g_att = sb("g_att", [P, NT, H], F32, c)
            g_ki, g_so = sb("g_ki", [P, 2], I32, c), sb("g_so", [P, 1], I32, c)
            g_key = sb("g_key", [P, 4], F32, c)
            g_trash, g_zero = sb("g_trash", [P, 1], F32, c), sb("g_zero", [P, GW], F32, c)
            g_low, g_same = sb("g_low", [P, P], F32, c), sb("g_same", [P, P], F32, c)
            g_diag = sb("g_diag", [P, H, P], F32, c)
            g_tmp = sb("g_tmp", [P, H, P], F32, c)
            g_a, g_b = sb("g_a", [P, GW], F32, c), sb("g_b", [P, GW], F32, c)
            g_old, g_msg, g_new = sb("g_old", [P, GW], F32, c), sb("g_msg", [P, GW], F32, c), sb("g_new", [P, GW], F32, c)
            g_s = sb("g_s", [P, 4, H], F32, c)
            g_m, g_e = sb("g_m", [P, NB, H], F32, c), sb("g_e", [P, NB, H], F32, c)
        g_num = ablk[:, 0:2, :].rearrange("p r n -> p (r n)")[:, 0:NB * MW].rearrange("p (b n) -> p b n", b=NB)
        hx = ablk[:, 0:2, :].rearrange("p r n -> p (r n)")[:, 0:NB * (D + 2 * H)].rearrange("p (b n) -> p b n", b=NB)

        HG, MG = (0, 1, 3), (7, 4)
        CUTS, DCUTS = (2, 4, 6), (2, 4, 6)
        cols = lambda a: a[:, :, :].rearrange("p b d -> p (b d)")
        arow = (arow0[:, :], cols(cur))
        y1 = cols(acc)
        bank = [ctx.enter_context(nc.psum_tensor(f"bank{i}", [P, BANK], F32)) for i in range(8)]

        names = """consts clears ld_idx ld_w ld_x zeroed ea0 ea1 first_ready base_ready ahead_bc
            ahead_ready base_ps wt_ps wt_sb eaT_ps eaT_sb se_ps se_free rec_se place_ready place_ps place_sb
            place_free rec_ready staged armed half0 half1 landed need_ready block_in upto_sb upto_ps edge_done
            r3a r3b r3_free0 r3_free1 oh_ready oh_used0 oh_used1 row_ps row_free row_sb diag_ps row_add adj_out0 adj_out1
            xst_sb l1_ps l1_free
            a0 a1 a2 a3 a4 a_used0 a_used1 a_used2 a_used3 a_used4 stage_sb stage_free lay_ps lay_sb lay_T cur_sb
            x1_ready x1T_ps x1T_sb h_ps h_sb h_split
            r6_in0 r6_in1 r6_in2 rT_in0 rT_in1 rT_in2 r6_free d6_ready dlr_ready d16_ready turn_ps turn_sb turn_out0 turn_out1 at_ps at_sb atT_ps z_sb zT_ps zs_sb v_ps m_sb emn_sb mg_ps arg_sb ex_sb
            flag_ready bad_sb bad_ps key_bc2 g_init g_ld g_zeroed g_x0 g_keys g_bc g_in0 g_in1 g_in2 g_in3 g_in4 g_armed g_msgs g_arg g_ex g_tot g_news g_out
            g_done g_back g_backed g_hx g_hr g_fin g_emn
            hg_ps msg_sb msg_used num_free y_sb outs rs_var rs_std""".split()
        s = {n: sem(n) for n in names}

        e_rows = lambda t: t[0:RF * RW].rearrange("(r w) -> r w", w=RW)
        e_rest = lambda t: t[RF * RW:E].rearrange("(r w) -> r w", r=1)

        ANY_LAYERS = [("spmm", g_x[l], g_x[l + 1], 2) for l in range(LAYERS)]
        ANY_ATT = [("max", g_h, g_max, 3), ("sum", g_h, g_sum, 3)]
        passes = ANY_LAYERS + ANY_ATT


        block = ctx.enter_context(nc.Block())

        @block.sync
        def _(sp):
            sp.wait_ge(s["clears"], 4)
            for a, t in ((src_i, src), (dst_i, dst)):
                sp.dma_start(a[0:RF, :], e_rows(t)).then_inc(s["ld_idx"], 16)
                sp.dma_start(a[RF:RF + 1, 0:RL], e_rest(t)).then_inc(s["ld_idx"], 16)
            for h in range(H):
                sp.dma_start(acat[h * HD:(h + 1) * HD, :, h], att[h, :].rearrange("(k d) -> d k", k=3),
                             allow_slow_non_contiguous=True).then_inc(s["ld_w"], 16)
            sp.dma_start(wn[:, :], w_node).then_inc(s["ld_w"], 16)
            for k in range(2):
                sp.dma_start(we2[:, k, :], w_edge).then_inc(s["ld_w"], 16)

            def load_attr(g, buf, tiles=SH, last=0):
                view = edge_attr[bass.ds(g * (SG * P), SG * P), :] if not last else None
                if view is not None:
                    view = view.rearrange("(k u p) d -> k p u d", k=2, p=P)
                    for k in range(2):
                        sp.dma_start(ea[:, buf, :, k, :], view[k]).then_inc(s[f"ea{buf}"], 16)
                else:
                    e0 = g * SG * P
                    sp.dma_start(ea[:, buf, :, 0, :], edge_attr[e0:e0 + SH * P, :].rearrange("(u p) d -> p u d", p=P))\
                        .then_inc(s[f"ea{buf}"], 16)
                    e0 += SH * P
                    sp.dma_start(ea[:, buf, 0:SH - 1, 1, :],
                                 edge_attr[e0:e0 + (SH - 1) * P, :].rearrange("(u p) d -> p u d", p=P))\
                        .then_inc(s[f"ea{buf}"], 16)
                    e0 += (SH - 1) * P
                    sp.dma_start(ea[0:EL, buf, SH - 1, 1, :], edge_attr[e0:E, :]).then_inc(s[f"ea{buf}"], 16)

            load_attr(0, 0)
            load_attr(1, 1)
            sp.wait_ge(s["consts"], 9)
            sp.dma_start(w_r[0:RF, :], e_rows(edge_weight)).then_inc(s["ld_x"], 16)
            sp.dma_start(w_r[RF:RF + 1, 0:RL], e_rest(edge_weight)).then_inc(s["ld_x"], 16)
            sp.dma_start(xs[:, 0:NB - 1, :], x[0:(NB - 1) * P, :].rearrange("(b p) d -> p b d", p=P))\
                .then_inc(s["ld_x"], 16)
            sp.dma_start(xs[0:NL, NB - 1, :], x[(NB - 1) * P:N, :]).then_inc(s["ld_x"], 16)
            sp.dma_start(slots[0:SLOTS, :].rearrange("(p j t) f -> p j (t f)", p=P, j=NB),
                         zrec[:, :].rearrange("p (o n) -> p o n", o=1).broadcast_to([P, NB, BT * REC]))\
                .then_inc(s["zeroed"], 16)
            sp.dma_start(slots[SLOTS:SLOTS + P, :], zrec[:, 0:REC]).then_inc(s["zeroed"], 16)
            with sp.Fori(1, NG // 2) as g2:
                for buf in range(2):
                    sp.wait_ge(s["eaT_ps"], (g2 * 2 + (buf - 1)) * -(-SH // BPB))
                    load_attr(g2 * 2 + buf, buf)
            sp.wait_ge(s["eaT_ps"], (NG - 2) * -(-SH // BPB))
            load_attr(NG - 1, 0, last=1)

            all_slots = slots[0:SLOTS, :].rearrange("(p t) f -> p (t f)", p=P)

            def fast_layers():
                sp.wait_ge(s["need_ready"], 1)
                sp.wait_ge(s["edge_done"], 2)
                with sp.Fori(0, NB) as j:
                    sp.wait_ge(s["landed"], sp.value_load(need[0:1, bass.ds(j, 1)], min_val=1, max_val=2 * NG))
                    sp.sem_inc(s["block_in"], 1)
                    for c in range(2):
                        sp.wait_ge(s[f"r3_free{c}"], j + 1)
                        n = HT if c == 0 else HT - 1
                        sp.dma_start(r3[:, c, 0:n, :].rearrange("p t f -> p (t f)"),
                                     all_slots[:, bass.ds(j * (BT * REC) + c * HT * REC, n * REC)])\
                            .then_inc(s["r3a" if c == 0 else "r3b"], 16)
                sp.wait_ge(s["adj_out0"], 16 * (NB - NB // 2))
                sp.wait_ge(s["adj_out1"], 16 * (NB // 2))
                for c in range(2):
                    sp.wait_ge(s[f"turn_out{c}"], 16 * NB)
                sp.wait_ge(s["l1_ps"], (NB + 1) * len(banks_of(NB)))
                with sp.Fori(0, (LAYERS - 1) * NB // RING) as r:
                    for u in range(RING):
                        sp.wait_ge(s[f"a_used{u}"], r + 1)
                        sp.dma_start(ablk[:, u, :], adj[bass.ds((r % (NB // RING)) * RING + u, 1), :, :]
                                     .rearrange("o p n -> (o p) n")).then_inc(s[f"a{u}"], 16)

            def any_layers():
                sp.wait_ge(s["g_init"], 5)
                for a, t in ((g_src, src), (g_dst, dst)):
                    sp.dma_start(a[:, 0:NT - 1], t[0:(NT - 1) * P].rearrange("(t p) -> p t", p=P),
                                 allow_slow_non_contiguous=True).then_inc(s["g_ld"], 16)
                    sp.dma_start(a[0:EL, NT - 1:NT], t[(NT - 1) * P:E].rearrange("(p o) -> p o", o=1))\
                        .then_inc(s["g_ld"], 16)
                for t in g_x + [g_h, g_max, g_sum]:
                    w = t.shape[1]
                    sp.dma_start(t.rearrange("(p r) w -> p r w", p=P), g_zero[:, 0:w].rearrange("p (o w) -> p o w", o=1)
                                 .broadcast_to([P, TBL // P, w])).then_inc(s["g_zeroed"], 16)
                sp.wait_ge(s["g_zeroed"], 16 * (LAYERS + 4))
                sp.wait_ge(s["ld_x"], 64)
                sp.dma_start(g_x[0][0:NP, :].rearrange("(b p) d -> p b d", p=P), xs[:, :, :]).then_inc(s["g_x0"], 16)
                sp.wait_ge(s["g_done"], LAYERS * NT + 1)
                for l in range(LAYERS):
                    sp.dma_start(ablk[:, l, :].rearrange("p (b d) -> p b d", b=NB),
                                 g_x[l + 1][0:NP, :].rearrange("(b p) d -> p b d", p=P)).then_inc(s["g_back"], 16)

            def any_attention():
                sp.wait_ge(s["g_hx"], 1)
                sp.dma_start(g_h[0:NP, :].rearrange("(b p) d -> p b d", p=P), hx).then_inc(s["g_hr"], 16)
                sp.wait_ge(s["g_done"], len(passes) * NT + 1)
                sp.wait_ge(s["g_hr"], 16)
                sp.dma_start(g_num, g_sum[0:NP, :].rearrange("(b p) d -> p b d", p=P)).then_inc(s["g_fin"], 16)
                sp.dma_start(g_m[:, :, :], g_max[0:NP, :].rearrange("(b p) d -> p b d", p=P)).then_inc(s["g_fin"], 16)

            def fast_attention():
                sp.wait_ge(s["h_split"], 1)

                def load(j, n, b, turns=True):
                    sp.wait_ge(s["r6_free"], n + 1)
                    sp.dma_start(r6[:, b, 0:BT, :].rearrange("p t f -> p (t f)"),
                                 all_slots[:, bass.ds(j * (BT * REC), BT * REC)]).then_inc(s[f"r6_in{b}"], 16)
                    if turns:
                        sp.wait_ge(s["hg_ps"], (n + 1) * NQ)
                        for c in range(2):
                            sp.dma_start(rT[:, b, c * HT:(c + 1) * HT, :, :].rearrange("p t k n -> p (t k n)"),
                                         turned[bass.ds(j, 1), :, c * HT:(c + 1) * HT, :, :]
                                         .rearrange("o p t k n -> (o p) (t k n)")).then_inc(s[f"rT_in{b}"], 16)

                with sp.Fori(0, NB // 3) as i:
                    for b in range(3):
                        load(i * 3 + b, i * 3 + b, b)
                load(NB - 1, NB - 1, 0)
                load(NB - 1, NB, 1, turns=False)

            sp.wait_ge(s["flag_ready"], 1)
            plain = sp.value_load(flag[0:1, 0:1], min_val=0, max_val=1)
            with sp.If(plain):
                fast_layers()
            with sp.Else():
                any_layers()
            with sp.If(plain):
                fast_attention()
            with sp.Else():
                any_attention()
            sp.wait_ge(s["y_sb"], 1)
            sp.dma_start(out[0:(NB - 1) * P, :].rearrange("(b p) d -> p b d", p=P), cur[:, 0:NB - 1, :])\
                .then_inc(s["outs"], 16)
            sp.dma_start(out[(NB - 1) * P:N, :], cur[0:NL, NB - 1, :]).then_inc(s["outs"], 16)
            sp.wait_ge(s["outs"], 32)

        @block.gpsimd
        def _(pool):
            pool.memset(src_i[:, :], -1).then_inc(s["clears"], 1)
            pool.memset(dst_i[:, :], NP - 1).then_inc(s["clears"], 1)
            pool.memset(acat[:, :, :], 0.0).then_inc(s["clears"], 1)
            pool.memset(zrec[:, :], 0.0).then_inc(s["clears"], 1)
            c = s["consts"]
            pool.memset(w_r[:, :], 0.0).then_inc(c, 1)
            pool.memset(ident[:, :], 0.0).then_inc(c, 1)
            pool.memset(identb[:, :], 0.0).then_inc(c, 1)
            pool.memset(ones[:, :], 1.0).then_inc(c, 1)
            pool.memset(upper[:, :], 1.0).then_inc(c, 1)
            pool.memset(xs[:, NB - 1, :], 0.0).then_inc(c, 1)
            pool.memset(trash[:, 1:2], 1.0).then_inc(c, 1)
            pool.memset(zerob[:, :], 0.0).then_inc(c, 1)
            pool.memset(rec[:, :, 3:4], 0.0).then_inc(c, 1)
            pool.wait_ge(c, 9)
            pool.affine_select(out=ident[:, :], in_=ident[:, :], compare_op=ALU.not_equal, fill=1.0, base=0,
                               pattern=[[-1, P]], channel_multiplier=1).then_inc(c, 1)
            pool.affine_select(out=identb[:, :], in_=identb[:, :], compare_op=ALU.not_equal, fill=1.0, base=0,
                               pattern=[[-1, P]], channel_multiplier=1).then_inc(c, 1)
            pool.affine_select(out=upper[:, :], in_=upper[:, :], compare_op=ALU.is_ge, fill=0.0, base=-1,
                               pattern=[[1, P]], channel_multiplier=-1).then_inc(c, 1)
            pool.affine_select(out=trash[:, 1:2], in_=trash[:, 1:2], compare_op=ALU.is_ge, fill=0.0, base=EL - 1,
                               pattern=[[0, 1]], channel_multiplier=-1).then_inc(c, 1)
            pool.iota(trash[:, 0:1], pattern=[[0, 1]], base=SLOTS, channel_multiplier=1,
                      allow_small_or_imprecise_dtypes=True).then_inc(c, 1)
            pool.iota(iota_n[:, :], pattern=[[1, P]], base=1, channel_multiplier=0,
                      allow_small_or_imprecise_dtypes=True).then_inc(c, 1)
            pool.iota(iota_nt[:, :, :], pattern=[[1, P], [0, BTP]], base=1, channel_multiplier=0,
                      allow_small_or_imprecise_dtypes=True).then_inc(c, 1)

            pool.wait_ge(s["zeroed"], 32)
            pool.wait_ge(s["rec_ready"], 1)

            def scatter(g, k, before_landed=None):
                pool.tensor_copy(st_rec[:, k, :, :], rec[:, bass.ds(g * SG + k * SH, SH), :]).then_inc(s["staged"], 1)
                pool.tensor_copy(st_slot[:, k, :], slot_i[:, bass.ds(g * SG + k * SH, SH)]).then_inc(s["staged"], 1)
                pool.wait_ge(s["staged"], g * 4 + (2 * k + 2))
                pool.sem_inc(s["armed"], 1)
                for u in range(SH):
                    pool.indirect_dma_start(
                        out=slots, out_offset=bass.IndirectOffsetOnAxis(ap=st_slot[:, k, u:u + 1], axis=0),
                        in_=st_rec[:, k, u, :], in_offset=None).then_inc(s[f"half{k}"], 16)
                    if u == 7 and before_landed is not None:
                        pool.wait_ge(s[f"half{1 - k}"], before_landed)
                        pool.sem_inc(s["landed"], 1)

            def fast_scatter():
                pool.wait_ge(s["rec_se"], 2)
                scatter(0, 0)
                scatter(0, 1, 16 * SH)
                with pool.Fori(1, NG) as g:
                    pool.wait_ge(s["rec_se"], g + 2)
                    scatter(g, 0, g * (16 * SH))
                    scatter(g, 1, (g + 1) * (16 * SH))
                pool.wait_ge(s["half1"], NG * 16 * SH)
                pool.sem_inc(s["landed"], 1)

            def any_tiles(k):
                kind, table, result, gathers = passes[k]
                n0 = k * NT
                with pool.Fori(0, NT) as t:
                    pool.wait_ge(s["g_keys"], t + (n0 + 1))
                    pool.sem_inc(s["g_armed"], 1)

                    def gather(rows, t_, col, w):
                        pool.indirect_dma_start(out=rows[:, 0:w], out_offset=None, in_=t_,
                                                in_offset=bass.IndirectOffsetOnAxis(ap=g_ki[:, col:col + 1], axis=0))\
                            .then_inc(s[f"g_in{k}"], 16)
                    gather(g_a, table, 0, table.shape[1])
                    if kind == "max":
                        gather(g_b, g_h, 1, GW)
                    elif kind == "sum":
                        gather(g_b, g_max, 1, H)
                    gather(g_old, result, 1, result.shape[1])
                    pool.wait_ge(s["g_news"], t + (n0 + 1))
                    pool.sem_inc(s["g_armed"], 1)
                    pool.indirect_dma_start(out=result, out_offset=bass.IndirectOffsetOnAxis(ap=g_so[:, 0:1], axis=0),
                                            in_=g_new[:, 0:result.shape[1]], in_offset=None).then_inc(s["g_out"], 16)
                    pool.wait_ge(s["g_out"], t * 16 + (n0 + 1) * 16)
                    pool.sem_inc(s["g_done"], 1)

            def any_layers():
                pool.wait_ge(s["edge_done"], 2)
                pool.memset(g_src[:, :], NP).then_inc(s["g_init"], 1)
                pool.memset(g_dst[:, :], NP).then_inc(s["g_init"], 1)
                pool.memset(g_zero[:, :], 0.0).then_inc(s["g_init"], 1)
                pool.memset(g_low[:, :], 1.0).then_inc(s["g_init"], 1)
                pool.iota(g_trash[:, :], pattern=[[0, 1]], base=NP + P, channel_multiplier=1,
                          allow_small_or_imprecise_dtypes=True).then_inc(s["g_init"], 1)
                pool.wait_ge(s["g_init"], 5)
                pool.affine_select(out=g_low[:, :], in_=g_low[:, :], compare_op=ALU.is_ge, fill=0.0, base=-1,
                                   pattern=[[-1, P]], channel_multiplier=1).then_inc(s["g_init"], 1)
                pool.sem_inc(s["g_done"], 1)
                pool.wait_ge(s["g_x0"], 16)
                for k in range(LAYERS):
                    any_tiles(k)

            def any_attention():
                pool.wait_ge(s["g_hr"], 16)
                for k in range(LAYERS, len(passes)):
                    any_tiles(k)

            pool.wait_ge(s["flag_ready"], 1)
            plain = pool.value_load(flag[0:1, 0:1], min_val=0, max_val=1)
            with pool.If(plain):
                fast_scatter()
            with pool.Else():
                any_layers()
                any_attention()

        @block.tensor
        def _(pe):
            for u in range(RING):
                pe.sem_inc(s[f"a_used{u}"], 1)
            pe.wait_ge(s["consts"], 16)
            pe.wait_ge(s["ld_w"], 16 * (H + 3))
            pe.transpose(bank[0][:, 0:D], wn[:, :], ident[:, :])
            pe.matmul(bank[1][:, 0:2 * H], wn[:, :], acat[:, 0:2, :].rearrange("p k h -> p (k h)"),
                      start=True, stop=True)
            pe.matmul(bank[2][:, 0:H], we2[:, :, :].rearrange("p k d -> p (k d)"), acat[:, 2, :],
                      start=True, stop=True).then_inc(s["wt_ps"], 1)
            pe.wait_ge(s["first_ready"], 1)
            pe.matmul(bank[3][:, 0:P], ones[:, :], diag[:, :], start=True, stop=True).then_inc(s["ahead_bc"], 1)
            pe.wait_ge(s["ahead_ready"], 1)
            pe.matmul(bank[4][:, 0:NB], ahead[:, :], lasts[:, :], start=True, stop=True).then_inc(s["base_ps"], 1)

            pe.wait_ge(s["wt_sb"], 1)
            chunks = [list(range(u, min(u + BPB, SH))) for u in range(0, SH, BPB)]
            NC = len(chunks)

            def group(g, buf, load_count):
                pe.wait_ge(s[f"ea{buf}"], load_count)
                for ci in range(NC + 1):
                    if ci < NC:
                        r = ci % 2
                        if ci:
                            pe.wait_ge(s["eaT_sb"], g * NC + (ci - 1))
                        for k, u in enumerate(chunks[ci]):
                            m = pe.transpose(bank[5 + r][:, k * P:(k + 1) * P],
                                             ea[:, buf, u, :, :].rearrange("p k d -> p (k d)"), ident[:, :])
                        m.then_inc(s["eaT_ps"], 1)
                    if ci >= 1:
                        if ci == 1:
                            pe.wait_ge(s["rec_se"], g + 1)
                        pe.wait_ge(s["eaT_sb"], g * NC + ci)
                        for k, u in enumerate(chunks[ci - 1]):
                            m = pe.matmul(bank[7][:, u * 2 * H:(u + 1) * 2 * H],
                                          eaT[:, (ci - 1) % 2, k * P:(k + 1) * P], wedge[:, :], start=True, stop=True)
                m.then_inc(s["se_ps"], 1)

            for buf in range(2):
                group(buf, buf, 32)

            pe.wait_ge(s["bad_sb"], 1)
            pe.matmul(bank[3][:, 0:P], ones[:, :], diag[:, :], start=True, stop=True).then_inc(s["key_bc2"], 1)
            pe.wait_ge(s["bad_sb"], 2)
            pe.matmul(bank[4][:, 0:1], ones[:, :], bad[:, 3:4], start=True, stop=True).then_inc(s["bad_ps"], 1)
            pe.wait_ge(s["place_ready"], 1)
            for n in range(4 * TR):
                f, b = n // TR, n % TR
                if n >= 2:
                    pe.wait_ge(s["place_sb"], n - 1)
                a = (rank, w_r, src1, dst1)[f]
                pe.transpose(bank[n % 2][:, 0:P], a[:, b * P:(b + 1) * P], ident[:, :]).then_inc(s["place_ps"], 1)
            pe.wait_ge(s["upto_sb"], 1)
            pe.matmul(bank[2][:, 0:NB], ones[:, :], upto[:, :], start=True, stop=True).then_inc(s["upto_ps"], 1)
            with pe.Fori(1, NG // 2) as g2:
                for buf in range(2):
                    group(g2 * 2 + buf, buf, (g2 + 1) * 32)
            group(NG - 1, 0, NG // 2 * 32 + 48)

            def fast_layers():
                groups = banks_of(NB)
                pe.wait_ge(s["rec_se"], NG + 1)
                NG7 = len(groups)

                def turn(j, c):
                    for k in range(TI):
                        n = c * TI + k
                        pe.wait_ge(s["turn_sb"], j * (2 * TI) + (n + 1))
                        for u in range(BPB * k, min(HT, BPB * (k + 1))):
                            for v, rows in enumerate((oh_d, oh_s)):
                                w = (u - BPB * k) * 2 + v
                                m = pe.transpose(bank[5 + n % 2][:, :].bitcast(BF16)[:, w * P:(w + 1) * P],
                                                 rows[:, c, :, u], identb[:, :])
                        m.then_inc(s["turn_ps"], 1)

                def first_product(j, par):
                    pe.wait_ge(s["row_add"], j + 2)
                    pe.wait_ge(s["xst_sb"], j + 1)
                    for g, bs in enumerate(groups):
                        pe.wait_ge(s["l1_free"], j * NG7 + (g + NG7 - 1 if g >= 2 else (NG7 - g)))
                        pe.matmul(bank[3 + g % 2][:, 0:len(bs) * P], xst[:, par, :],
                                  arow[par][:, g * BANK:g * BANK + len(bs) * P], start=True, stop=True)\
                            .then_inc(s["l1_ps"], 1)

                def row(j, par, first=False):
                    for i in range(NB):
                        g = i // BPB
                        if i % BPB == 0:
                            last = max(n for n in range(NG7) if n % RB == g) if g < RB else NG7 + g - RB
                            pe.wait_ge(s["row_free"], j * NG7 + (last + 1))
                        n = 0
                        for t in (2 * i, 2 * i + 1):
                            c, u = divmod(t, HT)
                            if u == 0:
                                pe.wait_ge(s["oh_ready"], j * 2 + (c + 1))
                            for k in range(3):
                                m = pe.matmul(bank[g % RB][:, i % BPB * P:(i % BPB + 1) * P], oh_d[:, c, :, u],
                                              oh_w[:, c, k, :, u], start=(n == 0), stop=(n == 5))
                                n += 1
                        if i == groups[g][-1]:
                            m.then_inc(s["row_ps"], 1)
                        elif 2 * i + 1 == HT - 1:
                            turn(j, 0)
                            if not first:
                                first_product(j - 1, 1 - par)
                    pe.wait_ge(s["row_add"], j + 1)
                    for k in range(3):
                        m = pe.matmul(bank[7][:, 0:P], oh_d[:, 1, :, BT - 1 - HT], oh_w[:, 1, k, :, BT - 1 - HT],
                                      start=(k == 0), stop=(k == 2))
                    m.then_inc(s["diag_ps"], 1)
                    turn(j, 1)

                pe.sem_inc(s["l1_ps"], NG7)
                row(0, 0, first=True)
                with pe.Fori(0, NB // 2) as i:
                    row(i * 2 + 1, 1)
                    row(i * 2 + 2, 0)
                first_product(NB - 1, 0)

                pe.wait_ge(s["l1_free"], (NB + 1) * NG7)
                pe.wait_ge(s["row_sb"], NB * NG7)
                pe.wait_ge(s["turn_sb"], NB * (2 * TI) + 2)
                for g, bs in enumerate(groups):
                    for k, b in enumerate(bs):
                        m = pe.transpose(bank[g][:, k * P:(k + 1) * P], acc[:, b, :], ident[:, :])
                    m.then_inc(s["lay_T"], 1)
                with pe.Fori(0, LAYERS - 1) as l:
                    pe.wait_ge(s["cur_sb"], (l + 1) * NG7)
                    for g, bs in enumerate(groups):
                        pe.matmul(bank[g][:, 0:len(bs) * P], zerob[:, 0:P], zerob[:, 0:len(bs) * P], start=True, stop=False)
                    with pe.Fori(0, NB // RING) as r:
                        for u in range(RING):
                            pe.wait_ge(s[f"a{u}"], (l * (NB // RING) + r + 1) * 16)
                            pe.wait_ge(s["stage_sb"], l * NB + r * RING + (u + 1))
                            for g, bs in enumerate(groups):
                                w = len(bs) * P
                                m = pe.matmul(bank[g][:, 0:w], stage[:, u, :], ablk[:, u, g * BANK:g * BANK + w],
                                              start=False, stop=False)
                            m.then_inc(s[f"a_used{u}"], 1)
                    for g, bs in enumerate(groups):
                        m = pe.matmul(bank[g][:, 0:len(bs) * P], zerob[:, 0:P], zerob[:, 0:len(bs) * P], start=False, stop=True)
                        m.then_inc(s["lay_ps"], 1)
                    for g, bs in enumerate(groups):
                        pe.wait_ge(s["lay_sb"], l * len(groups) + (g + 1))
                        for k, b in enumerate(bs):
                            m = pe.transpose(bank[g][:, k * P:(k + 1) * P], curT[:, b * P:(b + 1) * P], ident[:, :])
                        m.then_inc(s["lay_T"], 1)

            def any_tiles(k):
                kind = passes[k][0]
                w = {"spmm": D, "max": H * P, "sum": MW}[kind]
                n0 = k * NT
                with pe.Fori(0, NT) as t:
                    pe.wait_ge(s["g_keys"], t + (n0 + 1))
                    pe.matmul(bank[0][:, 0:P], ones[:, :], g_diag[:, 0, :], start=True, stop=True).then_inc(s["g_bc"], 1)
                    pe.wait_ge(s["g_msgs"], t + (n0 + 1))
                    if kind == "max":
                        m = pe.matmul(bank[1][:, :], ones[:, :], g_diag[:, :, :].rearrange("p h n -> p (h n)"), start=True, stop=True)
                    else:
                        m = pe.matmul(bank[1][:, 0:w], g_same[:, :], g_msg[:, 0:w], start=True, stop=True)
                    m.then_inc(s["g_tot"], 1)

            def any_layers():
                for k in range(LAYERS):
                    any_tiles(k)

            def any_attention():
                for k in range(LAYERS, len(passes)):
                    any_tiles(k)

            pe.wait_ge(s["flag_ready"], 1)
            plain = pe.value_load(flag[0:1, 0:1], min_val=0, max_val=1)
            with pe.If(plain):
                fast_layers()
            with pe.Else():
                any_layers()
            groups = banks_of(NB)
            pe.wait_ge(s["x1_ready"], 1)
            for g, bs in enumerate(groups):
                for k, b in enumerate(bs):
                    m = pe.transpose(bank[g][:, k * P:(k + 1) * P], cur[:, b, :], ident[:, :])
                m.then_inc(s["x1T_ps"], 1)
            W = D + 2 * H
            for b in range(NB):
                g, k = divmod(b, 3)
                if k == 0:
                    pe.wait_ge(s["x1T_sb"], len(groups))
                    if g >= 8:
                        pe.wait_ge(s["h_sb"], g - 7)
                m = pe.matmul(bank[g % 8][:, k * W:(k + 1) * W], curT[:, b * P:(b + 1) * P], wext[:, :],
                              start=True, stop=True)
                if k == 2 or b == NB - 1:
                    m.then_inc(s["h_ps"], 1)
            pe.wait_ge(s["h_split"], 1)

            def block_rows(j):
                return hsp[:, bass.ds(j, 1), :, :].rearrange("p o k n -> p (o k) n")

            def src_rows(t, j):
                return hsp[:, t // 2, :, :] if t < BT - 1 else block_rows(j)

            def gather_h(j, b, q):
                pe.wait_ge(s["msg_sb"], (j * NQ + before(q, HR)) * 2)
                for v in range(BPB):
                    t = BPB * q + v
                    if t < BT:
                        for k in range(3):
                            m = pe.matmul(bank[HG[q % HR]][:, v * P:(v + 1) * P], rT[:, b, t, 1, :],
                                          src_rows(t, j)[:, k, 0:D], start=(k == 0), stop=(k == 2))
                m.then_inc(s["hg_ps"], 1)

            def sum_dst(j, b, q):
                if q == 0:
                    pe.wait_ge(s["num_free"], j + 1)
                pe.wait_ge(s["d6_ready"], j * NQ + (2 * NQ + q + 1))
                pe.wait_ge(s["msg_sb"], (j * NQ + (NQ + q + 1)) * 2)
                for v in range(BPB):
                    t = BPB * q + v
                    if t < BT:
                        m = pe.matmul(bank[2][:, 0:MW], d6[:, q % MR, v, :], msg[:, q % MR, v, :],
                                      start=(t == 0), stop=(t == BT - 1))
                m.then_inc(s["msg_used"], 1)

            def sums_of(j, b, lo, hi):
                for q in range(lo, hi):
                    if q < NQ:
                        gather_h(j, b, q)
                    if q >= HR - 1:
                        sum_dst(j, b, q - (HR - 1))

            def step(j, b, par, turn, sums=True):
                def sums_to(lo, hi):
                    if sums:
                        sums_of(j - 1, (b - 1) % 3, lo, hi)
                pe.wait_ge(s[f"rT_in{b}"], turn * 32 + 32)
                pe.wait_ge(s["dlr_ready"], j + 1)
                for k in range(2):
                    pe.transpose(bank[6][0:HT * H, (2 + k) * P:(3 + k) * P],
                                 dlr[:, k * HT:(k + 1) * HT, :].rearrange("p t h -> p (t h)"), ident[:, :])
                for t in range(BT):
                    o = bank[5 + t // 40][:, t % 40 * 3 * H:(t % 40 + 1) * 3 * H]
                    pe.matmul(o, rT[:, b, t, 1, :], src_rows(t, j)[:, :, D:D + H], start=True, stop=False)
                    m = pe.matmul(o, rT[:, b, t, 0, :], block_rows(j)[:, :, D + H:D + 2 * H], start=False, stop=True)
                m.then_inc(s["at_ps"], 1)
                sums_to(0, CUTS[0])
                pe.wait_ge(s["at_sb"], j + 1)
                for k in range(2):
                    m = pe.transpose(bank[7][0:HT * H, k * P:(k + 1) * P],
                                     sc[:, k * HT:(k + 1) * HT, :].rearrange("p t h -> p (t h)"), ident[:, :])
                m.then_inc(s["atT_ps"], 1)
                sums_to(CUTS[0], CUTS[1])
                pe.wait_ge(s["z_sb"], j + 1)
                for k in range(2):
                    m = pe.transpose(bank[7][:, k * HT * H:(k + 1) * HT * H], run[0:HT * H, k, :], ident[0:HT * H, 0:HT * H])
                m.then_inc(s["zT_ps"], 1)
                sums_to(CUTS[1], CUTS[2])
                pe.wait_ge(s["zs_sb"], j + 1)
                pe.wait_ge(s["d16_ready"], j + 1)
                for t in range(BT):
                    m = pe.matmul(bank[5 + t // 40][:, t % 40 * 3 * H:(t % 40 + 1) * 3 * H], d16[:, par, :, t],
                                  zsp[:, :, t, :], start=True, stop=True)
                m.then_inc(s["v_ps"], 1)
                sums_to(CUTS[2], NQ + HR - 1)
                pe.wait_ge(s["m_sb"], j + 1)
                for t in range(BT):
                    m = pe.matmul(bank[MG[t // 40]][:, t % 40 * 3 * H:(t % 40 + 1) * 3 * H], rT[:, b, t, 0, :],
                                  msp[:, :, :].rearrange("p k h -> p (k h)"), start=True, stop=True)
                m.then_inc(s["mg_ps"], 1)

            def fast_attention():
                pe.sem_inc(s["hg_ps"], 3 * NQ)
                pe.sem_inc(s["msg_used"], NQ)
                step(0, 0, 0, 0, sums=False)
                with pe.Fori(0, NB // 6) as i:
                    for u in range(1, 7):
                        step(i * 6 + u, u % 3, u % 2, i * 2 + u // 3)
                sums_of(NB - 1, 0, 0, NQ + HR - 1)

            with pe.If(plain):
                fast_attention()
            with pe.Else():
                any_attention()

        @block.scalar
        def _(act):
            act.sem_inc(s["rec_se"], 1)
            act.sem_inc(s["row_free"], len(banks_of(NB)))
            act.sem_inc(s["turn_sb"], 2)
            act.wait_ge(s["wt_ps"], 1)
            act.copy(wext[:, 0:D], bank[0][:, 0:D])
            act.copy(wext[:, D:D + 2 * H], bank[1][:, 0:2 * H])
            act.mul(wedge[:, :], ones[:, 0:2 * H], 0.0)
            act.drain()
            act.copy(wedge[0:DE, 0:H], bank[2][0:DE, 0:H])
            act.copy(wedge[DE:2 * DE, H:2 * H], bank[2][DE:2 * DE, 0:H])
            act.drain()
            act.nop().then_inc(s["wt_sb"], 1)
            NC = -(-SH // BPB)

            def group(g):
                for ci in range(NC):
                    act.wait_ge(s["eaT_ps"], g * NC + (ci + 1))
                    w = (min(SH, BPB * (ci + 1)) - BPB * ci) * P
                    act.copy(eaT[:, ci % 2, 0:w], bank[5 + ci % 2][:, 0:w]).then_inc(s["eaT_sb"], 1)
                act.wait_ge(s["se_ps"], g + 1)
                act.copy(rec[:, bass.ds(g * SG, SG), H:2 * H].rearrange("p (k u) f -> p u k f", k=2),
                         bank[7][:, 0:SH * 2 * H].rearrange("p (u k f) -> p u k f", k=2, f=H)).then_inc(s["rec_se"], 1)

            with act.Fori(0, NG // 2) as g2:
                for b in range(2):
                    group(g2 * 2 + b)
            group(NG - 1)
            act.nop().then_inc(s["edge_done"], 1)

            def fast_layers():
                groups = banks_of(NB)
                NG7 = len(groups)

                def turn(j, c, first):
                    if not first:
                        act.wait_ge(s[f"turn_out{c}"], j * 16)
                    for k in range(TI):
                        act.wait_ge(s["turn_ps"], j * (2 * TI) + (c * TI + k + 1))
                        n = min(HT, BPB * (k + 1)) - BPB * k
                        act.copy(tb[:, c, BPB * k:BPB * k + n, :, :].rearrange("p t k n -> p (t k n)"),
                                 bank[5 + (c * TI + k) % 2][:, :].bitcast(BF16)[:, 0:n * 2 * P]).then_inc(s["turn_sb"], 1)
                    act.drain()
                    act.sem_inc(s[f"oh_used{c}"], 1)
                    act.wait_ge(s["turn_sb"], j * (2 * TI) + ((c + 1) * TI + 2))
                    act.dma_start(turned[bass.ds(j, 1), :, c * HT:(c + 1) * HT, :, :].rearrange("o p t k n -> (o p) (t k n)"),
                                  tb[:, c, :, :, :].rearrange("p t k n -> p (t k n)")).then_inc(s[f"turn_out{c}"], 16)

                def row(j, par, turn_no, first=False):
                    if not first:
                        act.wait_ge(s["l1_ps"], j * NG7)
                    act.copy(xst[:, par, :], xs[:, bass.ds(j, 1), :].rearrange("p o n -> p (o n)")).then_inc(s["xst_sb"], 1)
                    for g, bs in enumerate(groups):
                        if g == HT // 2 // BPB:
                            turn(j, 0, first)
                        act.wait_ge(s["row_ps"], j * NG7 + (g + 1))
                        act.copy(arow[par][:, g * BANK:g * BANK + len(bs) * P], bank[g % RB][:, 0:len(bs) * P])
                        act.drain()
                        act.nop().then_inc(s["row_free"], 1)
                        act.nop().then_inc(s["row_sb"], 1)
                    turn(j, 1, first)
                    act.wait_ge(s["row_add"], j + 2)
                    act.dma_start(adj[bass.ds(j, 1), :, :].rearrange("o p n -> (o p) n"), arow[par])\
                        .then_inc(s[f"adj_out{par}"], 16)
                    if not first:
                        act.wait_ge(s[f"adj_out{1 - par}"], turn_no * 16 + 16)

                row(0, 0, 0, first=True)
                with act.Fori(0, NB // 2) as i:
                    row(i * 2 + 1, 1, i)
                    row(i * 2 + 2, 0, i)

                with act.Fori(0, LAYERS - 1) as l:
                    act.wait_ge(s["cur_sb"], (l + 1) * NG7)
                    with act.Fori(0, NB // RING) as r:
                        for u in range(RING):
                            act.wait_ge(s[f"a_used{u}"], l * (NB // RING) + r + 1)
                            act.copy(stage[:, u, :], cur[:, bass.ds(r * RING + u, 1), :].rearrange("p o n -> p (o n)"))\
                                .then_inc(s["stage_sb"], 1)
                    for g, bs in enumerate(groups):
                        act.wait_ge(s["lay_ps"], l * len(groups) + (g + 1))
                        act.copy(curT[:, g * BANK:g * BANK + len(bs) * P], bank[g][:, 0:len(bs) * P]).then_inc(s["lay_sb"], 1)

            def any_attention():
                with act.Fori(0, NT) as t:
                    act.wait_ge(s["g_arg"], t + 1)
                    act.activation(g_s[:, 2, :], g_s[:, 1, :], ACT.Exp).then_inc(s["g_ex"], 1)
                act.wait_ge(s["g_fin"], 32)
                act.activation(g_e[:, :, :], g_m[:, :, :], ACT.Exp, scale=-1.0).then_inc(s["g_emn"], 1)

            act.wait_ge(s["flag_ready"], 1)
            plain = act.value_load(flag[0:1, 0:1], min_val=0, max_val=1)
            with act.If(plain):
                fast_layers()
            groups = banks_of(NB)
            act.wait_ge(s["rs_var"], 1)
            act.activation(st[:, 2, :], st[:, 1, :], ACT.Sqrt).then_inc(s["rs_std"], 1)
            for g, bs in enumerate(groups):
                act.wait_ge(s["x1T_ps"], g + 1)
                act.copy(curT[:, g * BANK:g * BANK + len(bs) * P], bank[g][:, 0:len(bs) * P]).then_inc(s["x1T_sb"], 1)
            W = D + 2 * H
            for g in range(-(-NB // 3)):
                n = min(NB, 3 * g + 3) - 3 * g
                act.wait_ge(s["h_ps"], g + 1)
                act.copy(hx[:, 3 * g:3 * g + n, :].rearrange("p b n -> p (b n)"), bank[g % 8][:, 0:n * W]).then_inc(s["h_sb"], 1)
            act.wait_ge(s["h_split"], 1)

            def rows_of(j, par):
                act.wait_ge(s["d16_ready"], j + 1)
                for q in range(NQ):
                    act.wait_ge(s["msg_used"], j * NQ + before(q, MR))
                    act.copy(d6[:, q % MR, :, :], d16[:, par, :, BPB * q:BPB * (q + 1)].rearrange("p n t -> p t n"))\
                        .then_inc(s["d6_ready"], 1)

            def sums_of(j):
                act.wait_ge(s["msg_used"], (j + 2) * NQ)
                act.copy(acc[:, bass.ds(j, 1), :].rearrange("p o n -> p (o n)"), bank[2][:, 0:D])
                act.copy(dens[:, bass.ds(j, 1), :].rearrange("p o h -> p (o h)"), bank[2][:, D:MW])
                act.drain()
                act.sem_inc(s["num_free"], 1)

            def step(j, b, par, sums=True):
                if sums:
                    rows_of(j - 1, 1 - par)
                act.wait_ge(s["m_sb"], j + 1)
                act.activation(emn[:, bass.ds(j, 1), :].rearrange("p o h -> p (o h)"), mm[:, 0, :], ACT.Exp, scale=-1.0)\
                    .then_inc(s["emn_sb"], 1)
                if sums:
                    sums_of(j - 1)
                act.wait_ge(s["arg_sb"], j + 1)
                act.activation(ex[:, b, 0:BT, 0:H], me[:, 0:BT, :], ACT.Exp).then_inc(s["ex_sb"], 1)

            def fast_attention():
                act.sem_inc(s["num_free"], 1)
                act.sem_inc(s["d6_ready"], 2 * NQ)
                step(0, 0, 0, sums=False)
                with act.Fori(0, NB // 6) as i:
                    for u in range(1, 7):
                        step(i * 6 + u, u % 3, u % 2)
                rows_of(NB - 1, 0)
                sums_of(NB - 1)

            with act.If(plain):
                fast_attention()
            with act.Else():
                any_attention()
            act.wait_ge(s["rs_var"], 2)
            act.activation(st[:, 2, :], st[:, 1, :], ACT.Sqrt).then_inc(s["rs_std"], 1)

        @block.vector
        def _(dve):
            def norm(dest, a, part):
                mean, var, std = st[:, 0, :], st[:, 1, :], st[:, 2, :]
                wide = lambda v: v.rearrange("p (b o) -> p b o", o=1).broadcast_to([P, NB, D])
                dve.tensor_reduce(mean, a, AX.X, ALU.add)
                dve.drain()
                dve.tensor_scalar(mean, mean, 1.0 / D, None, ALU.mult)
                dve.drain()
                dve.tensor_tensor(a, a, wide(mean), ALU.subtract)
                dve.drain()
                dve.tensor_tensor(dest, a, a, ALU.mult)
                dve.drain()
                dve.tensor_reduce(var, dest, AX.X, ALU.add)
                dve.drain()
                dve.tensor_scalar(var, var, 1.0 / D, EPS, ALU.mult, ALU.add)
                dve.drain()
                dve.nop().then_inc(s["rs_var"], 1)
                dve.wait_ge(s["rs_std"], part)
                dve.reciprocal(st[:, 3, :], std)
                dve.drain()
                dve.tensor_tensor(dest, a, wide(st[:, 3, :]), ALU.mult)
                dve.drain()

            for n in ("r3_free0", "r3_free1", "row_add"):
                dve.sem_inc(s[n], 1)
            dve.wait_ge(s["ld_idx"], 64)
            dve.wait_ge(s["consts"], 16)
            dve.tensor_single_scalar(ti[:, 0, :], dst_i[:, :], 7, op=ALU.arith_shift_right)
            dve.tensor_single_scalar(ti[:, 1, :], src_i[:, :], 7, op=ALU.arith_shift_right)
            dve.drain()
            dve.tensor_copy(dstb[:, :], ti[:, 0, :])
            dve.tensor_copy(srcb[:, :], ti[:, 1, :])
            dve.drain()
            dve.tensor_scalar(diag[:, :], ident[:, :], dstb[:, 0:1], None, ALU.mult)
            dve.drain()
            dve.nop().then_inc(s["first_ready"], 1)
            dve.tensor_single_scalar(ti[:, 0, :], dst_i[:, :], P - 1, op=ALU.bitwise_and)
            dve.tensor_single_scalar(ti[:, 1, :], src_i[:, :], P - 1, op=ALU.bitwise_and)
            dve.tensor_tensor(same[:, 1:RW], dstb[:, 1:RW], dstb[:, 0:RW - 1], ALU.is_equal)
            dve.memset(same[:, 0:1], 1.0)
            dve.tensor_scalar(tmp[:, 0, :], srcb[:, :], 1.0, None, ALU.add)
            dve.drain()
            dve.scalar_tensor_tensor(out=tmp[:, 1, :], in0=dstb[:, :], scalar=dstb[:, RW - 1:RW], in1=tmp[:, 0, :],
                                     op0=ALU.is_equal, op1=ALU.mult)
            dve.tensor_scalar(dst1[:, :], ti[:, 0, :], 1.0, None, ALU.add)
            dve.tensor_scalar(src1[:, :], ti[:, 1, :], 1.0, None, ALU.add)
            dve.drain()
            for i in range(NB):
                dve.tensor_scalar(tmp[:, 2 + i % 2, :], tmp[:, 1, :], float(i + 1), 0.0, ALU.is_equal, ALU.add,
                                  accum_out=lasts[:, i:i + 1])
                dve.drain()
            dve.wait_ge(s["ahead_bc"], 1)
            dve.scalar_tensor_tensor(out=ahead[:, :], in0=bank[3][:, 0:P], scalar=dstb[:, RW - 1:RW], in1=upper[:, :],
                                     op0=ALU.is_equal, op1=ALU.mult)
            dve.drain()
            dve.nop().then_inc(s["ahead_ready"], 1)
            dve.wait_ge(s["base_ps"], 1)
            dve.tensor_copy(base[:, :], bank[4][:, 0:NB])
            dve.memset(rank[:, :], -1.0)
            dve.drain()
            for i in range(NB):
                dve.tensor_scalar(tmp[:, 0, :], srcb[:, :], float(i), None, ALU.is_equal)
                dve.drain()
                dve.tensor_tensor_scan(tmp[:, 1, :], same[:, :], tmp[:, 0, :], base[:, i:i + 1], ALU.mult, ALU.add)
                dve.drain()
                dve.tensor_tensor(tmp[:, 2, :], tmp[:, 0, :], tmp[:, 1, :], ALU.mult)
                dve.drain()
                dve.tensor_tensor(rank[:, :], rank[:, :], tmp[:, 2, :], ALU.add)
                dve.drain()
            dve.scalar_tensor_tensor(out=tmp[:, 3, :], in0=dstb[:, :], scalar=float(P), in1=dst1[:, :], op0=ALU.mult, op1=ALU.add)
            dve.drain()
            dve.tensor_scalar(diag[:, :], ident[:, :], tmp[:, 3, 0:1], None, ALU.mult)
            dve.tensor_tensor(tmp[:, 2, 1:RW], tmp[:, 3, 1:RW], tmp[:, 3, 0:RW - 1], ALU.is_lt)
            dve.drain()
            dve.sem_inc(s["bad_sb"], 1)
            dve.tensor_reduce(bad[:, 0:1], tmp[:, 2, 1:RW], AX.X, ALU.max)
            dve.wait_ge(s["key_bc2"], 1)
            dve.scalar_tensor_tensor(out=ahead[:, :], in0=bank[3][:, 0:P], scalar=tmp[:, 3, RW - 1:RW], in1=upper[:, :],
                                     op0=ALU.is_lt, op1=ALU.mult)
            dve.drain()
            dve.tensor_reduce(bad[:, 1:2], ahead[:, :], AX.X, ALU.max)
            dve.drain()
            dve.tensor_copy(ti[:, 0, :], rank[:, :])
            dve.drain()
            dve.tensor_single_scalar(ti[:, 1, :], ti[:, 0, :], 7, op=ALU.arith_shift_right)
            dve.drain()
            dve.tensor_single_scalar(ti[:, 0, :], ti[:, 0, :], P - 1, op=ALU.bitwise_and)
            dve.tensor_copy(tmp[:, 0, :], ti[:, 1, :])
            dve.drain()
            dve.tensor_copy(rank[:, :], ti[:, 0, :])
            dve.scalar_tensor_tensor(out=tmp[:, 1, :], in0=srcb[:, :], scalar=2.0, in1=tmp[:, 0, :],
                                     op0=ALU.mult, op1=ALU.add)
            dve.drain()
            dve.tensor_tensor(tmp[:, 2, :], dstb[:, :], srcb[:, :], ALU.is_equal)
            dve.drain()
            dve.tensor_tensor(tmp[:, 3, :], tmp[:, 0, :], tmp[:, 2, :], ALU.subtract)
            dve.drain()
            dve.tensor_reduce(bad[:, 2:3], tmp[:, 3, :], AX.X, ALU.max)
            dve.drain()
            dve.tensor_scalar(bad[:, 2:3], bad[:, 2:3], 2.0, None, ALU.is_ge)
            dve.drain()
            dve.tensor_reduce(bad[:, 3:4], bad[:, 0:3], AX.X, ALU.add)
            dve.drain()
            dve.sem_inc(s["bad_sb"], 1)
            dve.tensor_scalar(tmp[:, 2, :], tmp[:, 1, :], -1.0, float(BT - 1), ALU.mult, ALU.add)
            dve.tensor_scalar(tmp[:, 3, :], tmp[:, 0, :], 2.0, None, ALU.is_equal)
            dve.drain()
            dve.tensor_tensor(tmp[:, 2, :], tmp[:, 2, :], tmp[:, 3, :], ALU.mult)
            dve.scalar_tensor_tensor(out=tmp[:, 1, :], in0=dstb[:, :], scalar=float(BT), in1=tmp[:, 1, :],
                                     op0=ALU.mult, op1=ALU.add)
            dve.drain()
            dve.tensor_tensor(tmp[:, 1, :], tmp[:, 1, :], tmp[:, 2, :], ALU.add)
            dve.drain()
            dve.scalar_tensor_tensor(out=rank[:, :], in0=rank[:, :], scalar=float(NB * BT), in1=tmp[:, 1, :],
                                     op0=ALU.mult, op1=ALU.add)
            dve.wait_ge(s["ld_x"], 64)
            dve.drain()
            dve.nop().then_inc(s["place_ready"], 1)
            dve.wait_ge(s["bad_ps"], 1)
            dve.tensor_scalar(flag[:, :], bank[4][:, 0:1], 0.0, None, ALU.is_equal)
            dve.drain()
            dve.sem_inc(s["flag_ready"], 1)
            for n in range(4 * TR):
                f, b = n // TR, n % TR
                o = (slot_i[:, :] if f == 0 else rec[:, :, f - 1]).rearrange("q (r b) -> q r b", b=TR)[:, :, b]
                dve.wait_ge(s["place_ps"], n + 1)
                dve.tensor_copy(o, bank[n % 2][:, 0:RR]).then_inc(s["place_sb"], 1)
            dve.drain()
            dve.tensor_copy(fix[:, 0:1], slot_i[:, NT - 1:NT])
            dve.drain()
            dve.tensor_tensor(fix[:, 1:2], fix[:, 0:1], trash[:, 0:1], ALU.subtract)
            dve.drain()
            dve.tensor_tensor(fix[:, 0:1], fix[:, 1:2], trash[:, 1:2], ALU.mult)
            dve.drain()
            dve.tensor_tensor(slot_i[:, NT - 1:NT], fix[:, 0:1], trash[:, 0:1], ALU.add)
            dve.drain()
            dve.nop().then_inc(s["rec_ready"], 1)
            for i in range(NB):
                dve.tensor_scalar(tmp[:, i % 2, :], dstb[:, :], float(i), 0.0, ALU.is_le, ALU.add,
                                  accum_out=upto[:, i:i + 1])
                dve.drain()
            dve.nop().then_inc(s["upto_sb"], 1)
            dve.wait_ge(s["upto_ps"], 1)
            dve.tensor_scalar(need_f[:, :], bank[2][:, 0:NB], 1.0 / (SH * P), 1.0, ALU.mult, ALU.add)
            dve.drain()
            dve.tensor_scalar(need[:, :], need_f[:, :], float(2 * NG), None, ALU.min)
            dve.drain()
            dve.nop().then_inc(s["need_ready"], 1)
            dve.nop().then_inc(s["edge_done"], 1)

            def fast_layers():
                dve.wait_ge(s["edge_done"], 2)
                dve.memset(r3[:, 1, HT - 1:HT, :], 0.0)
                iota_h = iota_nt[:, :, 0:HT]
                tall = lambda a: a.rearrange("p (o t) -> p o t", o=1).broadcast_to([P, P, HT])
                def one_hots(j, c):
                    dve.wait_ge(s["r3a" if c == 0 else "r3b"], j * 16 + 16)
                    r = r3[:, c, :, :]
                    dve.tensor_copy(loc[:, c, 0, :], r[:, :, 1])
                    dve.tensor_copy(loc[:, c, 1, :], r[:, :, 2])
                    dve.tensor_copy(wsp[:, c, 0, :], r[:, :, 0])
                    dve.drain()
                    dve.tensor_tensor(wres[:, c, 0, :], r[:, :, 0], wsp[:, c, 0, :], ALU.subtract)
                    dve.drain()
                    dve.nop().then_inc(s[f"r3_free{c}"], 1)
                    dve.tensor_copy(wsp[:, c, 1, :], wres[:, c, 0, :])
                    dve.drain()
                    dve.tensor_tensor(wres[:, c, 1, :], wres[:, c, 0, :], wsp[:, c, 1, :], ALU.subtract)
                    dve.drain()
                    dve.tensor_copy(wsp[:, c, 2, :], wres[:, c, 1, :])
                    dve.wait_ge(s[f"oh_used{c}"], j)
                    dve.tensor_tensor(oh_s[:, c, :, :], iota_h, tall(loc[:, c, 0, :]), ALU.is_equal)
                    dve.tensor_tensor(oh_d[:, c, :, :], iota_h, tall(loc[:, c, 1, :]), ALU.is_equal)
                    dve.drain()
                    for k in range(3):
                        dve.tensor_tensor(oh_w[:, c, k, :, :], oh_s[:, c, :, :], tall(wsp[:, c, k, :]), ALU.mult)
                    dve.drain()
                    dve.nop().then_inc(s["oh_ready"], 1)

                groups = banks_of(NB)
                NGR = len(groups)

                def add_diagonal(j, par):
                    dve.wait_ge(s["row_sb"], (j + 1) * NGR)
                    dve.wait_ge(s["diag_ps"], j + 1)
                    a = arow[par][:, bass.ds(j * P, P)]
                    dve.tensor_tensor(a, a, bank[7][:, 0:P], ALU.add)
                    dve.drain()
                    dve.nop().then_inc(s["row_add"], 1)

                def sum_first(j, first=False):
                    for g, bs in enumerate(groups):
                        dve.wait_ge(s["l1_ps"], j * NGR + (NGR + g + 1))
                        b, a = bank[3 + g % 2][:, 0:len(bs) * P], y1[:, g * BANK:g * BANK + len(bs) * P]
                        if first:
                            dve.tensor_copy(a, b).then_inc(s["l1_free"], 1)
                        else:
                            dve.tensor_tensor(a, a, b, ALU.add).then_inc(s["l1_free"], 1)
                    dve.drain()

                dve.sem_inc(s["l1_free"], NGR)
                one_hots(0, 0)
                one_hots(0, 1)

                def row(j, par, first=False):
                    one_hots(j, 0)
                    add_diagonal(j - 1, 1 - par)
                    one_hots(j, 1)
                    sum_first(j - 1, first)

                row(1, 1, first=True)
                row(2, 0)
                with dve.Fori(1, NB // 2) as i:
                    row(i * 2 + 1, 1)
                    row(i * 2 + 2, 0)
                add_diagonal(NB - 1, 0)
                sum_first(NB - 1)

                dve.wait_ge(s["adj_out1"], 16 * (NB // 2))
                for l in range(LAYERS):
                    for g, bs in enumerate(groups):
                        n = len(bs)
                        dve.wait_ge(s["lay_T"], l * NGR + (g + 1))
                        part = lambda a: a[:, bs[0]:bs[0] + n, :].rearrange("p b n -> p (b n)")
                        dve.tensor_copy(part(cur), bank[g][:, 0:n * P])
                        if l == 0:
                            dve.scalar_tensor_tensor(out=part(acc), in0=part(xs), scalar=2.0, in1=bank[g][:, 0:n * P],
                                                     op0=ALU.mult, op1=ALU.add)
                        else:
                            dve.tensor_tensor(part(acc), part(acc), bank[g][:, 0:n * P], ALU.add)
                        dve.drain()
                        dve.nop().then_inc(s["cur_sb"], 1)

            def any_tiles(k):
                kind = passes[k][0]
                n0 = k * NT
                gathers = passes[k][3]
                ia, ib = (g_dst, g_src) if kind == "spmm" else (g_src, g_dst)
                key, lead, shift, place = (g_key[:, c:c + 1] for c in range(4))
                with dve.Fori(0, NT) as t:
                    dve.wait_ge(s["g_done"], t + (n0 + 1))
                    dve.tensor_copy(g_ki[:, 0:1], ia[:, bass.ds(t, 1)])
                    dve.tensor_copy(g_ki[:, 1:2], ib[:, bass.ds(t, 1)])
                    dve.tensor_copy(key, ib[:, bass.ds(t, 1)])
                    dve.drain()
                    dve.tensor_scalar(g_diag[:, 0, :], ident[:, :], key, None, ALU.mult)
                    dve.drain()
                    dve.sem_inc(s["g_keys"], 1)
                    dve.wait_ge(s["g_bc"], t + (n0 + 1))
                    dve.tensor_scalar(g_same[:, :], bank[0][:, 0:P], key, None, ALU.is_equal)
                    dve.drain()
                    dve.tensor_tensor(g_tmp[:, 0, :], g_same[:, :], g_low[:, :], ALU.mult)
                    dve.tensor_tensor(shift, key, g_trash[:, :], ALU.subtract)
                    dve.drain()
                    dve.tensor_reduce(place, g_tmp[:, 0, :], AX.X, ALU.max)
                    dve.drain()
                    dve.tensor_scalar(lead, place, 0.0, None, ALU.is_equal)
                    dve.drain()
                    dve.tensor_tensor(place, lead, shift, ALU.mult)
                    dve.drain()
                    dve.tensor_tensor(g_so[:, :], place, g_trash[:, :], ALU.add)
                    dve.wait_ge(s[f"g_in{k}"], (t + 1) * (16 * gathers))
                    if kind == "spmm":
                        dve.tensor_scalar(g_msg[:, 0:D], g_a[:, 0:D], rec[:, bass.ds(t, 1), 0], None, ALU.mult)
                    elif kind == "max":
                        row = g_att[:, bass.ds(t, 1), :].rearrange("p o h -> p (o h)")
                        dve.tensor_tensor(g_s[:, 0, :], g_a[:, D:D + H], g_b[:, D + H:D + 2 * H], ALU.add)
                        dve.drain()
                        dve.tensor_tensor(g_s[:, 1, :], g_s[:, 0, :], row, ALU.add)
                        dve.drain()
                        dve.scalar_tensor_tensor(out=g_s[:, 2, :], in0=g_s[:, 1, :], scalar=0.2, in1=g_s[:, 1, :],
                                                 op0=ALU.mult, op1=ALU.max)
                        dve.drain()
                        dve.tensor_copy(row, g_s[:, 2, :])
                        for h in range(H):
                            dve.tensor_scalar(g_diag[:, h, :], ident[:, :], g_s[:, 2, h:h + 1], None, ALU.mult)
                    else:
                        dve.tensor_tensor(g_s[:, 1, :], g_att[:, bass.ds(t, 1), :].rearrange("p o h -> p (o h)"),
                                          g_b[:, 0:H], ALU.subtract)
                        dve.drain()
                        dve.sem_inc(s["g_arg"], 1)
                        dve.wait_ge(s["g_ex"], t + 1)
                        dve.tensor_tensor(g_msg[:, 0:D].rearrange("p (h d) -> p h d", h=H),
                                          g_a[:, 0:D].rearrange("p (h d) -> p h d", h=H),
                                          g_s[:, 2, :].rearrange("p (h o) -> p h o", o=1).broadcast_to([P, H, HD]), ALU.mult)
                        dve.tensor_copy(g_msg[:, D:D + H], g_s[:, 2, :])
                        dve.memset(g_msg[:, D + H:MW], 1.0)
                    dve.drain()
                    dve.sem_inc(s["g_msgs"], 1)
                    dve.wait_ge(s["g_tot"], t + (n0 + 1))
                    if kind == "max":
                        dve.tensor_tensor(g_tmp[:, :, :], bank[1][:, :].rearrange("p (h n) -> p h n", h=H),
                                          g_same[:, :].rearrange("p (o n) -> p o n", o=1).broadcast_to([P, H, P]), ALU.mult)
                        dve.drain()
                        dve.tensor_reduce(g_s[:, 3, :], g_tmp[:, :, :], AX.X, ALU.max)
                        dve.drain()
                        dve.tensor_tensor(g_new[:, 0:H], g_s[:, 3, :], g_old[:, 0:H], ALU.max)
                    else:
                        w = D if kind == "spmm" else MW
                        dve.tensor_tensor(g_new[:, 0:w], bank[1][:, 0:w], g_old[:, 0:w], ALU.add)
                    dve.drain()
                    dve.sem_inc(s["g_news"], 1)

            def any_layers():
                dve.wait_ge(s["g_init"], 6)
                dve.wait_ge(s["g_ld"], 64)
                dve.wait_ge(s["rec_se"], NG + 1)
                dve.tensor_copy(g_att[:, :, :], rec[:, 0:NT, H:2 * H])
                dve.tensor_scalar(acc[:, :, :], xs[:, :, :], 2.0, None, ALU.mult)
                dve.drain()
                for k in range(LAYERS):
                    any_tiles(k)
                dve.wait_ge(s["g_back"], 16 * LAYERS)
                for l in range(LAYERS):
                    dve.tensor_tensor(acc[:, :, :], acc[:, :, :], ablk[:, l, :].rearrange("p (b d) -> p b d", b=NB), ALU.add)
                    dve.drain()

            def any_attention():
                dve.tensor_tensor(hx, hsp[:, :, 0, :], hsp[:, :, 1, :], ALU.add)
                dve.drain()
                dve.tensor_tensor(hx, hx, hsp[:, :, 2, :], ALU.add)
                dve.drain()
                dve.sem_inc(s["g_hx"], 1)
                for k in range(LAYERS, len(passes)):
                    any_tiles(k)
                dve.wait_ge(s["g_fin"], 32)
                dve.wait_ge(s["g_emn"], 1)
                dve.tensor_scalar(g_m[:, :, :], g_num[:, :, D + H:MW].broadcast_to([P, NB, H]), -1.0, float(E), ALU.mult, ALU.add)
                dve.drain()
                dve.tensor_tensor(g_m[:, :, :], g_m[:, :, :], g_e[:, :, :], ALU.mult)
                dve.drain()
                dve.tensor_tensor(g_m[:, :, :], g_m[:, :, :], g_num[:, :, D:D + H], ALU.add)
                dve.drain()
                dve.reciprocal(g_e[:, :, :], g_m[:, :, :])
                dve.drain()
                for h in range(H):
                    dve.tensor_tensor(acc[:, :, h * HD:(h + 1) * HD], g_num[:, :, h * HD:(h + 1) * HD],
                                      g_e[:, :, h:h + 1].broadcast_to([P, NB, HD]), ALU.mult)
                dve.drain()

            dve.wait_ge(s["flag_ready"], 1)
            plain = dve.value_load(flag[0:1, 0:1], min_val=0, max_val=1)
            with dve.If(plain):
                fast_layers()
            with dve.Else():
                any_layers()
            groups = banks_of(NB)
            norm(cur[:, :, :], acc[:, :, :], 1)
            dve.nop().then_inc(s["x1_ready"], 1)
            dve.wait_ge(s["h_sb"], -(-NB // 3))
            for k in range(3):
                dve.tensor_copy(hsp[:, :, k, :], hx[:, :, :])
                dve.drain()
                if k < 2:
                    dve.tensor_tensor(hx[:, :, :], hx[:, :, :], hsp[:, :, k, :], ALU.subtract)
                    dve.drain()
            dve.nop().then_inc(s["h_split"], 1)

            RH = HT * H

            def take_records(b, turn):
                dve.wait_ge(s[f"r6_in{b}"], turn * 16 + 16)
                dve.tensor_copy(loc6[:, b, :], r6[:, b, :, 2])
                dve.tensor_copy(dlr[:, :, :], r6[:, b, :, 2:3].broadcast_to([P, BTP, H]))
                dve.drain()
                dve.sem_inc(s["dlr_ready"], 1)

            def one_hot(j, b, par):
                dve.wait_ge(s["d6_ready"], j * NQ + NQ)
                dve.tensor_tensor(d16[:, par, :, :], iota_nt[:, :, :],
                                  loc6[:, b, :].rearrange("p (o t) -> p o t", o=1).broadcast_to([P, P, BTP]),
                                  ALU.is_equal).then_inc(s["d16_ready"], 1)

            def messages(j, par, lo, hi):
                for q in range(lo, hi):
                    n = min(BT, BPB * (q + 1)) - BPB * q
                    if q == 0:
                        dve.wait_ge(s["ex_sb"], j + 1)
                    dve.wait_ge(s["hg_ps"], j * NQ + (3 * NQ + q + 1))
                    dve.wait_ge(s["msg_used"], j * NQ + before(q, MR))
                    dve.tensor_copy(msg[:, q % MR, 0:n, D:D + H], ex[:, par, BPB * q:BPB * q + n, :])\
                        .then_inc(s["msg_sb"], 1)
                    dve.tensor_tensor(
                        msg[:, q % MR, 0:n, 0:D].rearrange("p t (h d) -> p t h d", h=H),
                        bank[HG[q % HR]][:, 0:n * P].rearrange("p (t h d) -> p t h d", h=H, d=HD),
                        ex[:, par, BPB * q:BPB * q + n, 0:H].rearrange("p t (h o) -> p t h o", o=1).broadcast_to([P, n, H, HD]),
                        ALU.mult).then_inc(s["msg_sb"], 1)

            def sum_parts(b0, b1):
                for lo, hi, k in ((0, 40, b0), (40, BT, b1)):
                    dve.tensor_reduce(sc2[:, lo:hi, :], bank[k][:, 0:(hi - lo) * 3 * H]
                                      .rearrange("p (t k h) -> p t h k", k=3, h=H), AX.X, ALU.add)
                dve.drain()

            def step(j, b, par, after, sums=True):
                def msgs(lo, hi):
                    if sums:
                        messages(j - 1, (b - 1) % 3, lo, hi)

                dve.wait_ge(s["at_ps"], j + 1)
                sum_parts(5, 6)
                dve.tensor_tensor(sc2[:, 0:BT, :], sc2[:, 0:BT, :], r6[:, b, 0:BT, H:2 * H], ALU.add)
                dve.drain()
                dve.sem_inc(s["r6_free"], 1)
                dve.scalar_tensor_tensor(out=sc[:, 0:BT, :], in0=sc2[:, 0:BT, :], scalar=0.2, in1=sc2[:, 0:BT, :],
                                         op0=ALU.mult, op1=ALU.max)
                dve.drain()
                dve.sem_inc(s["at_sb"], 1)
                msgs(0, DCUTS[0])
                dve.tensor_copy(dlT[0:RH, :, :].rearrange("p k n -> p (k n)"), bank[6][0:RH, 2 * P:4 * P])
                dve.drain()
                dve.tensor_tensor(keep[0:RH, :, 1:P], dlT[0:RH, :, 1:P], dlT[0:RH, :, 0:P - 1], ALU.is_equal)
                dve.tensor_tensor(endz[0:RH, :, 0:P - 1], dlT[0:RH, :, 1:P], dlT[0:RH, :, 0:P - 1], ALU.not_equal)
                dve.drain()
                dve.wait_ge(s["atT_ps"], j + 1)
                dve.tensor_tensor_scan(run[0:RH, :, :].rearrange("p k n -> p (k n)"),
                                       keep[0:RH, :, :].rearrange("p k n -> p (k n)"), bank[7][0:RH, 0:2 * P],
                                       0.0, ALU.mult, ALU.max)
                dve.drain()
                dve.tensor_tensor(run[0:RH, :, :], run[0:RH, :, :], endz[0:RH, :, :], ALU.mult)
                dve.drain()
                dve.sem_inc(s["z_sb"], 1)
                take_records((b + 1) % 3, after)
                msgs(DCUTS[0], DCUTS[1])
                dve.wait_ge(s["zT_ps"], j + 1)
                dve.tensor_copy(zs[:, 0, :, :].rearrange("p t h -> p (t h)"), bank[7][:, 0:BTP * H])
                dve.drain()
                for k in range(3):
                    dve.tensor_copy(zsp[:, k, :, :], zs[:, k, :, :])
                    dve.drain()
                    if k < 2:
                        dve.tensor_tensor(zs[:, k + 1, :, :], zs[:, k, :, :], zsp[:, k, :, :], ALU.subtract)
                        dve.drain()
                dve.sem_inc(s["zs_sb"], 1)
                msgs(DCUTS[1], DCUTS[2])
                dve.wait_ge(s["v_ps"], j + 1)
                sum_parts(5, 6)
                dve.tensor_reduce(mm[:, 0, :], sc2[:, 0:BT, :].rearrange("p t h -> p h t"), AX.X, ALU.max)
                dve.drain()
                dve.tensor_copy(msp[:, 0, :], mm[:, 0, :])
                dve.drain()
                dve.tensor_tensor(mm[:, 1, :], mm[:, 0, :], msp[:, 0, :], ALU.subtract)
                dve.drain()
                dve.tensor_copy(msp[:, 1, :], mm[:, 1, :])
                dve.drain()
                dve.tensor_tensor(mm[:, 2, :], mm[:, 1, :], msp[:, 1, :], ALU.subtract)
                dve.drain()
                dve.tensor_copy(msp[:, 2, :], mm[:, 2, :])
                dve.drain()
                dve.sem_inc(s["m_sb"], 1)
                msgs(DCUTS[2], NQ)
                one_hot(j + 1, (b + 1) % 3, 1 - par)
                dve.wait_ge(s["mg_ps"], j + 1)
                sum_parts(*MG)
                dve.tensor_tensor(me[:, 0:BT, :], sc[:, 0:BT, :], sc2[:, 0:BT, :], ALU.subtract)
                dve.drain()
                dve.sem_inc(s["arg_sb"], 1)

            def fast_attention():
                dve.memset(r6[:, :, BT:BTP, :], 0.0)
                dve.memset(sc[:, BT:BTP, :], 0.0)
                dve.memset(keep[:, :, 0:1], 0.0)
                dve.memset(endz[:, :, P - 1:P], 1.0)
                dve.memset(msg[:, :, :, D + H:MW], 1.0)
                dve.drain()
                dve.sem_inc(s["r6_free"], 3)
                dve.sem_inc(s["msg_sb"], 2 * NQ)
                take_records(0, 0)
                one_hot(0, 0, 0)
                step(0, 0, 0, 0, sums=False)
                with dve.Fori(0, NB // 6) as i:
                    for u in range(1, 7):
                        step(i * 6 + u, u % 3, u % 2, i * 2 + (u + 1) // 3)
                messages(NB - 1, 0, 0, NQ)
                dve.wait_ge(s["num_free"], NB + 1)
                dve.wait_ge(s["emn_sb"], NB)
                dve.tensor_scalar(den[:, 0, :, :], dens[:, :, H:H + 1].broadcast_to([P, NB, H]), -1.0, float(E),
                                  ALU.mult, ALU.add)
                dve.drain()
                dve.tensor_tensor(den[:, 1, :, :], den[:, 0, :, :], emn[:, :, :], ALU.mult)
                dve.drain()
                dve.tensor_tensor(den[:, 0, :, :], den[:, 1, :, :], dens[:, :, 0:H], ALU.add)
                dve.drain()
                dve.reciprocal(den[:, 1, :, :], den[:, 0, :, :])
                dve.drain()
                for h in range(H):
                    a = acc[:, :, h * HD:(h + 1) * HD]
                    dve.tensor_tensor(a, a, den[:, 1, :, h:h + 1].broadcast_to([P, NB, HD]), ALU.mult)
                dve.drain()

            with dve.If(plain):
                fast_attention()
            with dve.Else():
                any_attention()
            dve.tensor_tensor(acc[:, :, :], acc[:, :, :], cur[:, :, :], ALU.add)
            dve.drain()
            norm(cur[:, :, :], acc[:, :, :], 2)
            dve.nop().then_inc(s["y_sb"], 1)


INPUTS = ["x", "src", "dst", "edge_attr_64", "edge_weight", "L1_gnn_W_node", "L1_gnn_W_edge", "L1_gnn_a"]


def kernel(**inputs):
    import concourse.bacc as bacc
    from concourse.bass_utils import run_bass_kernel_spmd as run

    nc = bacc.Bacc("TRN2", target_bir_lowering=False, num_devices=1)
    arrays, args = {}, []
    for name in INPUTS:
        a = np.ascontiguousarray(inputs[name])
        arrays[f"in_{name}"] = a
        args.append(nc.dram_tensor(f"in_{name}", a.shape, mybir.dt.from_np(a.dtype), kind="ExternalInput").ap())
    out = nc.dram_tensor("out", (N, D), F32, kind="ExternalOutput").ap()
    build(nc, *args, out)
    r = run(nc, [arrays], core_ids=[0])
    return r.results[0]["out"]
```

```python
from contextlib import ExitStack

import numpy as np

import concourse.bass as bass
from concourse import mybir

F32, BF16, I32 = mybir.dt.float32, mybir.dt.bfloat16, mybir.dt.int32
ALU, ACT = mybir.AluOpType, mybir.ActivationFunctionType
AX = mybir.AxisListType

P = 128
N, D, E, DE = 3125, 128, 103125, 64
H, HD = 4, 32
NB = -(-N // P)
NL = N - (NB - 1) * P
NP = NB * P
SH = 31
HE = SH * P
NH = -(-E // HE)
NG = NH // 2
SG = 2 * SH
NT = NH * SH
LP, LU = divmod(E - (NH - 1) * HE, SH)
RW = -(-E // P)
RF, RL = divmod(E, RW)
RR = RF + 1
BT = 2 * NB + 1
BTP = BT + 1
HT = BTP // 2
NPAIR = -(-NB // 2)
HI = 4096
SLOTS = P * NB * BT
REC = 8
assert NH == 2 * NG and NG % 2 == 1 and RR <= P and NH * HE <= RR * RW and BT == 51 and HT == 26
AHEAD = 4
LAYERS = 3
GW = D + 2 * H
TBL = NP + 2 * P
EPS = 1e-5
MW = D + H + 1
BANK = 512
BPB = BANK // P
UNITS = [(k, u, min(2, SH - u)) for k in range(2) for u in range(0, SH, 2)]
CHUNKS = [UNITS[i:i + BPB] for i in range(0, len(UNITS), BPB)]
NC = len(CHUNKS)
SQ = 14
HC = -(-NB // 3)
RING = 5
NQ = BTP // BPB
TI = -(-HT // BPB)
ER = 4
RB = 3
HR, MR = 3, 4
NR = NB // RING
assert LAYERS == 3 and NB % RING == 0 and NB % 6 == 1


def banks_of(n):
    return [list(range(s, min(s + BPB, n))) for s in range(0, n, BPB)]


def before(n, ring):
    if n >= ring:
        return NQ + n - ring + 1
    return max(m for m in range(NQ) if m % ring == n) + 1


def build(nc, x, src, dst, edge_attr, edge_weight, w_node, w_edge, att, out):
    ctx = ExitStack()
    slots = nc.dram_tensor("slots", (SLOTS + P, REC), F32, kind="Internal").ap()
    g_x = [nc.dram_tensor(f"g_x{l}", (TBL, D), F32, kind="Internal").ap() for l in range(LAYERS + 1)]
    g_h = nc.dram_tensor("g_h", (TBL, GW), F32, kind="Internal").ap()
    g_max = nc.dram_tensor("g_max", (TBL, H), F32, kind="Internal").ap()
    g_sum = nc.dram_tensor("g_sum", (TBL, MW), F32, kind="Internal").ap()
    slot_d = nc.dram_tensor("slot_d", (RR * RW,), I32, kind="Internal").ap()
    turned = nc.dram_tensor("turned", (NB, P, BTP, 2, P), BF16, kind="Internal").ap()
    adj = nc.dram_tensor("adj", (NB, P, NP), F32, kind="Internal").ap()

    with ctx:
        def sb(name, shape, dt, c=ctx):
            return c.enter_context(nc.sbuf_tensor(name, shape, dt))

        def sem(name):
            return ctx.enter_context(nc.semaphore(name))

        ident = sb("ident", [P, P], F32)
        identb = sb("identb", [P, P], BF16)
        ones = sb("ones", [P, P], F32)
        zerob = sb("zerob", [P, BANK], BF16)
        iota_nt = sb("iota_nt", [P, P, BTP], BF16)
        cur = sb("cur", [P, NB, D], F32)
        acc = sb("acc", [P, NB, D], F32)
        acat = sb("acat", [P, 3, H], F32)
        wn = sb("wn", [P, D], F32)
        we2 = sb("we2", [P, 2, DE], F32)
        wext = sb("wext", [P, D + 2 * H], F32)
        wedge = sb("wedge", [P, 2 * H], F32)
        st = sb("st", [P, 4, NB], F32)
        junk, junk2 = sb("junk", [P, D], F32), sb("junk2", [P, 2, D], F32)
        upto = sb("upto", [P, NB], F32)
        need_f = sb("need_f", [P, NB], F32)
        need = sb("need", [P, NB], I32)
        bad = sb("bad", [P, 4], F32)
        flag = sb("flag", [P, 1], I32)

        early = ExitStack()
        xs = sb("xs", [P, NB, D], F32, early)
        rec = sb("rec", [P, NT, REC], F32, early)
        slot_i = sb("slot_i", [P, NT], I32, early)
        st_rec = sb("st_rec", [P, 2, SH, REC], F32, early)
        st_slot = sb("st_slot", [P, 2, SH], I32, early)

        with ExitStack() as c:
            src_i, dst_i = sb("src_i", [P, RW], I32, c), sb("dst_i", [P, RW], I32, c)
            w_t = sb("w_t", [P, NT], F32, c)
            past = sb("past", [P, RW], I32, c)
            ti = sb("ti", [P, 2, RW], I32, c)
            odd = sb("odd", [P, RW], I32, c)
            pair, unit = sb("pair", [P, RW], F32, c), sb("unit", [P, RW], F32, c)
            packed = sb("packed", [P, 3, RW], F32, c)
            scans = sb("scans", [P, 2, RW], F32, c)
            srcb, dstb = sb("srcb", [P, RW], F32, c), sb("dstb", [P, RW], F32, c)
            same = sb("same", [P, RW], F32, c)
            tmp = sb("tmp", [P, 4, RW], F32, c)
            rank = sb("rank", [P, RW], F32, c)
            lasts = sb("lasts", [P, NPAIR], F32, c)
            base = sb("base", [P, NPAIR], F32, c)
            ahead = sb("ahead", [P, P], F32, c)
            diag = sb("diag", [P, 2, P], F32, c)
            below = sb("below", [P, P], F32, c)
            upper = sb("upper", [P, P], F32, c)
            starts = sb("starts", [P, NH], F32, c)
            zrec = sb("zrec", [P, BT * REC], F32, c)
            ea = sb("ea", [P, 2, 2, SH, DE], F32, c)
            eaT = sb("eaT", [P, ER, BANK], F32, c)
        with ExitStack() as c:
            r3 = sb("r3", [P, 2, HT, REC], F32, c)
            oh_d, oh_s = sb("oh_d", [P, 2, P, HT], BF16, c), sb("oh_s", [P, 2, P, HT], BF16, c)
            oh_w = sb("oh_w", [P, 2, 3, P, HT], BF16, c)
            loc = sb("loc", [P, 2, 2, HT], BF16, c)
            wsp = sb("wsp", [P, 2, 3, HT], BF16, c)
            wres = sb("wres", [P, 2, 2, HT], F32, c)
            arow0 = sb("arow0", [P, NP], F32, c)
            xst = sb("xst", [P, 2, D], F32, c)
            tb = sb("tb", [P, 2, HT, 2, P], BF16, c)
        with ExitStack() as c:
            ablk = sb("ablk", [P, RING, NP], F32, c)
            stage = sb("stage", [P, RING, D], F32, c)
            curT = sb("curT", [P, NP], F32, c)
        early.close()
        with ExitStack() as c:
            hsp = sb("hsp", [P, NB, 3, D + 2 * H], BF16, c)
            r6 = sb("r6", [P, 3, BTP, REC], F32, c)
            loc6 = sb("loc6", [P, 3, BTP], BF16, c)
            d16 = sb("d16", [P, 2, P, BTP], BF16, c)
            d6 = sb("d6", [P, MR, BPB, P], F32, c)
            rT = sb("rT", [P, 3, BTP, 2, P], BF16, c)
            dlr = sb("dlr", [P, BTP, H], F32, c)
            sc = sb("sc", [P, BTP, H], F32, c)
            sc2 = sb("sc2", [P, BTP, H], F32, c)
            dlT = sb("dlT", [P, 2, P], F32, c)
            keep = sb("keep", [P, 2, P], F32, c)
            endz = sb("endz", [P, 2, P], F32, c)
            run = sb("run", [P, 2, P], F32, c)
            zs = sb("zs", [P, 3, BTP, H], F32, c)
            zsp = sb("zsp", [P, 3, BTP, H], BF16, c)
            mm = sb("mm", [P, 3, H], F32, c)
            msp = sb("msp", [P, 3, H], BF16, c)
            emn = sb("emn", [P, NB, H], F32, c)
            dens = sb("dens", [P, NB, H + 1], F32, c)
            den = sb("den", [P, 2, NB, H], F32, c)
            me = sb("me", [P, BTP, H], F32, c)
            ex = sb("ex", [P, 3, BTP, H], F32, c)
            msg = sb("msg", [P, MR, BPB, MW], F32, c)
        with ExitStack() as c:
            sb("any_skip", [P, NB * D + NT * (REC + 1) + 2 * SH * (REC + 1) + RING * (NP + D) + NP], F32, c)
            g_src, g_dst = sb("g_src", [P, NT], I32, c), sb("g_dst", [P, NT], I32, c)
            g_att = sb("g_att", [P, NT, H], F32, c)
            g_ki, g_so = sb("g_ki", [P, 2], I32, c), sb("g_so", [P, 1], I32, c)
            g_key = sb("g_key", [P, 4], F32, c)
            g_trash, g_zero = sb("g_trash", [P, 1], F32, c), sb("g_zero", [P, GW], F32, c)
            g_low, g_same = sb("g_low", [P, P], F32, c), sb("g_same", [P, P], F32, c)
            g_diag = sb("g_diag", [P, H, P], F32, c)
            g_tmp = sb("g_tmp", [P, H, P], F32, c)
            g_a, g_b = sb("g_a", [P, GW], F32, c), sb("g_b", [P, GW], F32, c)
            g_old, g_msg, g_new = sb("g_old", [P, GW], F32, c), sb("g_msg", [P, GW], F32, c), sb("g_new", [P, GW], F32, c)
            g_s = sb("g_s", [P, 4, H], F32, c)
            g_m, g_e = sb("g_m", [P, NB, H], F32, c), sb("g_e", [P, NB, H], F32, c)
        g_num = ablk[:, 0:2, :].rearrange("p r n -> p (r n)")[:, 0:NB * MW].rearrange("p (b n) -> p b n", b=NB)
        hx = ablk[:, 0:2, :].rearrange("p r n -> p (r n)")[:, 0:NB * (D + 2 * H)].rearrange("p (b n) -> p b n", b=NB)

        TB, HB = 3, (3, 4, 5, 6, 7)
        EB = (0, 1, 5, 6)
        HG, MG = (0, 1, 3), (7, 4)
        CUTS, DCUTS = (2, 6, 8), (3, 6, 8)
        cols = lambda a: a[:, :, :].rearrange("p b d -> p (b d)")
        src_t, dst_t = (packed[:, k, 0:NT].bitcast(I32) for k in (1, 2))
        loc_t = scans[:, :, 0:NT].bitcast(I32)
        slot_r = ti[:, 0, :]
        arow = (arow0[:, :], cols(cur))
        y1 = cols(acc)
        bank = [ctx.enter_context(nc.psum_tensor(f"bank{i}", [P, BANK], F32)) for i in range(8)]

        names = """consts clears ld_idx ld_w ld_x zeroed ea0 ea1 first_ready ahead_bc
            ahead_ready base_ps wt_ps wt_sb eaT_ps eaT_sb eaT_used rec_se ld_t rec_set slot_out slot_in0 slot_in1 place_ready staged armed half0 half1 landed need_ready block_in upto_sb upto_ps edge_done
            r3a r3b r3_free0 r3_free1 oh_ready oh_used0 oh_used1 row_ps row_free row_sb diag_ps row_add adj_out0 adj_out1
            xst_sb l1_ps l1_free
            a0 a1 a2 a3 a4 a_used0 a_used1 a_used2 a_used3 a_used4 stage_sb lay_ps lay_sb lay_T cur_sb acc_sb
            x1_ready x1T_ps x1T_sb h_ps part0 part1 part2 rest1 rest2 h_split
            r6_in0 r6_in1 r6_in2 rT_in0 rT_in1 rT_in2 r6_free d6_ready dlr_ready d16_ready turn_ps turn_sb turn_out0 turn_out1 at_ps at_sb atT_ps z_sb zT_ps zs_sb v_ps m_sb emn_sb mg_ps arg_sb ex_sb
            flag_ready bad_sb bad_ps g_init g_ld g_zeroed g_x0 g_keys g_bc g_in0 g_in1 g_in2 g_in3 g_in4 g_armed g_msgs g_arg g_ex g_tot g_news g_out
            g_done g_back g_hx g_hr g_fin g_emn
            hg_ps msg_sb msg_used num_free y_sb outs less_ready squares rs_var rs_std""".split()
        s = {n: sem(n) for n in names}

        e_rows = lambda t: t[0:RF * RW].rearrange("(r w) -> r w", w=RW)
        e_rest = lambda t: t[RF * RW:E].rearrange("(r w) -> r w", r=1)

        ANY_LAYERS = [("spmm", g_x[l], g_x[l + 1], 2) for l in range(LAYERS)]
        ANY_ATT = [("max", g_h, g_max, 3), ("sum", g_h, g_sum, 3)]
        passes = ANY_LAYERS + ANY_ATT


        def edge_tiles(eng, tiles, edges, signal, h0=0, h1=NH):
            full = min(h1, NH - 1)
            split = lambda a: a.rearrange("p (h u) -> p h u", u=SH)
            eng.dma_start(split(tiles)[:, h0:full, :],
                          edges[h0 * HE:full * HE].rearrange("(h p u) -> p h u", p=P, u=SH)).then_inc(signal, 16)
            if h1 == NH:
                last = edges[(NH - 1) * HE:E]
                eng.dma_start(tiles[0:LP, (NH - 1) * SH:NT], last[0:LP * SH].rearrange("(p u) -> p u", u=SH))\
                    .then_inc(signal, 16)
                eng.dma_start(tiles[LP:LP + 1, (NH - 1) * SH:(NH - 1) * SH + LU],
                              last[LP * SH:LP * SH + LU].rearrange("(o u) -> o u", o=1)).then_inc(signal, 16)

        block = ctx.enter_context(nc.Block())

        @block.sync
        def _(sp):
            sp.wait_ge(s["clears"], 4)
            for a, t in ((src_i, src), (dst_i, dst)):
                sp.dma_start(a[0:RF, :], e_rows(t)).then_inc(s["ld_idx"], 16)
                sp.dma_start(a[RF:RF + 1, 0:RL], e_rest(t)).then_inc(s["ld_idx"], 16)
            for h in range(H):
                sp.dma_start(acat[h * HD:(h + 1) * HD, :, h], att[h, :].rearrange("(k d) -> d k", k=3),
                             allow_slow_non_contiguous=True).then_inc(s["ld_w"], 16)
            sp.dma_start(wn[:, :], w_node).then_inc(s["ld_w"], 16)
            for k in range(2):
                sp.dma_start(we2[:, k, :], w_edge).then_inc(s["ld_w"], 16)

            def load_attr(g, buf, last=False):
                view = edge_attr[bass.ds(g * (SG * P), SG * P if not last else HE), :]\
                    .rearrange("(k p u) d -> k p (u d)", p=P, u=SH)
                for k in range(1 if last else 2):
                    sp.dma_start(ea[:, buf, k, :, :].rearrange("p u d -> p (u d)"), view[k]).then_inc(s[f"ea{buf}"], 16)
                if last:
                    rest = edge_attr[(NH - 1) * HE:E, :]
                    sp.dma_start(ea[0:LP, buf, 1, :, :].rearrange("p u d -> p (u d)"),
                                 rest[0:LP * SH, :].rearrange("(p u) d -> p (u d)", u=SH)).then_inc(s[f"ea{buf}"], 16)
                    sp.dma_start(ea[LP:LP + 1, buf, 1, 0:LU, :].rearrange("p u d -> p (u d)"),
                                 rest[LP * SH:LP * SH + LU, :].rearrange("(o u) d -> o (u d)", o=1))\
                        .then_inc(s[f"ea{buf}"], 16)

            load_attr(0, 0)
            sp.wait_ge(s["consts"], 9)
            edge_tiles(sp, w_t[:, :], edge_weight, s["ld_x"])
            load_attr(1, 1)
            sp.dma_start(xs[:, 0:NB - 1, :], x[0:(NB - 1) * P, :].rearrange("(b p) d -> p b d", p=P))\
                .then_inc(s["ld_x"], 16)
            sp.dma_start(xs[0:NL, NB - 1, :], x[(NB - 1) * P:N, :]).then_inc(s["ld_x"], 16)
            edge_tiles(sp, src_t, src, s["ld_t"])
            edge_tiles(sp, dst_t, dst, s["ld_t"])
            sp.dma_start(slots[0:SLOTS, :].rearrange("(p j t) f -> p j (t f)", p=P, j=NB),
                         zrec[:, :].rearrange("p (o n) -> p o n", o=1).broadcast_to([P, NB, BT * REC]))\
                .then_inc(s["zeroed"], 16)
            sp.dma_start(slots[SLOTS:SLOTS + P, :], zrec[:, 0:REC]).then_inc(s["zeroed"], 16)

            def slots_to_tiles():
                sp.wait_ge(s["place_ready"], 1)
                sp.dma_start(slot_d.rearrange("(r w) -> r w", w=RW), ti[0:RR, 0, :]).then_inc(s["slot_out"], 16)
                sp.wait_ge(s["slot_out"], 16)
                sp.dma_start(slot_i[:, 0:SG].rearrange("p (h u) -> p h u", u=SH),
                             slot_d[0:2 * HE].rearrange("(h p u) -> p h u", p=P, u=SH)).then_inc(s["slot_in0"], 16)
                sp.dma_start(slot_i[:, SG:NT].rearrange("p (h u) -> p h u", u=SH),
                             slot_d[2 * HE:NH * HE].rearrange("(h p u) -> p h u", p=P, u=SH)).then_inc(s["slot_in1"], 16)

            def load_groups(lo, hi):
                with sp.Fori(lo // 2, hi // 2) as g2:
                    for buf in range(2):
                        sp.wait_ge(s["eaT_ps"], (g2 * 2 + (buf - 1)) * NC)
                        load_attr(g2 * 2 + buf, buf)

            load_groups(2, AHEAD)
            slots_to_tiles()
            load_groups(AHEAD, NG - 1)
            sp.wait_ge(s["eaT_ps"], (NG - 2) * NC)
            load_attr(NG - 1, 0, last=True)

            all_slots = slots[0:SLOTS, :].rearrange("(p t) f -> p (t f)", p=P)

            def fast_layers():
                sp.wait_ge(s["need_ready"], 1)
                sp.wait_ge(s["edge_done"], 2)
                with sp.Fori(0, NB) as j:
                    sp.wait_ge(s["landed"], sp.value_load(need[0:1, bass.ds(j, 1)], min_val=1, max_val=2 * NG))
                    sp.sem_inc(s["block_in"], 1)
                    for c in range(2):
                        sp.wait_ge(s[f"r3_free{c}"], j + 1)
                        n = HT if c == 0 else HT - 1
                        sp.dma_start(r3[:, c, 0:n, :].rearrange("p t f -> p (t f)"),
                                     all_slots[:, bass.ds(j * (BT * REC) + c * HT * REC, n * REC)])\
                            .then_inc(s["r3a" if c == 0 else "r3b"], 16)
                for c in range(2):
                    sp.wait_ge(s[f"oh_used{c}"], NB)

                def load_rows(r, uses):
                    for u in range(RING):
                        sp.wait_ge(s[f"a_used{u}"], uses)
                        sp.dma_start(ablk[:, u, :], adj[bass.ds(r * RING + u, 1), :, :]
                                     .rearrange("o p n -> (o p) n")).then_inc(s[f"a{u}"], 16)

                sp.wait_ge(s["adj_out0"], 16 * -(-RING // 2))
                sp.wait_ge(s["adj_out1"], 16 * (RING // 2))
                load_rows(0, 1)
                sp.wait_ge(s["adj_out0"], 16 * (NB - NB // 2))
                sp.wait_ge(s["adj_out1"], 16 * (NB // 2))
                with sp.Fori(1, NR) as r:
                    load_rows(r, r + 1)
                with sp.Fori(0, NR - 1) as r:
                    load_rows(r, r + (NR + 2))

            def any_layers():
                sp.wait_ge(s["g_init"], 5)
                edge_tiles(sp, g_src[:, :], src, s["g_ld"])
                edge_tiles(sp, g_dst[:, :], dst, s["g_ld"])
                for t in g_x + [g_h, g_max, g_sum]:
                    w = t.shape[1]
                    sp.dma_start(t.rearrange("(p r) w -> p r w", p=P), g_zero[:, 0:w].rearrange("p (o w) -> p o w", o=1)
                                 .broadcast_to([P, TBL // P, w])).then_inc(s["g_zeroed"], 16)
                sp.wait_ge(s["g_zeroed"], 16 * (LAYERS + 4))
                sp.wait_ge(s["ld_x"], 80)
                sp.dma_start(g_x[0][0:NP, :].rearrange("(b p) d -> p b d", p=P), xs[:, :, :]).then_inc(s["g_x0"], 16)
                sp.wait_ge(s["g_done"], LAYERS * NT + 1)
                for l in range(LAYERS):
                    sp.dma_start(ablk[:, l, :].rearrange("p (b d) -> p b d", b=NB),
                                 g_x[l + 1][0:NP, :].rearrange("(b p) d -> p b d", p=P)).then_inc(s["g_back"], 16)

            def any_attention():
                sp.wait_ge(s["g_hx"], 1)
                sp.dma_start(g_h[0:NP, :].rearrange("(b p) d -> p b d", p=P), hx).then_inc(s["g_hr"], 16)
                sp.wait_ge(s["g_done"], len(passes) * NT + 1)
                sp.wait_ge(s["g_hr"], 16)
                sp.dma_start(g_num, g_sum[0:NP, :].rearrange("(b p) d -> p b d", p=P)).then_inc(s["g_fin"], 16)
                sp.dma_start(g_m[:, :, :], g_max[0:NP, :].rearrange("(b p) d -> p b d", p=P)).then_inc(s["g_fin"], 16)

            def load(j, n, b, turns=True):
                sp.wait_ge(s["r6_free"], n + 1)
                sp.dma_start(r6[:, b, 0:BT, :].rearrange("p t f -> p (t f)"),
                             all_slots[:, bass.ds(j * (BT * REC), BT * REC)]).then_inc(s[f"r6_in{b}"], 16)
                if turns:
                    sp.wait_ge(s["hg_ps"], (n + 1) * NQ)
                    for c in range(2):
                        sp.dma_start(rT[:, b, c * HT:(c + 1) * HT, :, :].rearrange("p t k n -> p (t k n)"),
                                     turned[bass.ds(j, 1), :, c * HT:(c + 1) * HT, :, :]
                                     .rearrange("o p t k n -> (o p) (t k n)")).then_inc(s[f"rT_in{b}"], 16)

            def fast_attention():
                sp.wait_ge(s["h_split"], 1)
                with sp.Fori(0, NB // 3) as i:
                    for u in range(1, 4):
                        load(i * 3 + u, i * 3 + u, u % 3)
                load(NB - 1, NB, 1, turns=False)

            sp.wait_ge(s["flag_ready"], 1)
            plain = sp.value_load(flag[0:1, 0:1], min_val=0, max_val=1)
            with sp.If(plain):
                fast_layers()
                for c in range(2):
                    sp.wait_ge(s[f"turn_out{c}"], 16 * NB)
                sp.wait_ge(s["x1_ready"], 1)
                load(0, 0, 0)
            with sp.Else():
                any_layers()
            with sp.If(plain):
                fast_attention()
            with sp.Else():
                any_attention()
            half = NB // 2
            for b0, b1 in ((0, half), (half, NB - 1)):
                sp.wait_ge(s["y_sb"], b1)
                sp.dma_start(out[b0 * P:b1 * P, :].rearrange("(b p) d -> p b d", p=P), cur[:, b0:b1, :])\
                    .then_inc(s["outs"], 16)
            sp.wait_ge(s["y_sb"], NB)
            sp.dma_start(out[(NB - 1) * P:N, :], cur[0:NL, NB - 1, :]).then_inc(s["outs"], 16)
            sp.wait_ge(s["outs"], 48)

        @block.gpsimd
        def _(pool):
            pool.memset(src_i[:, :], -1).then_inc(s["clears"], 1)
            pool.memset(dst_i[:, :], NP - 1).then_inc(s["clears"], 1)
            pool.memset(acat[:, :, :], 0.0).then_inc(s["clears"], 1)
            pool.memset(zrec[:, :], 0.0).then_inc(s["clears"], 1)
            c = s["consts"]
            pool.memset(w_t[:, :], 0.0).then_inc(c, 1)
            pool.memset(src_t[:, (NH - 1) * SH:NT], 0).then_inc(c, 1)
            pool.memset(dst_t[:, (NH - 1) * SH:NT], 0).then_inc(c, 1)
            pool.memset(ident[:, :], 0.0).then_inc(c, 1)
            pool.memset(identb[:, :], 0.0).then_inc(c, 1)
            pool.memset(ones[:, :], 1.0).then_inc(c, 1)
            pool.memset(upper[:, :], 1.0).then_inc(c, 1)
            pool.memset(xs[:, NB - 1, :], 0.0).then_inc(c, 1)
            pool.memset(zerob[:, :], 0.0).then_inc(c, 1)
            pool.wait_ge(c, 9)
            pool.affine_select(out=ident[:, :], in_=ident[:, :], compare_op=ALU.not_equal, fill=1.0, base=0,
                               pattern=[[-1, P]], channel_multiplier=1).then_inc(c, 1)
            pool.affine_select(out=identb[:, :], in_=identb[:, :], compare_op=ALU.not_equal, fill=1.0, base=0,
                               pattern=[[-1, P]], channel_multiplier=1).then_inc(c, 1)
            pool.affine_select(out=upper[:, :], in_=upper[:, :], compare_op=ALU.is_ge, fill=0.0, base=-1,
                               pattern=[[1, P]], channel_multiplier=-1).then_inc(c, 1)
            pool.iota(past[:, :], pattern=[[1, RW]], base=SLOTS - RL, channel_multiplier=0).then_inc(c, 1)
            pool.iota(starts[:, :], pattern=[[HE, NH]], base=0, channel_multiplier=0,
                      allow_small_or_imprecise_dtypes=True).then_inc(c, 1)
            pool.iota(iota_nt[:, :, :], pattern=[[1, P], [0, BTP]], base=1, channel_multiplier=0,
                      allow_small_or_imprecise_dtypes=True).then_inc(c, 1)
            pool.memset(rec[:, :, 3:4], 0.0).then_inc(s["rec_set"], 1)

            pool.wait_ge(s["zeroed"], 32)
            pool.wait_ge(s["rec_set"], 4)
            pool.wait_ge(s["slot_in0"], 16)

            def scatter(g, k, before_landed=None):
                pool.tensor_copy(st_rec[:, k, :, :], rec[:, bass.ds(g * SG + k * SH, SH), :]).then_inc(s["staged"], 1)
                pool.tensor_copy(st_slot[:, k, :], slot_i[:, bass.ds(g * SG + k * SH, SH)]).then_inc(s["staged"], 1)
                pool.wait_ge(s["staged"], g * 4 + (2 * k + 2))
                pool.sem_inc(s["armed"], 1)
                for u in range(SH):
                    pool.indirect_dma_start(
                        out=slots, out_offset=bass.IndirectOffsetOnAxis(ap=st_slot[:, k, u:u + 1], axis=0),
                        in_=st_rec[:, k, u, :], in_offset=None).then_inc(s[f"half{k}"], 16)
                    if u == 7 and before_landed is not None:
                        pool.wait_ge(s[f"half{1 - k}"], before_landed)
                        pool.sem_inc(s["landed"], 1)

            def fast_scatter():
                pool.wait_ge(s["rec_se"], 2)
                scatter(0, 0)
                scatter(0, 1, 16 * SH)
                pool.wait_ge(s["slot_in1"], 16)
                with pool.Fori(1, NG) as g:
                    pool.wait_ge(s["rec_se"], g + 2)
                    scatter(g, 0, g * (16 * SH))
                    scatter(g, 1, (g + 1) * (16 * SH))
                pool.wait_ge(s["half1"], NG * 16 * SH)
                pool.sem_inc(s["landed"], 1)

            def any_tiles(k):
                kind, table, result, gathers = passes[k]
                n0 = k * NT
                with pool.Fori(0, NT) as t:
                    pool.wait_ge(s["g_keys"], t + (n0 + 1))
                    pool.sem_inc(s["g_armed"], 1)

                    def gather(rows, t_, col, w):
                        pool.indirect_dma_start(out=rows[:, 0:w], out_offset=None, in_=t_,
                                                in_offset=bass.IndirectOffsetOnAxis(ap=g_ki[:, col:col + 1], axis=0))\
                            .then_inc(s[f"g_in{k}"], 16)
                    gather(g_a, table, 0, table.shape[1])
                    if kind == "max":
                        gather(g_b, g_h, 1, GW)
                    elif kind == "sum":
                        gather(g_b, g_max, 1, H)
                    gather(g_old, result, 1, result.shape[1])
                    pool.wait_ge(s["g_news"], t + (n0 + 1))
                    pool.sem_inc(s["g_armed"], 1)
                    pool.indirect_dma_start(out=result, out_offset=bass.IndirectOffsetOnAxis(ap=g_so[:, 0:1], axis=0),
                                            in_=g_new[:, 0:result.shape[1]], in_offset=None).then_inc(s["g_out"], 16)
                    pool.wait_ge(s["g_out"], t * 16 + (n0 + 1) * 16)
                    pool.sem_inc(s["g_done"], 1)

            def any_layers():
                pool.wait_ge(s["edge_done"], 2)
                pool.memset(g_src[:, :], NP).then_inc(s["g_init"], 1)
                pool.memset(g_dst[:, :], NP).then_inc(s["g_init"], 1)
                pool.memset(g_zero[:, :], 0.0).then_inc(s["g_init"], 1)
                pool.memset(g_low[:, :], 1.0).then_inc(s["g_init"], 1)
                pool.iota(g_trash[:, :], pattern=[[0, 1]], base=NP + P, channel_multiplier=1,
                          allow_small_or_imprecise_dtypes=True).then_inc(s["g_init"], 1)
                pool.wait_ge(s["g_init"], 5)
                pool.affine_select(out=g_low[:, :], in_=g_low[:, :], compare_op=ALU.is_ge, fill=0.0, base=-1,
                                   pattern=[[-1, P]], channel_multiplier=1).then_inc(s["g_init"], 1)
                pool.sem_inc(s["g_done"], 1)
                pool.wait_ge(s["g_x0"], 16)
                for k in range(LAYERS):
                    any_tiles(k)

            def any_attention():
                pool.wait_ge(s["g_hr"], 16)
                for k in range(LAYERS, len(passes)):
                    any_tiles(k)

            pool.wait_ge(s["flag_ready"], 1)
            plain = pool.value_load(flag[0:1, 0:1], min_val=0, max_val=1)
            with pool.If(plain):
                fast_scatter()
            with pool.Else():
                any_layers()
                any_attention()

        @block.tensor
        def _(pe):
            pe.sem_inc(s["eaT_used"], ER)
            pe.sem_inc(s["hg_ps"], 3 * NQ)
            for u in range(RING):
                pe.sem_inc(s[f"a_used{u}"], 1)
            pe.wait_ge(s["consts"], 12)
            pe.wait_ge(s["ld_w"], 16 * (H + 3))
            pe.transpose(bank[0][:, 0:D], wn[:, :], ident[:, :])
            pe.matmul(bank[1][:, 0:2 * H], wn[:, :], acat[:, 0:2, :].rearrange("p k h -> p (k h)"),
                      start=True, stop=True)
            pe.matmul(bank[2][:, 0:H], we2[:, :, :].rearrange("p k d -> p (k d)"), acat[:, 2, :],
                      start=True, stop=True).then_inc(s["wt_ps"], 1)
            pe.wait_ge(s["wt_sb"], 1)
            def group(g, buf, load_count):
                pe.wait_ge(s[f"ea{buf}"], load_count)
                for ci in range(NC + ER - 2):
                    if ci < NC:
                        pe.wait_ge(s["eaT_sb"], g * NC + (ci + 1))
                        for n, (k, u, w) in enumerate(CHUNKS[ci]):
                            m = pe.transpose(bank[EB[ci % ER]][0:w * DE, n * P:(n + 1) * P],
                                             ea[:, buf, k, u:u + w, :].rearrange("p u d -> p (u d)"), ident[:, :])
                        m.then_inc(s["eaT_ps"], 1)
                    c = ci - (ER - 2)
                    if c >= 0:
                        if c == 0:
                            pe.wait_ge(s["rec_se"], g + 1)
                        pe.wait_ge(s["eaT_sb"], g * NC + (ER + c + 1))
                        for n, (k, u, w) in enumerate(CHUNKS[c]):
                            m = pe.matmul(bank[7][:, (k * SH + u) * H:(k * SH + u + w) * H],
                                          eaT[0:w * DE, c % ER, n * P:(n + 1) * P], wedge[0:w * DE, 0:w * H],
                                          start=True, stop=True)
                        m.then_inc(s["eaT_used"], 1)

            group(0, 0, 32)
            pe.wait_ge(s["first_ready"], 1)
            pe.matmul(bank[3][:, 0:2 * P], ones[:, :], diag[:, :, :].rearrange("p k n -> p (k n)"), start=True, stop=True).then_inc(s["ahead_bc"], 1)
            pe.wait_ge(s["ahead_ready"], 1)
            pe.matmul(bank[4][:, 0:NPAIR], ahead[:, :], lasts[:, :], start=True, stop=True).then_inc(s["base_ps"], 1)
            group(1, 1, 32)

            def groups_from(lo, hi):
                with pe.Fori(lo // 2, hi // 2) as g2:
                    for buf in range(2):
                        group(g2 * 2 + buf, buf, (g2 + 1) * 32)

            groups_from(2, AHEAD)
            pe.wait_ge(s["bad_sb"], 1)
            pe.matmul(bank[4][:, 0:1], ones[:, :], bad[:, 3:4], start=True, stop=True).then_inc(s["bad_ps"], 1)
            groups_from(AHEAD, NG - 1)
            group(NG - 1, 0, NG // 2 * 32 + 48)
            pe.wait_ge(s["upto_sb"], 1)
            pe.matmul(bank[2][:, 0:NB], ones[:, :], upto[:, :], start=True, stop=True).then_inc(s["upto_ps"], 1)
            def fast_layers():
                groups = banks_of(NB)
                pe.wait_ge(s["rec_se"], NG + 1)
                NG7 = len(groups)

                def turn(j, c):
                    for k in range(TI):
                        n = c * TI + k
                        pe.wait_ge(s["turn_sb"], j * (2 * TI) + (n + 1))
                        for u in range(BPB * k, min(HT, BPB * (k + 1))):
                            for v, rows in enumerate((oh_d, oh_s)):
                                w = (u - BPB * k) * 2 + v
                                m = pe.transpose(bank[5 + n % 2][:, :].bitcast(BF16)[:, w * P:(w + 1) * P],
                                                 rows[:, c, :, u], identb[:, :])
                        m.then_inc(s["turn_ps"], 1)

                def first_product(j, par):
                    pe.wait_ge(s["row_add"], j + 2)
                    pe.wait_ge(s["xst_sb"], j + 1)
                    for g, bs in enumerate(groups):
                        pe.wait_ge(s["l1_free"], j * NG7 + (g + NG7 - 1 if g >= 2 else (NG7 - g)))
                        pe.matmul(bank[3 + g % 2][:, 0:len(bs) * P], xst[:, par, :],
                                  arow[par][:, g * BANK:g * BANK + len(bs) * P], start=True, stop=True)\
                            .then_inc(s["l1_ps"], 1)

                def row(j, par, first=False):
                    for i in range(NB):
                        g = i // BPB
                        if i % BPB == 0:
                            last = max(n for n in range(NG7) if n % RB == g) if g < RB else NG7 + g - RB
                            pe.wait_ge(s["row_free"], j * NG7 + (last + 1))
                        n = 0
                        for t in (2 * i, 2 * i + 1):
                            c, u = divmod(t, HT)
                            if u == 0:
                                pe.wait_ge(s["oh_ready"], j * 2 + (c + 1))
                            for k in range(3):
                                m = pe.matmul(bank[g % RB][:, i % BPB * P:(i % BPB + 1) * P], oh_d[:, c, :, u],
                                              oh_w[:, c, k, :, u], start=(n == 0), stop=(n == 5))
                                n += 1
                        if i == groups[g][-1]:
                            m.then_inc(s["row_ps"], 1)
                        elif 2 * i + 1 == HT - 1:
                            turn(j, 0)
                            if not first:
                                first_product(j - 1, 1 - par)
                    pe.wait_ge(s["row_add"], j + 1)
                    for k in range(3):
                        m = pe.matmul(bank[7][:, 0:P], oh_d[:, 1, :, BT - 1 - HT], oh_w[:, 1, k, :, BT - 1 - HT],
                                      start=(k == 0), stop=(k == 2))
                    m.then_inc(s["diag_ps"], 1)
                    turn(j, 1)

                pe.sem_inc(s["l1_ps"], NG7)
                row(0, 0, first=True)
                with pe.Fori(0, NB // 2) as i:
                    row(i * 2 + 1, 1)
                    row(i * 2 + 2, 0)
                first_product(NB - 1, 0)

                pe.wait_ge(s["l1_free"], (NB + 1) * NG7)
                pe.wait_ge(s["row_sb"], NB * NG7)
                pe.wait_ge(s["turn_sb"], NB * (2 * TI) + 2)
                for g, bs in enumerate(groups):
                    for k, b in enumerate(bs):
                        m = pe.transpose(bank[g][:, k * P:(k + 1) * P], acc[:, b, :], ident[:, :])
                    m.then_inc(s["lay_T"], 1)
                with pe.Fori(0, LAYERS - 1) as l:
                    pe.wait_ge(s["cur_sb"], (l + 1) * NG7)
                    for g, bs in enumerate(groups):
                        pe.matmul(bank[g][:, 0:len(bs) * P], zerob[:, 0:P], zerob[:, 0:len(bs) * P], start=True, stop=False)
                    with pe.Fori(0, NR) as r:
                        for u in range(RING):
                            pe.wait_ge(s[f"a{u}"], (l * (NR - 1) + r + 1) * 16)
                            pe.wait_ge(s["stage_sb"], l * NB + r * RING + (u + 1))
                            for g, bs in enumerate(groups):
                                w = len(bs) * P
                                m = pe.matmul(bank[g][:, 0:w], stage[:, u, :], ablk[:, u, g * BANK:g * BANK + w],
                                              start=False, stop=False)
                            m.then_inc(s[f"a_used{u}"], 1)
                    for g, bs in enumerate(groups):
                        m = pe.matmul(bank[g][:, 0:len(bs) * P], zerob[:, 0:P], zerob[:, 0:len(bs) * P], start=False, stop=True)
                        m.then_inc(s["lay_ps"], 1)
                    for g, bs in enumerate(groups):
                        pe.wait_ge(s["lay_sb"], l * len(groups) + (g + 1))
                        for k, b in enumerate(bs):
                            m = pe.transpose(bank[g][:, k * P:(k + 1) * P], curT[:, b * P:(b + 1) * P], ident[:, :])
                        m.then_inc(s["lay_T"], 1)

            def any_tiles(k):
                kind = passes[k][0]
                w = {"spmm": D, "max": H * P, "sum": MW}[kind]
                n0 = k * NT
                with pe.Fori(0, NT) as t:
                    pe.wait_ge(s["g_keys"], t + (n0 + 1))
                    pe.matmul(bank[0][:, 0:P], ones[:, :], g_diag[:, 0, :], start=True, stop=True).then_inc(s["g_bc"], 1)
                    pe.wait_ge(s["g_msgs"], t + (n0 + 1))
                    if kind == "max":
                        m = pe.matmul(bank[1][:, :], ones[:, :], g_diag[:, :, :].rearrange("p h n -> p (h n)"), start=True, stop=True)
                    else:
                        m = pe.matmul(bank[1][:, 0:w], g_same[:, :], g_msg[:, 0:w], start=True, stop=True)
                    m.then_inc(s["g_tot"], 1)

            def any_layers():
                for k in range(LAYERS):
                    any_tiles(k)

            def any_attention():
                for k in range(LAYERS, len(passes)):
                    any_tiles(k)

            pe.wait_ge(s["flag_ready"], 1)
            plain = pe.value_load(flag[0:1, 0:1], min_val=0, max_val=1)
            with pe.If(plain):
                fast_layers()
            with pe.Else():
                any_layers()
            groups = banks_of(NB)
            W = D + 2 * H
            done = 0
            for g, bs in enumerate(groups + [[]]):
                ready = BPB * g if g < len(groups) else NB
                while done < HC and (3 * done + 3 <= ready - BPB or g == len(groups)):
                    last = min(NB, 3 * done + 3)
                    pe.wait_ge(s["x1T_sb"], (last - 1) // BPB + 1)
                    if done >= len(HB):
                        pe.wait_ge(s["rest1"], done - len(HB) + 1)
                    for k, b in enumerate(range(3 * done, last)):
                        m = pe.matmul(bank[HB[done % len(HB)]][:, k * W:(k + 1) * W], curT[:, b * P:(b + 1) * P],
                                      wext[:, :], start=True, stop=True)
                    m.then_inc(s["h_ps"], 1)
                    done += 1
                if bs:
                    pe.wait_ge(s["x1_ready"], bs[-1] + 1)
                    if g >= TB:
                        pe.wait_ge(s["x1T_sb"], g - TB + 1)
                    for k, b in enumerate(bs):
                        m = pe.transpose(bank[g % TB][:, k * P:(k + 1) * P], cur[:, b, :], ident[:, :])
                    m.then_inc(s["x1T_ps"], 1)
            pe.wait_ge(s["h_split"], 1)

            def block_rows(j):
                return hsp[:, bass.ds(j, 1), :, :].rearrange("p o k n -> p (o k) n")

            def src_rows(t, j):
                return hsp[:, t // 2, :, :] if t < BT - 1 else block_rows(j)

            def gather_h(j, b, q):
                pe.wait_ge(s["msg_sb"], (j * NQ + before(q, HR)) * 2)
                for v in range(BPB):
                    t = BPB * q + v
                    if t < BT:
                        for k in range(3):
                            m = pe.matmul(bank[HG[q % HR]][:, v * P:(v + 1) * P], rT[:, b, t, 1, :],
                                          src_rows(t, j)[:, k, 0:D], start=(k == 0), stop=(k == 2))
                m.then_inc(s["hg_ps"], 1)

            def sum_dst(j, b, q):
                if q == 0:
                    pe.wait_ge(s["num_free"], j + 1)
                pe.wait_ge(s["d6_ready"], j * NQ + (2 * NQ + q + 1))
                pe.wait_ge(s["msg_sb"], (j * NQ + (NQ + q + 1)) * 2)
                for v in range(BPB):
                    t = BPB * q + v
                    if t < BT:
                        m = pe.matmul(bank[2][:, 0:MW], d6[:, q % MR, v, :], msg[:, q % MR, v, :],
                                      start=(t == 0), stop=(t == BT - 1))
                m.then_inc(s["msg_used"], 1)

            def sums_of(j, b, lo, hi):
                for q in range(lo, hi):
                    if q < NQ:
                        gather_h(j, b, q)
                    if q >= HR - 1:
                        sum_dst(j, b, q - (HR - 1))

            def step(j, b, par, turn, sums=True):
                def sums_to(lo, hi):
                    if sums:
                        sums_of(j - 1, (b - 1) % 3, lo, hi)
                pe.wait_ge(s[f"rT_in{b}"], turn * 32 + 32)
                pe.wait_ge(s["dlr_ready"], j + 1)
                for k in range(2):
                    pe.transpose(bank[6][0:HT * H, (2 + k) * P:(3 + k) * P],
                                 dlr[:, k * HT:(k + 1) * HT, :].rearrange("p t h -> p (t h)"), ident[:, :])
                for t in range(BT):
                    o = bank[5 + t // 40][:, t % 40 * 3 * H:(t % 40 + 1) * 3 * H]
                    pe.matmul(o, rT[:, b, t, 1, :], src_rows(t, j)[:, :, D:D + H], start=True, stop=False)
                    m = pe.matmul(o, rT[:, b, t, 0, :], block_rows(j)[:, :, D + H:D + 2 * H], start=False, stop=True)
                m.then_inc(s["at_ps"], 1)
                sums_to(0, CUTS[0])
                pe.wait_ge(s["at_sb"], j + 1)
                for k in range(2):
                    m = pe.transpose(bank[7][0:HT * H, k * P:(k + 1) * P],
                                     sc[:, k * HT:(k + 1) * HT, :].rearrange("p t h -> p (t h)"), ident[:, :])
                m.then_inc(s["atT_ps"], 1)
                sums_to(CUTS[0], CUTS[1])
                pe.wait_ge(s["z_sb"], j + 1)
                for k in range(2):
                    m = pe.transpose(bank[7][:, k * HT * H:(k + 1) * HT * H], run[0:HT * H, k, :], ident[0:HT * H, 0:HT * H])
                m.then_inc(s["zT_ps"], 1)
                sums_to(CUTS[1], CUTS[2])
                pe.wait_ge(s["zs_sb"], j + 1)
                pe.wait_ge(s["d16_ready"], j + 1)
                for t in range(BT):
                    m = pe.matmul(bank[5 + t // 40][:, t % 40 * 3 * H:(t % 40 + 1) * 3 * H], d16[:, par, :, t],
                                  zsp[:, :, t, :], start=True, stop=True)
                m.then_inc(s["v_ps"], 1)
                sums_to(CUTS[2], NQ + HR - 1)
                pe.wait_ge(s["m_sb"], j + 1)
                for t in range(BT):
                    m = pe.matmul(bank[MG[t // 40]][:, t % 40 * 3 * H:(t % 40 + 1) * 3 * H], rT[:, b, t, 0, :],
                                  msp[:, :, :].rearrange("p k h -> p (k h)"), start=True, stop=True)
                m.then_inc(s["mg_ps"], 1)

            def fast_attention():
                pe.sem_inc(s["msg_used"], NQ)
                step(0, 0, 0, 0, sums=False)
                with pe.Fori(0, NB // 6) as i:
                    for u in range(1, 7):
                        step(i * 6 + u, u % 3, u % 2, i * 2 + u // 3)
                sums_of(NB - 1, 0, 0, NQ + HR - 1)

            with pe.If(plain):
                fast_attention()
            with pe.Else():
                any_attention()

        @block.scalar
        def _(act):
            act.sem_inc(s["rec_se"], 1)
            act.sem_inc(s["eaT_sb"], ER)
            act.sem_inc(s["row_free"], len(banks_of(NB)))
            act.sem_inc(s["turn_sb"], 2)
            act.wait_ge(s["wt_ps"], 1)
            act.copy(wext[:, 0:D], bank[0][:, 0:D])
            act.copy(wext[:, D:D + 2 * H], bank[1][:, 0:2 * H])
            act.mul(wedge[:, :], ones[:, 0:2 * H], 0.0)
            act.drain()
            act.copy(wedge[0:DE, 0:H], bank[2][0:DE, 0:H])
            act.copy(wedge[DE:2 * DE, H:2 * H], bank[2][DE:2 * DE, 0:H])
            act.drain()
            act.nop().then_inc(s["wt_sb"], 1)

            def group(g):
                for ci, units in enumerate(CHUNKS):
                    act.wait_ge(s["eaT_ps"], g * NC + (ci + 1))
                    act.wait_ge(s["eaT_used"], g * NC + (ci + 1))
                    full = sum(w == 2 for _, _, w in units) * P
                    m = act.copy(eaT[:, ci % ER, 0:full], bank[EB[ci % ER]][:, 0:full])
                    if full < len(units) * P:
                        m = act.copy(eaT[0:DE, ci % ER, full:full + P], bank[EB[ci % ER]][0:DE, full:full + P])
                    m.then_inc(s["eaT_sb"], 1)
                act.wait_ge(s["eaT_used"], g * NC + (NC + ER))
                act.copy(rec[:, bass.ds(g * SG, SG), H:2 * H],
                         bank[7][:, 0:SG * H].rearrange("p (t f) -> p t f", f=H)).then_inc(s["rec_se"], 1)

            group(0)
            act.wait_ge(s["ld_x"], 80)
            act.copy(rec[:, :, 0], w_t[:, :]).then_inc(s["rec_set"], 1)
            group(1)
            with act.Fori(1, NG // 2) as g2:
                for b in range(2):
                    group(g2 * 2 + b)
            group(NG - 1)
            act.nop().then_inc(s["edge_done"], 1)

            def fast_layers():
                groups = banks_of(NB)
                NG7 = len(groups)

                def turn(j, c, first):
                    if not first:
                        act.wait_ge(s[f"turn_out{c}"], j * 16)
                    for k in range(TI):
                        act.wait_ge(s["turn_ps"], j * (2 * TI) + (c * TI + k + 1))
                        n = min(HT, BPB * (k + 1)) - BPB * k
                        act.copy(tb[:, c, BPB * k:BPB * k + n, :, :].rearrange("p t k n -> p (t k n)"),
                                 bank[5 + (c * TI + k) % 2][:, :].bitcast(BF16)[:, 0:n * 2 * P]).then_inc(s["turn_sb"], 1)
                    act.drain()
                    act.sem_inc(s[f"oh_used{c}"], 1)
                    act.wait_ge(s["turn_sb"], j * (2 * TI) + ((c + 1) * TI + 2))
                    act.dma_start(turned[bass.ds(j, 1), :, c * HT:(c + 1) * HT, :, :].rearrange("o p t k n -> (o p) (t k n)"),
                                  tb[:, c, :, :, :].rearrange("p t k n -> p (t k n)")).then_inc(s[f"turn_out{c}"], 16)

                def row(j, par, turn_no, first=False):
                    if not first:
                        act.wait_ge(s["l1_ps"], j * NG7)
                    act.copy(xst[:, par, :], xs[:, bass.ds(j, 1), :].rearrange("p o n -> p (o n)")).then_inc(s["xst_sb"], 1)
                    for g, bs in enumerate(groups):
                        if g == HT // 2 // BPB:
                            turn(j, 0, first)
                        act.wait_ge(s["row_ps"], j * NG7 + (g + 1))
                        act.copy(arow[par][:, g * BANK:g * BANK + len(bs) * P], bank[g % RB][:, 0:len(bs) * P])
                        act.drain()
                        act.nop().then_inc(s["row_free"], 1)
                        act.nop().then_inc(s["row_sb"], 1)
                    turn(j, 1, first)
                    act.wait_ge(s["row_add"], j + 2)
                    act.dma_start(adj[bass.ds(j, 1), :, :].rearrange("o p n -> (o p) n"), arow[par])\
                        .then_inc(s[f"adj_out{par}"], 16)
                    if not first:
                        act.wait_ge(s[f"adj_out{1 - par}"], turn_no * 16 + 16)

                row(0, 0, 0, first=True)
                with act.Fori(0, NB // 2) as i:
                    row(i * 2 + 1, 1, i)
                    row(i * 2 + 2, 0, i)

                def to_cur(l):
                    for g, bs in enumerate(groups):
                        act.wait_ge(s["lay_T"], l * NG7 + (g + 1))
                        act.copy(cur[:, bs[0]:bs[0] + len(bs), :].rearrange("p b n -> p (b n)"),
                                 bank[g][:, 0:len(bs) * P]).then_inc(s["cur_sb"], 1)

                act.wait_ge(s["adj_out1"], 16 * (NB // 2))
                to_cur(0)
                with act.Fori(0, LAYERS - 1) as l:
                    act.wait_ge(s["cur_sb"], (l + 1) * NG7)
                    with act.Fori(0, NR) as r:
                        for u in range(RING):
                            act.wait_ge(s[f"a_used{u}"], l * NR + r + 1)
                            act.copy(stage[:, u, :], cur[:, bass.ds((r + l * (NR - 1)) % NR * RING + u, 1), :].rearrange("p o n -> p (o n)"))\
                                .then_inc(s["stage_sb"], 1)
                    act.wait_ge(s["acc_sb"], l * NB + NB)
                    to_cur(l + 1)

            def any_attention():
                with act.Fori(0, NT) as t:
                    act.wait_ge(s["g_arg"], t + 1)
                    act.activation(g_s[:, 2, :], g_s[:, 1, :], ACT.Exp).then_inc(s["g_ex"], 1)
                act.wait_ge(s["g_fin"], 32)
                act.activation(g_e[:, :, :], g_m[:, :, :], ACT.Exp, scale=-1.0).then_inc(s["g_emn"], 1)

            act.wait_ge(s["flag_ready"], 1)
            plain = act.value_load(flag[0:1, 0:1], min_val=0, max_val=1)
            with act.If(plain):
                fast_layers()
            groups = banks_of(NB)
            def norm(part):
                act.wait_ge(s["less_ready"], part)
                for b in range(SQ):
                    act.activation(junk[:, :], acc[:, b, :], ACT.Square, bias=st[:, 0, b:b + 1],
                                   accum_out=st[:, 1, b:b + 1]).then_inc(s["squares"], 1)
                    act.drain()
                act.wait_ge(s["rs_var"], part)
                act.activation(st[:, 2, :], st[:, 1, :], ACT.Sqrt).then_inc(s["rs_std"], 1)

            norm(1)
            W = D + 2 * H

            def cast(k, c):
                bs = slice(3 * c, min(NB, 3 * c + 3))
                n = bs.stop - bs.start
                if k == 0:
                    act.wait_ge(s["h_ps"], c + 1)
                    a = bank[HB[c % len(HB)]][:, 0:n * W].rearrange("p (b n) -> p b n", b=n)
                else:
                    act.wait_ge(s[f"rest{k}"], c + 1)
                    a = hx[:, bs, :]
                act.copy(hsp[:, bs, k, :], a).then_inc(s[f"part{k}"], 1)

            turned_groups = 0
            for c in range(HC + 2):
                while turned_groups < min(len(groups), (3 * c + 5) // BPB + 1):
                    g, bs = turned_groups, groups[turned_groups]
                    act.wait_ge(s["x1T_ps"], g + 1)
                    act.copy(curT[:, g * BANK:g * BANK + len(bs) * P], bank[g % TB][:, 0:len(bs) * P]).then_inc(s["x1T_sb"], 1)
                    turned_groups += 1
                for k in range(3):
                    if 0 <= c - k < HC:
                        cast(k, c - k)
            act.wait_ge(s["h_split"], 1)

            def rows_of(j, par):
                act.wait_ge(s["d16_ready"], j + 1)
                for q in range(NQ):
                    act.wait_ge(s["msg_used"], j * NQ + before(q, MR))
                    act.copy(d6[:, q % MR, :, :], d16[:, par, :, BPB * q:BPB * (q + 1)].rearrange("p n t -> p t n"))\
                        .then_inc(s["d6_ready"], 1)

            def sums_of(j):
                act.wait_ge(s["msg_used"], (j + 2) * NQ)
                act.copy(acc[:, bass.ds(j, 1), :].rearrange("p o n -> p (o n)"), bank[2][:, 0:D])
                act.copy(dens[:, bass.ds(j, 1), :].rearrange("p o h -> p (o h)"), bank[2][:, D:MW])
                act.drain()
                act.sem_inc(s["num_free"], 1)

            def step(j, b, par, sums=True):
                if sums:
                    rows_of(j - 1, 1 - par)
                act.wait_ge(s["m_sb"], j + 1)
                act.activation(emn[:, bass.ds(j, 1), :].rearrange("p o h -> p (o h)"), mm[:, 0, :], ACT.Exp, scale=-1.0)\
                    .then_inc(s["emn_sb"], 1)
                if sums:
                    sums_of(j - 1)
                act.wait_ge(s["arg_sb"], j + 1)
                act.activation(ex[:, b, 0:BT, 0:H], me[:, 0:BT, :], ACT.Exp).then_inc(s["ex_sb"], 1)

            def fast_attention():
                act.sem_inc(s["num_free"], 1)
                act.sem_inc(s["d6_ready"], 2 * NQ)
                step(0, 0, 0, sums=False)
                with act.Fori(0, NB // 6) as i:
                    for u in range(1, 7):
                        step(i * 6 + u, u % 3, u % 2)
                rows_of(NB - 1, 0)
                sums_of(NB - 1)

            with act.If(plain):
                fast_attention()
            with act.Else():
                any_attention()
            norm(2)

        @block.vector
        def _(dve):
            def norm(dest, a, part, ready):
                less, var, std, inv = (st[:, k, :] for k in range(4))
                dve.tensor_scalar(less, less, -1.0 / D, None, ALU.mult)
                dve.drain()
                dve.sem_inc(s["less_ready"], 1)
                for b in range(SQ, NB):
                    dve.tensor_scalar(dest[:, b, :], a[:, b, :], less[:, b:b + 1], None, ALU.add)
                dve.drain()
                for b in range(SQ, NB):
                    dve.scalar_tensor_tensor(out=junk2[:, b % 2, :], in0=dest[:, b, :], scalar=1.0, in1=dest[:, b, :],
                                             op0=ALU.mult, op1=ALU.mult, accum_out=var[:, b:b + 1])
                    dve.drain()
                dve.wait_ge(s["squares"], part * SQ)
                dve.tensor_scalar(var, var, 1.0 / D, EPS, ALU.mult, ALU.add)
                dve.drain()
                dve.nop().then_inc(s["rs_var"], 1)
                dve.wait_ge(s["rs_std"], part)
                dve.reciprocal(inv, std)
                dve.drain()
                for b in range(NB):
                    dve.tensor_scalar(dest[:, b, :], a[:, b, :], less[:, b:b + 1], inv[:, b:b + 1], ALU.add, ALU.mult)\
                        .then_inc(s[ready], 1)
                dve.drain()

            for n in ("r3_free0", "r3_free1", "row_add"):
                dve.sem_inc(s[n], 1)
            dve.sem_inc(s["r6_free"], 3)
            dve.wait_ge(s["ld_idx"], 64)
            dve.wait_ge(s["consts"], 12)
            dve.tensor_single_scalar(ti[:, 0, :], dst_i[:, :], 7, op=ALU.arith_shift_right)
            dve.tensor_single_scalar(ti[:, 1, :], src_i[:, :], 7, op=ALU.arith_shift_right)
            dve.drain()
            dve.tensor_copy(dstb[:, :], ti[:, 0, :])
            dve.tensor_copy(srcb[:, :], ti[:, 1, :])
            dve.drain()
            dve.tensor_copy(rank[:, :], dst_i[:, :])
            dve.tensor_scalar(diag[:, 0, :], ident[:, :], dstb[:, 0:1], None, ALU.mult)
            dve.drain()
            dve.tensor_scalar(diag[:, 1, :], ident[:, :], rank[:, 0:1], None, ALU.mult)
            dve.drain()
            dve.nop().then_inc(s["first_ready"], 1)
            dve.tensor_single_scalar(ti[:, 0, :], src_i[:, :], 8, op=ALU.arith_shift_right)
            dve.tensor_scalar(odd[:, :], src_i[:, :], 7, 1, ALU.arith_shift_right, ALU.bitwise_and)
            dve.tensor_tensor(same[:, 1:RW], dstb[:, 1:RW], dstb[:, 0:RW - 1], ALU.is_equal)
            dve.memset(same[:, 0:1], 1.0)
            dve.drain()
            dve.tensor_copy(pair[:, :], ti[:, 0, :])
            dve.tensor_scalar(unit[:, :], odd[:, :], float(HI - 1), 1.0, ALU.mult, ALU.add)
            dve.drain()
            dve.scalar_tensor_tensor(out=tmp[:, 1, :], in0=dstb[:, :], scalar=dstb[:, RW - 1:RW], in1=unit[:, :],
                                     op0=ALU.is_equal, op1=ALU.mult)
            dve.drain()
            for i in range(NPAIR):
                dve.scalar_tensor_tensor(out=tmp[:, 2 + i % 2, :], in0=pair[:, :], scalar=float(i), in1=tmp[:, 1, :],
                                         op0=ALU.is_equal, op1=ALU.mult, accum_out=lasts[:, i:i + 1])
                dve.drain()
            dve.tensor_tensor(tmp[:, 0, 1:RW], rank[:, 1:RW], rank[:, 0:RW - 1], ALU.is_lt)
            offs, third, room, pad = (tmp[:, k, :] for k in range(4))
            dve.tensor_scalar(room, srcb[:, :], 2.0, None, ALU.mult)
            dve.tensor_scalar(third, dstb[:, :], float(BT), float(BT - 1), ALU.mult, ALU.add)
            dve.tensor_scalar(pad, srcb[:, :], 0.0, None, ALU.is_lt)
            dve.drain()
            dve.tensor_reduce(bad[:, 0:1], tmp[:, 0, 1:RW], AX.X, ALU.max)
            dve.drain()
            dve.scalar_tensor_tensor(out=offs, in0=dstb[:, :], scalar=float(BT), in1=room, op0=ALU.mult, op1=ALU.add)
            dve.tensor_tensor(srcb[:, :], dstb[:, :], srcb[:, :], ALU.is_equal)
            dve.drain()
            dve.tensor_scalar(room, srcb[:, :], float(P), float(2 * P), ALU.mult, ALU.add)
            dve.wait_ge(s["ahead_bc"], 1)
            dve.scalar_tensor_tensor(out=ahead[:, :], in0=bank[3][:, 0:P], scalar=dstb[:, RW - 1:RW], in1=upper[:, :],
                                     op0=ALU.is_equal, op1=ALU.mult)
            dve.scalar_tensor_tensor(out=below[:, :], in0=bank[3][:, P:2 * P], scalar=rank[:, RW - 1:RW], in1=upper[:, :],
                                     op0=ALU.is_lt, op1=ALU.mult)
            dve.drain()
            dve.nop().then_inc(s["ahead_ready"], 1)
            dve.tensor_reduce(bad[:, 1:2], below[:, :], AX.X, ALU.max)
            dve.drain()

            def pack(i):
                dve.scalar_tensor_tensor(out=packed[:, i % 3, :], in0=pair[:, :], scalar=float(i), in1=unit[:, :],
                                         op0=ALU.is_equal, op1=ALU.mult)
            pack(0)
            dve.memset(rank[:, :], 0.0)
            dve.wait_ge(s["ld_t"], 96)
            dve.tensor_single_scalar(loc_t[:, 0, :], src_t, P - 1, op=ALU.bitwise_and)
            dve.tensor_single_scalar(loc_t[:, 1, :], dst_t, P - 1, op=ALU.bitwise_and)
            dve.drain()
            for k in range(2):
                dve.tensor_scalar(rec[:, :, 1 + k], loc_t[:, k, :], 1.0, None, ALU.add).then_inc(s["rec_set"], 1)
            dve.wait_ge(s["base_ps"], 1)
            dve.tensor_copy(base[:, :], bank[4][:, 0:NPAIR])
            dve.drain()
            for i in range(NPAIR):
                dve.tensor_tensor_scan(scans[:, i % 2, :], same[:, :], packed[:, i % 3, :], base[:, i:i + 1], ALU.mult, ALU.add)
                if i + 1 < NPAIR:
                    pack(i + 1)
                dve.drain()
                dve.copy_predicated(rank[:, :], packed[:, i % 3, :].bitcast(I32), scans[:, i % 2, :])
            dve.drain()
            dve.tensor_copy(ti[:, 0, :], rank[:, :])
            dve.drain()
            dve.tensor_single_scalar(ti[:, 1, :], ti[:, 0, :], HI.bit_length() - 1, op=ALU.arith_shift_right)
            dve.tensor_single_scalar(ti[:, 0, :], ti[:, 0, :], HI - 1, op=ALU.bitwise_and)
            dve.drain()
            dve.copy_predicated(ti[:, 0, :], odd[:, :], ti[:, 1, :])
            dve.drain()
            dve.tensor_scalar(rank[:, :], ti[:, 0, :], 1.0, None, ALU.subtract)
            dve.tensor_scalar(ti[:, 1, :], ti[:, 0, :], 1, None, ALU.subtract)
            dve.drain()
            dve.scalar_tensor_tensor(out=pair[:, :], in0=rank[:, :], scalar=1.0, in1=room, op0=ALU.mult, op1=ALU.is_ge,
                                     accum_out=bad[:, 2:3])
            dve.tensor_single_scalar(odd[:, :], ti[:, 1, :], 7, op=ALU.arith_shift_right)
            dve.tensor_single_scalar(ti[:, 0, :], ti[:, 1, :], P - 1, op=ALU.bitwise_and)
            dve.drain()
            dve.tensor_reduce(bad[:, 3:4], bad[:, 0:3], AX.X, ALU.add)
            dve.tensor_single_scalar(ti[:, 1, :], ti[:, 1, :], 2 * P, op=ALU.bitwise_and)
            dve.tensor_tensor(rank[:, :], odd[:, :], offs, ALU.add)
            dve.drain()
            dve.sem_inc(s["bad_sb"], 1)
            dve.copy_predicated(rank[:, :], ti[:, 1, :], third)
            dve.drain()
            dve.scalar_tensor_tensor(out=rank[:, :], in0=ti[:, 0, :], scalar=float(NB * BT), in1=rank[:, :],
                                     op0=ALU.mult, op1=ALU.add)
            dve.drain()
            dve.wait_ge(s["consts"], 14)
            dve.tensor_copy(slot_r, rank[:, :])
            dve.drain()
            dve.copy_predicated(slot_r, pad.bitcast(I32), past[:, :])
            dve.drain()
            dve.nop().then_inc(s["place_ready"], 1)
            dve.wait_ge(s["bad_ps"], 1)
            dve.tensor_scalar(flag[:, :], bank[4][:, 0:1], 0.0, None, ALU.is_equal)
            dve.drain()
            dve.sem_inc(s["flag_ready"], 1)
            for i in range(NB):
                dve.tensor_scalar(tmp[:, i % 2, :], dstb[:, :], float(i), 0.0, ALU.is_le, ALU.add,
                                  accum_out=upto[:, i:i + 1])
                dve.drain()
            dve.nop().then_inc(s["upto_sb"], 1)
            dve.wait_ge(s["upto_ps"], 1)
            dve.tensor_copy(need_f[:, :], bank[2][:, 0:NB])
            dve.drain()
            over = tmp[:, 0, 0:NB * NH].rearrange("p (b h) -> p b h", b=NB)
            dve.tensor_tensor(over, need_f[:, :].rearrange("p (b o) -> p b o", o=1).broadcast_to([P, NB, NH]),
                              starts[:, :].rearrange("p (o h) -> p o h", o=1).broadcast_to([P, NB, NH]), ALU.is_gt)
            dve.drain()
            dve.tensor_reduce(upto[:, :], over, AX.X, ALU.add)
            dve.drain()
            dve.tensor_scalar(need[:, :], upto[:, :], 1.0, None, ALU.max)
            dve.drain()
            dve.nop().then_inc(s["need_ready"], 1)
            dve.nop().then_inc(s["edge_done"], 1)

            def fast_layers():
                dve.wait_ge(s["edge_done"], 2)
                dve.memset(r3[:, 1, HT - 1:HT, :], 0.0)
                iota_h = iota_nt[:, :, 0:HT]
                tall = lambda a: a.rearrange("p (o t) -> p o t", o=1).broadcast_to([P, P, HT])
                def one_hots(j, c):
                    dve.wait_ge(s["r3a" if c == 0 else "r3b"], j * 16 + 16)
                    r = r3[:, c, :, :]
                    dve.tensor_copy(loc[:, c, 0, :], r[:, :, 1])
                    dve.tensor_copy(loc[:, c, 1, :], r[:, :, 2])
                    dve.tensor_copy(wsp[:, c, 0, :], r[:, :, 0])
                    dve.drain()
                    dve.tensor_tensor(wres[:, c, 0, :], r[:, :, 0], wsp[:, c, 0, :], ALU.subtract)
                    dve.drain()
                    dve.nop().then_inc(s[f"r3_free{c}"], 1)
                    dve.tensor_copy(wsp[:, c, 1, :], wres[:, c, 0, :])
                    dve.drain()
                    dve.tensor_tensor(wres[:, c, 1, :], wres[:, c, 0, :], wsp[:, c, 1, :], ALU.subtract)
                    dve.drain()
                    dve.tensor_copy(wsp[:, c, 2, :], wres[:, c, 1, :])
                    dve.wait_ge(s[f"oh_used{c}"], j)
                    dve.tensor_tensor(oh_s[:, c, :, :], iota_h, tall(loc[:, c, 0, :]), ALU.is_equal)
                    dve.tensor_tensor(oh_d[:, c, :, :], iota_h, tall(loc[:, c, 1, :]), ALU.is_equal)
                    dve.drain()
                    for k in range(3):
                        dve.tensor_tensor(oh_w[:, c, k, :, :], oh_s[:, c, :, :], tall(wsp[:, c, k, :]), ALU.mult)
                    dve.drain()
                    dve.nop().then_inc(s["oh_ready"], 1)

                groups = banks_of(NB)
                NGR = len(groups)

                def add_diagonal(j, par):
                    dve.wait_ge(s["row_sb"], (j + 1) * NGR)
                    dve.wait_ge(s["diag_ps"], j + 1)
                    a = arow[par][:, bass.ds(j * P, P)]
                    dve.tensor_tensor(a, a, bank[7][:, 0:P], ALU.add)
                    dve.drain()
                    dve.nop().then_inc(s["row_add"], 1)

                def sum_first(j, first=False):
                    for g, bs in enumerate(groups):
                        dve.wait_ge(s["l1_ps"], j * NGR + (NGR + g + 1))
                        b, a = bank[3 + g % 2][:, 0:len(bs) * P], y1[:, g * BANK:g * BANK + len(bs) * P]
                        if first:
                            dve.tensor_copy(a, b).then_inc(s["l1_free"], 1)
                        else:
                            dve.tensor_tensor(a, a, b, ALU.add).then_inc(s["l1_free"], 1)
                    dve.drain()

                dve.sem_inc(s["l1_free"], NGR)
                one_hots(0, 0)
                one_hots(0, 1)

                def row(j, par, first=False):
                    one_hots(j, 0)
                    add_diagonal(j - 1, 1 - par)
                    one_hots(j, 1)
                    sum_first(j - 1, first)

                row(1, 1, first=True)
                row(2, 0)
                with dve.Fori(1, NB // 2) as i:
                    row(i * 2 + 1, 1)
                    row(i * 2 + 2, 0)
                add_diagonal(NB - 1, 0)
                sum_first(NB - 1)

                dve.wait_ge(s["adj_out0"], 16 * (NB - NB // 2))
                for l in range(LAYERS):
                    if l:
                        for g, bs in enumerate(groups):
                            dve.wait_ge(s["lay_ps"], (l - 1) * NGR + (g + 1))
                            dve.tensor_copy(curT[:, g * BANK:g * BANK + len(bs) * P], bank[g][:, 0:len(bs) * P])\
                                .then_inc(s["lay_sb"], 1)
                    for b in range(NB):
                        if b % BPB == 0:
                            dve.wait_ge(s["cur_sb"], l * NGR + (b // BPB + 1))
                        dve.scalar_tensor_tensor(out=acc[:, b, :], in0=xs[:, b, :] if l == 0 else acc[:, b, :],
                                                 scalar=2.0 if l == 0 else 1.0, in1=cur[:, b, :],
                                                 op0=ALU.mult, op1=ALU.add,
                                                 **(dict(accum_out=st[:, 0, b:b + 1]) if l == LAYERS - 1 else {}))\
                            .then_inc(s["acc_sb"], 1)
                    dve.drain()

            def add_x(b0, b1):
                for b in range(b0, b1):
                    dve.scalar_tensor_tensor(out=acc[:, b, :], in0=acc[:, b, :], scalar=1.0, in1=cur[:, b, :],
                                             op0=ALU.mult, op1=ALU.add, accum_out=st[:, 0, b:b + 1])
                dve.drain()

            def any_tiles(k):
                kind = passes[k][0]
                n0 = k * NT
                gathers = passes[k][3]
                ia, ib = (g_dst, g_src) if kind == "spmm" else (g_src, g_dst)
                key, lead, shift, place = (g_key[:, c:c + 1] for c in range(4))
                with dve.Fori(0, NT) as t:
                    dve.wait_ge(s["g_done"], t + (n0 + 1))
                    dve.tensor_copy(g_ki[:, 0:1], ia[:, bass.ds(t, 1)])
                    dve.tensor_copy(g_ki[:, 1:2], ib[:, bass.ds(t, 1)])
                    dve.tensor_copy(key, ib[:, bass.ds(t, 1)])
                    dve.drain()
                    dve.tensor_scalar(g_diag[:, 0, :], ident[:, :], key, None, ALU.mult)
                    dve.drain()
                    dve.sem_inc(s["g_keys"], 1)
                    dve.wait_ge(s["g_bc"], t + (n0 + 1))
                    dve.tensor_scalar(g_same[:, :], bank[0][:, 0:P], key, None, ALU.is_equal)
                    dve.drain()
                    dve.tensor_tensor(g_tmp[:, 0, :], g_same[:, :], g_low[:, :], ALU.mult)
                    dve.tensor_tensor(shift, key, g_trash[:, :], ALU.subtract)
                    dve.drain()
                    dve.tensor_reduce(place, g_tmp[:, 0, :], AX.X, ALU.max)
                    dve.drain()
                    dve.tensor_scalar(lead, place, 0.0, None, ALU.is_equal)
                    dve.drain()
                    dve.tensor_tensor(place, lead, shift, ALU.mult)
                    dve.drain()
                    dve.tensor_tensor(g_so[:, :], place, g_trash[:, :], ALU.add)
                    dve.wait_ge(s[f"g_in{k}"], (t + 1) * (16 * gathers))
                    if kind == "spmm":
                        dve.tensor_scalar(g_msg[:, 0:D], g_a[:, 0:D], rec[:, bass.ds(t, 1), 0], None, ALU.mult)
                    elif kind == "max":
                        row = g_att[:, bass.ds(t, 1), :].rearrange("p o h -> p (o h)")
                        dve.tensor_tensor(g_s[:, 0, :], g_a[:, D:D + H], g_b[:, D + H:D + 2 * H], ALU.add)
                        dve.drain()
                        dve.tensor_tensor(g_s[:, 1, :], g_s[:, 0, :], row, ALU.add)
                        dve.drain()
                        dve.scalar_tensor_tensor(out=g_s[:, 2, :], in0=g_s[:, 1, :], scalar=0.2, in1=g_s[:, 1, :],
                                                 op0=ALU.mult, op1=ALU.max)
                        dve.drain()
                        dve.tensor_copy(row, g_s[:, 2, :])
                        for h in range(H):
                            dve.tensor_scalar(g_diag[:, h, :], ident[:, :], g_s[:, 2, h:h + 1], None, ALU.mult)
                    else:
                        dve.tensor_tensor(g_s[:, 1, :], g_att[:, bass.ds(t, 1), :].rearrange("p o h -> p (o h)"),
                                          g_b[:, 0:H], ALU.subtract)
                        dve.drain()
                        dve.sem_inc(s["g_arg"], 1)
                        dve.wait_ge(s["g_ex"], t + 1)
                        dve.tensor_tensor(g_msg[:, 0:D].rearrange("p (h d) -> p h d", h=H),
                                          g_a[:, 0:D].rearrange("p (h d) -> p h d", h=H),
                                          g_s[:, 2, :].rearrange("p (h o) -> p h o", o=1).broadcast_to([P, H, HD]), ALU.mult)
                        dve.tensor_copy(g_msg[:, D:D + H], g_s[:, 2, :])
                        dve.memset(g_msg[:, D + H:MW], 1.0)
                    dve.drain()
                    dve.sem_inc(s["g_msgs"], 1)
                    dve.wait_ge(s["g_tot"], t + (n0 + 1))
                    if kind == "max":
                        dve.tensor_tensor(g_tmp[:, :, :], bank[1][:, :].rearrange("p (h n) -> p h n", h=H),
                                          g_same[:, :].rearrange("p (o n) -> p o n", o=1).broadcast_to([P, H, P]), ALU.mult)
                        dve.drain()
                        dve.tensor_reduce(g_s[:, 3, :], g_tmp[:, :, :], AX.X, ALU.max)
                        dve.drain()
                        dve.tensor_tensor(g_new[:, 0:H], g_s[:, 3, :], g_old[:, 0:H], ALU.max)
                    else:
                        w = D if kind == "spmm" else MW
                        dve.tensor_tensor(g_new[:, 0:w], bank[1][:, 0:w], g_old[:, 0:w], ALU.add)
                    dve.drain()
                    dve.sem_inc(s["g_news"], 1)

            def any_layers():
                dve.wait_ge(s["g_init"], 6)
                dve.wait_ge(s["rec_set"], 4)
                dve.wait_ge(s["g_ld"], 96)
                dve.wait_ge(s["rec_se"], NG + 1)
                dve.tensor_copy(g_att[:, :, :], rec[:, 0:NT, H:2 * H])
                dve.tensor_scalar(acc[:, :, :], xs[:, :, :], 2.0, None, ALU.mult)
                dve.drain()
                for k in range(LAYERS):
                    any_tiles(k)
                dve.wait_ge(s["g_back"], 16 * LAYERS)
                for l in range(LAYERS):
                    dve.tensor_tensor(acc[:, :, :], acc[:, :, :], ablk[:, l, :].rearrange("p (b d) -> p b d", b=NB), ALU.add)
                    dve.drain()
                dve.tensor_reduce(st[:, 0, :], acc[:, :, :], AX.X, ALU.add)
                dve.drain()

            def any_attention():
                dve.tensor_tensor(hx, hsp[:, :, 0, :], hsp[:, :, 1, :], ALU.add)
                dve.drain()
                dve.tensor_tensor(hx, hx, hsp[:, :, 2, :], ALU.add)
                dve.drain()
                dve.sem_inc(s["g_hx"], 1)
                for k in range(LAYERS, len(passes)):
                    any_tiles(k)
                dve.wait_ge(s["g_fin"], 32)
                dve.wait_ge(s["g_emn"], 1)
                dve.tensor_scalar(g_m[:, :, :], g_num[:, :, D + H:MW].broadcast_to([P, NB, H]), -1.0, float(E), ALU.mult, ALU.add)
                dve.drain()
                dve.tensor_tensor(g_m[:, :, :], g_m[:, :, :], g_e[:, :, :], ALU.mult)
                dve.drain()
                dve.tensor_tensor(g_m[:, :, :], g_m[:, :, :], g_num[:, :, D:D + H], ALU.add)
                dve.drain()
                dve.reciprocal(g_e[:, :, :], g_m[:, :, :])
                dve.drain()
                for h in range(H):
                    dve.tensor_tensor(acc[:, :, h * HD:(h + 1) * HD], g_num[:, :, h * HD:(h + 1) * HD],
                                      g_e[:, :, h:h + 1].broadcast_to([P, NB, HD]), ALU.mult)
                dve.drain()
                add_x(0, NB)

            dve.wait_ge(s["flag_ready"], 1)
            plain = dve.value_load(flag[0:1, 0:1], min_val=0, max_val=1)
            with dve.If(plain):
                fast_layers()
            with dve.Else():
                any_layers()
            groups = banks_of(NB)
            norm(cur, acc, 1, "x1_ready")
            W = D + 2 * H

            def rest(k, c):
                bs = slice(3 * c, min(NB, 3 * c + 3))
                n = bs.stop - bs.start
                dve.wait_ge(s[f"part{k - 1}"], c + 1)
                a = bank[HB[c % len(HB)]][:, 0:n * W].rearrange("p (b n) -> p b n", b=n) if k == 1 else hx[:, bs, :]
                dve.tensor_tensor(hx[:, bs, :], a, hsp[:, bs, k - 1, :], ALU.subtract).then_inc(s[f"rest{k}"], 1)

            for c in range(HC + 1):
                for k in (1, 2):
                    if 0 <= c - k + 1 < HC:
                        rest(k, c - k + 1)
            dve.wait_ge(s["part2"], HC)
            dve.nop().then_inc(s["h_split"], 1)

            RH = HT * H

            def take_records(b, turn):
                dve.wait_ge(s[f"r6_in{b}"], turn * 16 + 16)
                dve.tensor_copy(loc6[:, b, :], r6[:, b, :, 2])
                dve.tensor_copy(dlr[:, :, :], r6[:, b, :, 2:3].broadcast_to([P, BTP, H]))
                dve.drain()
                dve.sem_inc(s["dlr_ready"], 1)

            def one_hot(j, b, par):
                dve.wait_ge(s["d6_ready"], j * NQ + NQ)
                dve.tensor_tensor(d16[:, par, :, :], iota_nt[:, :, :],
                                  loc6[:, b, :].rearrange("p (o t) -> p o t", o=1).broadcast_to([P, P, BTP]),
                                  ALU.is_equal).then_inc(s["d16_ready"], 1)

            def messages(j, par, lo, hi):
                for q in range(lo, hi):
                    n = min(BT, BPB * (q + 1)) - BPB * q
                    if q == 0:
                        dve.wait_ge(s["ex_sb"], j + 1)
                    dve.wait_ge(s["hg_ps"], j * NQ + (3 * NQ + q + 1))
                    dve.wait_ge(s["msg_used"], j * NQ + before(q, MR))
                    dve.tensor_copy(msg[:, q % MR, 0:n, D:D + H], ex[:, par, BPB * q:BPB * q + n, :])\
                        .then_inc(s["msg_sb"], 1)
                    dve.tensor_tensor(
                        msg[:, q % MR, 0:n, 0:D].rearrange("p t (h d) -> p t h d", h=H),
                        bank[HG[q % HR]][:, 0:n * P].rearrange("p (t h d) -> p t h d", h=H, d=HD),
                        ex[:, par, BPB * q:BPB * q + n, 0:H].rearrange("p t (h o) -> p t h o", o=1).broadcast_to([P, n, H, HD]),
                        ALU.mult).then_inc(s["msg_sb"], 1)

            def denominators(b0, b1):
                n = b1 - b0
                x, y = den[:, 0, b0:b1, :], den[:, 1, b0:b1, :]
                dve.tensor_scalar(x, dens[:, b0:b1, H:H + 1].broadcast_to([P, n, H]), -1.0, float(E), ALU.mult, ALU.add)
                dve.drain()
                dve.tensor_tensor(y, x, emn[:, b0:b1, :], ALU.mult)
                dve.drain()
                dve.tensor_tensor(x, y, dens[:, b0:b1, 0:H], ALU.add)
                dve.drain()
                dve.reciprocal(y, x)
                dve.drain()

            def results(b0, b1):
                for b in range(b0, b1):
                    a = acc[:, b, :].rearrange("p (h d) -> p h d", h=H)
                    dve.tensor_tensor(a, a, den[:, 1, b, :].rearrange("p (h o) -> p h o", o=1).broadcast_to([P, H, HD]), ALU.mult)
                dve.drain()
                add_x(b0, b1)

            def sum_parts(b0, b1):
                for lo, hi, k in ((0, 40, b0), (40, BT, b1)):
                    dve.tensor_reduce(sc2[:, lo:hi, :], bank[k][:, 0:(hi - lo) * 3 * H]
                                      .rearrange("p (t k h) -> p t h k", k=3, h=H), AX.X, ALU.add)
                dve.drain()

            def step(j, b, par, after, sums=True):
                def msgs(lo, hi):
                    if sums:
                        messages(j - 1, (b - 1) % 3, lo, hi)

                dve.wait_ge(s["at_ps"], j + 1)
                sum_parts(5, 6)
                dve.tensor_tensor(sc2[:, 0:BT, :], sc2[:, 0:BT, :], r6[:, b, 0:BT, H:2 * H], ALU.add)
                dve.drain()
                dve.sem_inc(s["r6_free"], 1)
                dve.scalar_tensor_tensor(out=sc[:, 0:BT, :], in0=sc2[:, 0:BT, :], scalar=0.2, in1=sc2[:, 0:BT, :],
                                         op0=ALU.mult, op1=ALU.max)
                dve.drain()
                dve.sem_inc(s["at_sb"], 1)
                if not sums:
                    one_hot(j, b, par)
                msgs(0, DCUTS[0])
                dve.tensor_copy(dlT[0:RH, :, :].rearrange("p k n -> p (k n)"), bank[6][0:RH, 2 * P:4 * P])
                dve.drain()
                dve.tensor_tensor(keep[0:RH, :, 1:P], dlT[0:RH, :, 1:P], dlT[0:RH, :, 0:P - 1], ALU.is_equal)
                dve.tensor_tensor(endz[0:RH, :, 0:P - 1], dlT[0:RH, :, 1:P], dlT[0:RH, :, 0:P - 1], ALU.not_equal)
                dve.drain()
                dve.wait_ge(s["atT_ps"], j + 1)
                dve.tensor_tensor_scan(run[0:RH, :, :].rearrange("p k n -> p (k n)"),
                                       keep[0:RH, :, :].rearrange("p k n -> p (k n)"), bank[7][0:RH, 0:2 * P],
                                       0.0, ALU.mult, ALU.max)
                dve.drain()
                dve.tensor_tensor(run[0:RH, :, :], run[0:RH, :, :], endz[0:RH, :, :], ALU.mult)
                dve.drain()
                dve.sem_inc(s["z_sb"], 1)
                take_records((b + 1) % 3, after)
                msgs(DCUTS[0], DCUTS[1])
                dve.wait_ge(s["zT_ps"], j + 1)
                dve.tensor_copy(zs[:, 0, :, :].rearrange("p t h -> p (t h)"), bank[7][:, 0:BTP * H])
                dve.drain()
                for k in range(3):
                    dve.tensor_copy(zsp[:, k, :, :], zs[:, k, :, :])
                    dve.drain()
                    if k < 2:
                        dve.tensor_tensor(zs[:, k + 1, :, :], zs[:, k, :, :], zsp[:, k, :, :], ALU.subtract)
                        dve.drain()
                dve.sem_inc(s["zs_sb"], 1)
                msgs(DCUTS[1], DCUTS[2])
                dve.wait_ge(s["v_ps"], j + 1)
                sum_parts(5, 6)
                dve.tensor_reduce(mm[:, 0, :], sc2[:, 0:BT, :].rearrange("p t h -> p h t"), AX.X, ALU.max)
                dve.drain()
                dve.tensor_copy(msp[:, 0, :], mm[:, 0, :])
                dve.drain()
                dve.tensor_tensor(mm[:, 1, :], mm[:, 0, :], msp[:, 0, :], ALU.subtract)
                dve.drain()
                dve.tensor_copy(msp[:, 1, :], mm[:, 1, :])
                dve.drain()
                dve.tensor_tensor(mm[:, 2, :], mm[:, 1, :], msp[:, 1, :], ALU.subtract)
                dve.drain()
                dve.tensor_copy(msp[:, 2, :], mm[:, 2, :])
                dve.drain()
                dve.sem_inc(s["m_sb"], 1)
                msgs(DCUTS[2], NQ)
                one_hot(j + 1, (b + 1) % 3, 1 - par)
                dve.wait_ge(s["mg_ps"], j + 1)
                sum_parts(*MG)
                dve.tensor_tensor(me[:, 0:BT, :], sc[:, 0:BT, :], sc2[:, 0:BT, :], ALU.subtract)
                dve.drain()
                dve.sem_inc(s["arg_sb"], 1)

            def fast_attention():
                dve.memset(r6[:, :, BT:BTP, :], 0.0)
                dve.memset(sc[:, BT:BTP, :], 0.0)
                dve.memset(keep[:, :, 0:1], 0.0)
                dve.memset(endz[:, :, P - 1:P], 1.0)
                dve.memset(msg[:, :, :, D + H:MW], 1.0)
                dve.drain()
                dve.sem_inc(s["msg_sb"], 2 * NQ)
                take_records(0, 0)
                step(0, 0, 0, 0, sums=False)
                with dve.Fori(0, NB // 6) as i:
                    for u in range(1, 7):
                        step(i * 6 + u, u % 3, u % 2, i * 2 + (u + 1) // 3)
                messages(NB - 1, 0, 0, 2)
                dve.wait_ge(s["num_free"], NB)
                dve.wait_ge(s["emn_sb"], NB)
                denominators(0, NB - 1)
                done = 0
                for q in range(2, NQ):
                    messages(NB - 1, 0, q, q + 1)
                    upto_b = (NB - 1) * (q - 1) // (NQ - 2)
                    results(done, upto_b)
                    done = upto_b
                dve.wait_ge(s["num_free"], NB + 1)
                denominators(NB - 1, NB)
                results(NB - 1, NB)

            with dve.If(plain):
                fast_attention()
            with dve.Else():
                any_attention()
            norm(cur, acc, 2, "y_sb")


INPUTS = ["x", "src", "dst", "edge_attr_64", "edge_weight", "L1_gnn_W_node", "L1_gnn_W_edge", "L1_gnn_a"]


def kernel(**inputs):
    import concourse.bacc as bacc
    from concourse.bass_utils import run_bass_kernel_spmd as run

    nc = bacc.Bacc("TRN2", target_bir_lowering=False, num_devices=1)
    arrays, args = {}, []
    for name in INPUTS:
        a = np.ascontiguousarray(inputs[name])
        arrays[f"in_{name}"] = a
        args.append(nc.dram_tensor(f"in_{name}", a.shape, mybir.dt.from_np(a.dtype), kind="ExternalInput").ap())
    out = nc.dram_tensor("out", (N, D), F32, kind="ExternalOutput").ap()
    build(nc, *args, out)
    r = run(nc, [arrays], core_ids=[0])
    return r.results[0]["out"]
```
